# Optimizing a Trainium2 kernel written in Bass

```python
import numpy as np
import jax
import jax.numpy as jnp

def _softmax(x, axis=-1):
    return jax.nn.softmax(x, axis=axis)

def _gelu(x):
    return jax.nn.gelu(x, approximate=True)

def _silu(x):
    return jax.nn.silu(x)

def _sigmoid(x):
    return jax.nn.sigmoid(x)

def _layernorm(x, axis=-1, eps=1e-05):
    m = jnp.mean(x, axis=axis, keepdims=True)
    v = jnp.var(x, axis=axis, keepdims=True)
    return (x - m) / jnp.sqrt(v + eps)

def _scatter_add(tgt, idx, src, axis=0):
    return tgt.at[idx].add(src)

def _segment_sum(src, seg, n):
    return jax.ops.segment_sum(src, seg, n)
kernel_name = 'mk_seq_postln_d2_jaxref_r8_c75c58'

def setup_inputs(seed: int=0):
    np.random.seed(seed)
    _w = jnp.asarray

    def _L0_attn_setup():
        import jax, jax.numpy as jnp
        import numpy as np
        D_MODEL = 256
        D_INNER = 512
        D_STATE = 64
        N_QK_HEADS = 8
        N_V_HEADS = 64
        CHUNK = 128
        KSIZE = 4
        CONV_DIM = D_INNER + 2 * N_QK_HEADS * D_STATE
        PROJ_DIM = CONV_DIM + D_INNER + N_V_HEADS

        def segsum(x):
            T = x.shape[-1]
            xe = jnp.broadcast_to(x[..., None], x.shape + (T,))
            strict_lower = jnp.tril(jnp.ones((T, T), dtype=bool), -1)
            xe = jnp.where(strict_lower, xe, 0.0)
            s = jnp.cumsum(xe, axis=-2)
            lower = jnp.tril(jnp.ones((T, T), dtype=bool), 0)
            return jnp.where(lower, s, -jnp.inf)

        def ssd_chunk_scan(X, dA, Bm, Cm, chunk):
            b, l, h, p = X.shape
            g = Bm.shape[2]
            rep = h // g
            Bm = jnp.repeat(Bm, rep, axis=2)
            Cm = jnp.repeat(Cm, rep, axis=2)
            c = l // chunk
            X = X.reshape(b, c, chunk, h, p)
            Bm = Bm.reshape(b, c, chunk, h, -1)
            Cm = Cm.reshape(b, c, chunk, h, -1)
            A = jnp.transpose(dA.reshape(b, c, chunk, h), (0, 3, 1, 2))
            A_cum = jnp.cumsum(A, axis=-1)
            Lm = jnp.exp(segsum(A))
            Y_diag = jnp.einsum('bcshn,bczhn,bhcsz,bczhp->bcshp', Cm, Bm, Lm, X)
            decay_states = jnp.exp(A_cum[..., -1:] - A_cum)
            states = jnp.einsum('bcshn,bhcs,bcshp->bchpn', Bm, decay_states, X)
            states = jnp.concatenate([jnp.zeros_like(states[:, :1]), states], axis=1)
            chunk_sums = jnp.pad(A_cum[..., -1], ((0, 0), (0, 0), (1, 0)))
            decay_chunk = jnp.exp(segsum(chunk_sums))
            new_states = jnp.einsum('bhzc,bchpn->bzhpn', decay_chunk, states)
            states = new_states[:, :-1]
            state_decay_out = jnp.exp(A_cum)
            Y_off = jnp.einsum('bcshn,bchpn,bhcs->bcshp', Cm, states, state_decay_out)
            return (Y_diag + Y_off).reshape(b, l, h, p)
        key = jax.random.key(seed)
        ks = jax.random.split(key, 6)
        input_ = jax.random.normal(ks[0], (2, 512, D_MODEL), dtype=jnp.float32)
        in_proj_w = jax.random.normal(ks[1], (PROJ_DIM, D_MODEL), dtype=jnp.float32) * (2.0 / D_MODEL) ** 0.5
        cb = (CONV_DIM * KSIZE) ** (-0.5)
        conv1d_weight = jax.random.uniform(ks[2], (CONV_DIM, 1, KSIZE), dtype=jnp.float32, minval=-cb, maxval=cb)
        conv1d_bias = jax.random.uniform(ks[3], (CONV_DIM,), dtype=jnp.float32, minval=-0.5, maxval=0.5)
        z_bias = jnp.zeros((D_INNER,), dtype=jnp.float32)
        D = jnp.ones((N_V_HEADS,), dtype=jnp.float32)
        out_proj_w = jax.random.normal(ks[4], (D_MODEL, D_INNER), dtype=jnp.float32) * (2.0 / D_INNER) ** 0.5
        return {'input_': input_, 'in_proj_w': in_proj_w, 'conv1d_weight': conv1d_weight, 'conv1d_bias': conv1d_bias, 'z_bias': z_bias, 'D': D, 'out_proj_w': out_proj_w}
    _L0_attn_in = _L0_attn_setup()

    def _L0_ffn_setup():
        import jax, jax.numpy as jnp
        import numpy as np
        EPS = 1e-08

        def _quantize(w):
            gamma = jnp.mean(jnp.abs(w))
            return jnp.clip(jnp.round(w / (gamma + EPS)), -1.0, 1.0)

        def _bitlinear(x, w):
            return jnp.matmul(x, _quantize(w).T)
        key = jax.random.key(seed)
        k1, k2, k3, k4 = jax.random.split(key, 4)
        d, h = (256, 704)
        x = jax.random.normal(k1, (4, 256, d), dtype=jnp.float32)
        w1 = jax.random.normal(k2, (h, d), dtype=jnp.float32)
        w2 = jax.random.normal(k3, (h, d), dtype=jnp.float32)
        w3 = jax.random.normal(k4, (d, h), dtype=jnp.float32)
        return {'x': x, 'w1': w1, 'w2': w2, 'w3': w3}
    _L0_ffn_in = _L0_ffn_setup()

    def _L1_attn_setup():
        import jax, jax.numpy as jnp
        import numpy as np
        EPS = 1e-06

        def elu1(x):
            return jax.nn.elu(x) + 1.0

        def causal_linear_attention(q, k, v, chunk=128):
            b, h, s, d = q.shape
            sq, sk = (elu1(q), elu1(k))
            nc = s // chunk
            rs = lambda x: x.reshape(b, h, nc, chunk, d).transpose(2, 0, 1, 3, 4)
            sqc, skc, vc = (rs(sq), rs(sk), rs(v))
            mask = jnp.tril(jnp.ones((chunk, chunk), dtype=q.dtype))

            def step(carry, xs):
                S, z = carry
                qc, kc, vcc = xs
                scores = jnp.einsum('bhid,bhjd->bhij', qc, kc) * mask
                num = jnp.einsum('bhij,bhje->bhie', scores, vcc) + jnp.einsum('bhid,bhde->bhie', qc, S)
                den = scores.sum(-1) + jnp.einsum('bhid,bhd->bhi', qc, z)
                out = num / jnp.clip(den, EPS)[..., None]
                S = S + jnp.einsum('bhjd,bhje->bhde', kc, vcc)
                z = z + kc.sum(2)
                return ((S, z), out)
            S0 = jnp.zeros((b, h, d, d), q.dtype)
            z0 = jnp.zeros((b, h, d), q.dtype)
            _, outs = jax.lax.scan(step, (S0, z0), (sqc, skc, vc))
            return outs.transpose(1, 2, 0, 3, 4).reshape(b, h, s, d)
        B, S, H, NH, NM = (2, 512, 256, 16, 4)
        HD = H // NH
        key = jax.random.key(seed)
        ks = jax.random.split(key, 12)
        p = lambda k, shp: jax.random.normal(k, shp, dtype=jnp.float32) * 0.02
        return {'hidden_states': jax.random.normal(ks[0], (B, S, H), dtype=jnp.float32), 'w_q': p(ks[1], (H, H)), 'w_k': p(ks[2], (H, H)), 'w_v': p(ks[3], (H, H)), 'w_o': p(ks[4], (H, H)), 'eg_w1': p(ks[5], (H // 4, H)), 'eg_b1': jnp.zeros((H // 4,), jnp.float32), 'eg_w2': p(ks[6], (1, H // 4)), 'eg_b2': jnp.zeros((1,), jnp.float32), 'memory_gate': jnp.zeros((NH,), jnp.float32), 'fine_memories': jax.random.uniform(ks[7], (NM, NH, HD, HD), dtype=jnp.float32) * 0.1, 'fine_memory_norms': jax.random.uniform(ks[8], (NM, NH, HD), dtype=jnp.float32) + 0.1}
    _L1_attn_in = _L1_attn_setup()

    def _L1_ffn_setup():
        import jax, jax.numpy as jnp
        import numpy as np
        TOPK = 2
        NORM_TOPK = True
        SCALE = 1.0
        EPS = 1e-09
        key = jax.random.key(seed)
        ks = jax.random.split(key, 9)
        h, i, E = (256, 128, 16)
        std = 0.02
        return {'x': jax.random.normal(ks[0], (1, 256, h), jnp.float32), 'Wr': jax.random.normal(ks[1], (E, h), jnp.float32) * std, 'bias': jnp.zeros((E,), jnp.float32), 'Wg': jax.random.normal(ks[2], (E, h, i), jnp.float32) * std, 'Wu': jax.random.normal(ks[3], (E, h, i), jnp.float32) * std, 'Wd': jax.random.normal(ks[4], (E, i, h), jnp.float32) * std, 'sWg': jax.random.normal(ks[5], (h, i), jnp.float32) * std, 'sWu': jax.random.normal(ks[6], (h, i), jnp.float32) * std, 'sWd': jax.random.normal(ks[7], (i, h), jnp.float32) * std}
    _L1_ffn_in = _L1_ffn_setup()
    _d = {'L0_attn_input_': _L0_attn_in['input_'], 'L0_attn_in_proj_w': _L0_attn_in['in_proj_w'], 'L0_attn_conv1d_weight': _L0_attn_in['conv1d_weight'], 'L0_attn_conv1d_bias': _L0_attn_in['conv1d_bias'], 'L0_attn_z_bias': _L0_attn_in['z_bias'], 'L0_attn_D': _L0_attn_in['D'], 'L0_attn_out_proj_w': _L0_attn_in['out_proj_w'], 'L0_ffn_w1': _L0_ffn_in['w1'], 'L0_ffn_w2': _L0_ffn_in['w2'], 'L0_ffn_w3': _L0_ffn_in['w3'], 'L1_attn_w_q': _L1_attn_in['w_q'], 'L1_attn_w_k': _L1_attn_in['w_k'], 'L1_attn_w_v': _L1_attn_in['w_v'], 'L1_attn_w_o': _L1_attn_in['w_o'], 'L1_attn_eg_w1': _L1_attn_in['eg_w1'], 'L1_attn_eg_b1': _L1_attn_in['eg_b1'], 'L1_attn_eg_w2': _L1_attn_in['eg_w2'], 'L1_attn_eg_b2': _L1_attn_in['eg_b2'], 'L1_attn_memory_gate': _L1_attn_in['memory_gate'], 'L1_attn_fine_memories': _L1_attn_in['fine_memories'], 'L1_attn_fine_memory_norms': _L1_attn_in['fine_memory_norms'], 'L1_ffn_Wr': _L1_ffn_in['Wr'], 'L1_ffn_bias': _L1_ffn_in['bias'], 'L1_ffn_Wg': _L1_ffn_in['Wg'], 'L1_ffn_Wu': _L1_ffn_in['Wu'], 'L1_ffn_Wd': _L1_ffn_in['Wd'], 'L1_ffn_sWg': _L1_ffn_in['sWg'], 'L1_ffn_sWu': _L1_ffn_in['sWu'], 'L1_ffn_sWd': _L1_ffn_in['sWd']}
    _x0 = _d['L0_attn_input_']
    _d['L0_attn_input_'] = jax.random.normal(jax.random.fold_in(jax.random.key(seed), 1), (2, 2048, 256), dtype=_x0.dtype)
    del _x0
    return _d

def reference(L0_attn_input_, L0_attn_in_proj_w, L0_attn_conv1d_weight, L0_attn_conv1d_bias, L0_attn_z_bias, L0_attn_D, L0_attn_out_proj_w, L0_ffn_w1, L0_ffn_w2, L0_ffn_w3, L1_attn_w_q, L1_attn_w_k, L1_attn_w_v, L1_attn_w_o, L1_attn_eg_w1, L1_attn_eg_b1, L1_attn_eg_w2, L1_attn_eg_b2, L1_attn_memory_gate, L1_attn_fine_memories, L1_attn_fine_memory_norms, L1_ffn_Wr, L1_ffn_bias, L1_ffn_Wg, L1_ffn_Wu, L1_ffn_Wd, L1_ffn_sWg, L1_ffn_sWu, L1_ffn_sWd):

    def _L0_attn_ref(input_, in_proj_w, conv1d_weight, conv1d_bias, z_bias, D, out_proj_w):
        import jax, jax.numpy as jnp
        import numpy as np
        D_MODEL = 256
        D_INNER = 512
        D_STATE = 64
        N_QK_HEADS = 8
        N_V_HEADS = 64
        CHUNK = 128
        KSIZE = 4
        CONV_DIM = D_INNER + 2 * N_QK_HEADS * D_STATE
        PROJ_DIM = CONV_DIM + D_INNER + N_V_HEADS

        def segsum(x):
            T = x.shape[-1]
            xe = jnp.broadcast_to(x[..., None], x.shape + (T,))
            strict_lower = jnp.tril(jnp.ones((T, T), dtype=bool), -1)
            xe = jnp.where(strict_lower, xe, 0.0)
            s = jnp.cumsum(xe, axis=-2)
            lower = jnp.tril(jnp.ones((T, T), dtype=bool), 0)
            return jnp.where(lower, s, -jnp.inf)

        def ssd_chunk_scan(X, dA, Bm, Cm, chunk):
            b, l, h, p = X.shape
            g = Bm.shape[2]
            rep = h // g
            Bm = jnp.repeat(Bm, rep, axis=2)
            Cm = jnp.repeat(Cm, rep, axis=2)
            c = l // chunk
            X = X.reshape(b, c, chunk, h, p)
            Bm = Bm.reshape(b, c, chunk, h, -1)
            Cm = Cm.reshape(b, c, chunk, h, -1)
            A = jnp.transpose(dA.reshape(b, c, chunk, h), (0, 3, 1, 2))
            A_cum = jnp.cumsum(A, axis=-1)
            Lm = jnp.exp(segsum(A))
            Y_diag = jnp.einsum('bcshn,bczhn,bhcsz,bczhp->bcshp', Cm, Bm, Lm, X)
            decay_states = jnp.exp(A_cum[..., -1:] - A_cum)
            states = jnp.einsum('bcshn,bhcs,bcshp->bchpn', Bm, decay_states, X)
            states = jnp.concatenate([jnp.zeros_like(states[:, :1]), states], axis=1)
            chunk_sums = jnp.pad(A_cum[..., -1], ((0, 0), (0, 0), (1, 0)))
            decay_chunk = jnp.exp(segsum(chunk_sums))
            new_states = jnp.einsum('bhzc,bchpn->bzhpn', decay_chunk, states)
            states = new_states[:, :-1]
            state_decay_out = jnp.exp(A_cum)
            Y_off = jnp.einsum('bcshn,bchpn,bhcs->bcshp', Cm, states, state_decay_out)
            return (Y_diag + Y_off).reshape(b, l, h, p)
        b, L, _ = input_.shape
        xBCzA = jnp.einsum('bld,ed->ble', input_, in_proj_w)
        xBC = xBCzA[..., :CONV_DIM]
        z = xBCzA[..., CONV_DIM:CONV_DIM + D_INNER]
        A_log = xBCzA[..., CONV_DIM + D_INNER:]
        xt = jnp.transpose(xBC, (0, 2, 1))
        y = jax.lax.conv_general_dilated(xt, conv1d_weight, (1,), [(KSIZE - 1, 0)], feature_group_count=CONV_DIM, dimension_numbers=('NCH', 'OIH', 'NCH'))
        xBC = jax.nn.silu(jnp.transpose(y + conv1d_bias[None, :, None], (0, 2, 1)))
        x = xBC[..., :D_INNER].reshape(b, L, N_V_HEADS, D_INNER // N_V_HEADS)
        Bm = xBC[..., D_INNER:D_INNER + N_QK_HEADS * D_STATE].reshape(b, L, N_QK_HEADS, D_STATE)
        Cm = xBC[..., D_INNER + N_QK_HEADS * D_STATE:].reshape(b, L, N_QK_HEADS, D_STATE)
        dt = jax.nn.softplus(A_log)
        x_in = x / dt[..., None]
        y_ssm = ssd_chunk_scan(x_in * dt[..., None], -dt, Bm, Cm, CHUNK)
        Du = D[None, None, :, None] * x_in
        yf = (y_ssm + Du).reshape(b, L, D_INNER)
        out = jnp.einsum('bld,ed->ble', yf * jax.nn.silu(z + z_bias), out_proj_w)
        return out

    def _L0_ffn_ref(x, w1, w2, w3):
        import jax, jax.numpy as jnp
        import numpy as np
        EPS = 1e-08

        def _quantize(w):
            gamma = jnp.mean(jnp.abs(w))
            return jnp.clip(jnp.round(w / (gamma + EPS)), -1.0, 1.0)

        def _bitlinear(x, w):
            return jnp.matmul(x, _quantize(w).T)
        x1 = _bitlinear(x, w1)
        x2 = _bitlinear(x, w2)
        hidden = jax.nn.sigmoid(x1) * x2
        return _bitlinear(hidden, w3)

    def _L1_attn_ref(hidden_states, w_q, w_k, w_v, w_o, eg_w1, eg_b1, eg_w2, eg_b2, memory_gate, fine_memories, fine_memory_norms):
        import jax, jax.numpy as jnp
        import numpy as np
        EPS = 1e-06

        def elu1(x):
            return jax.nn.elu(x) + 1.0

        def causal_linear_attention(q, k, v, chunk=128):
            b, h, s, d = q.shape
            sq, sk = (elu1(q), elu1(k))
            nc = s // chunk
            rs = lambda x: x.reshape(b, h, nc, chunk, d).transpose(2, 0, 1, 3, 4)
            sqc, skc, vc = (rs(sq), rs(sk), rs(v))
            mask = jnp.tril(jnp.ones((chunk, chunk), dtype=q.dtype))

            def step(carry, xs):
                S, z = carry
                qc, kc, vcc = xs
                scores = jnp.einsum('bhid,bhjd->bhij', qc, kc) * mask
                num = jnp.einsum('bhij,bhje->bhie', scores, vcc) + jnp.einsum('bhid,bhde->bhie', qc, S)
                den = scores.sum(-1) + jnp.einsum('bhid,bhd->bhi', qc, z)
                out = num / jnp.clip(den, EPS)[..., None]
                S = S + jnp.einsum('bhjd,bhje->bhde', kc, vcc)
                z = z + kc.sum(2)
                return ((S, z), out)
            S0 = jnp.zeros((b, h, d, d), q.dtype)
            z0 = jnp.zeros((b, h, d), q.dtype)
            _, outs = jax.lax.scan(step, (S0, z0), (sqc, skc, vc))
            return outs.transpose(1, 2, 0, 3, 4).reshape(b, h, s, d)
        B, S, H = hidden_states.shape
        NH = memory_gate.shape[0]
        HD = H // NH
        split = lambda x: x.reshape(B, S, NH, HD).transpose(0, 2, 1, 3)
        q = split(hidden_states @ w_q.T)
        k = split(hidden_states @ w_k.T)
        v = split(hidden_states @ w_v.T)
        sq = elu1(q)
        M = fine_memories.sum(0)
        z = fine_memory_norms.sum(0)
        a_c = jnp.einsum('bhsd,hde->bhse', sq, M)
        n_c = jnp.clip(jnp.einsum('bhsd,hd->bhs', sq, z), EPS)[..., None]
        out_coarse = jnp.where(z.sum() < EPS, 0.0, a_c / n_c)
        a_f = jnp.einsum('bhsd,mhde->mbhse', sq, fine_memories)
        n_f = jnp.einsum('bhsd,mhd->mbhs', sq, fine_memory_norms)
        bank_dead = (fine_memory_norms.sum((1, 2)) < EPS)[:, None, None, None, None]
        outs = jnp.where(bank_dead, 0.0, a_f / jnp.clip(n_f, EPS)[..., None])
        rel = n_f.mean(-1)
        w = jax.nn.softmax(rel, axis=0)[..., None, None]
        out_fine = (outs * w).sum(0)
        coarse_repr = out_coarse.transpose(0, 2, 1, 3).reshape(B, S, H)
        gprob = jax.nn.sigmoid(jax.nn.relu(coarse_repr @ eg_w1.T + eg_b1) @ eg_w2.T + eg_b2)
        exp_prob = gprob.transpose(0, 2, 1)[..., None]
        memory_output = exp_prob * out_fine + (1.0 - exp_prob) * out_coarse
        local_output = causal_linear_attention(q, k, v)
        gate = jax.nn.sigmoid(memory_gate).reshape(1, NH, 1, 1)
        output = gate * memory_output + (1.0 - gate) * local_output
        output = output.transpose(0, 2, 1, 3).reshape(B, S, H)
        return output @ w_o.T

    def _L1_ffn_ref(x, Wr, bias, Wg, Wu, Wd, sWg, sWu, sWd):
        import jax, jax.numpy as jnp
        import numpy as np
        TOPK = 2
        NORM_TOPK = True
        SCALE = 1.0
        EPS = 1e-09
        b, s, h = x.shape
        E = Wr.shape[0]
        xt = x.reshape(b * s, h)
        logits = xt @ Wr.T + bias
        probs = jax.nn.softmax(logits, axis=-1)
        topk_val, topk_idx = jax.lax.top_k(probs, TOPK)
        if NORM_TOPK:
            w = topk_val / (jnp.sum(topk_val, axis=-1, keepdims=True) + EPS)
        else:
            w = topk_val
        w = w * SCALE
        g = jnp.einsum('th,ehi->tei', xt, Wg)
        u = jnp.einsum('th,ehi->tei', xt, Wu)
        y = jnp.einsum('tei,eih->teh', jax.nn.silu(g) * u, Wd)
        oh = jax.nn.one_hot(topk_idx, E, dtype=x.dtype)
        routed = jnp.einsum('tke,tk,teh->th', oh, w, y)
        shared = jax.nn.silu(xt @ sWg) * (xt @ sWu) @ sWd
        return (routed + shared).reshape(b, s, h)
    x = L0_attn_input_
    x = _layernorm(x + _L0_attn_ref(x, L0_attn_in_proj_w, L0_attn_conv1d_weight, L0_attn_conv1d_bias, L0_attn_z_bias, L0_attn_D, L0_attn_out_proj_w), axis=-1)
    x = _layernorm(x + _L0_ffn_ref(x, L0_ffn_w1, L0_ffn_w2, L0_ffn_w3), axis=-1)
    x = _layernorm(x + _L1_attn_ref(x, L1_attn_w_q, L1_attn_w_k, L1_attn_w_v, L1_attn_w_o, L1_attn_eg_w1, L1_attn_eg_b1, L1_attn_eg_w2, L1_attn_eg_b2, L1_attn_memory_gate, L1_attn_fine_memories, L1_attn_fine_memory_norms), axis=-1)
    x = _layernorm(x + _L1_ffn_ref(x, L1_ffn_Wr, L1_ffn_bias, L1_ffn_Wg, L1_ffn_Wu, L1_ffn_Wd, L1_ffn_sWg, L1_ffn_sWu, L1_ffn_sWd), axis=-1)
    return x

_drawn_inputs = setup_inputs


def setup_inputs(seed=0):
    import zlib

    import numpy as np

    out = dict(_drawn_inputs(seed))
    spreads = {'L0_attn_z_bias': (0.0, 0.1),
     'L0_attn_D': (1.0, 0.2),
     'L1_attn_eg_b1': (0.0, 2.0),
     'L1_attn_memory_gate': (0.0, 0.8),
     'L1_ffn_bias': (0.0, 0.8)}
    factors = {'L1_attn_w_q': 8.0,
     'L1_attn_w_k': 8.0,
     'L1_attn_w_v': 6.914,
     'L1_attn_w_o': 3.611,
     'L1_attn_eg_w1': 200.0,
     'L1_attn_eg_w2': 200.0,
     'L1_attn_fine_memories': 8.0,
     'L1_attn_fine_memory_norms': 8.0,
     'L1_ffn_Wr': 7.203,
     'L1_ffn_Wg': 6.698,
     'L1_ffn_Wu': 6.64,
     'L1_ffn_Wd': 6.647,
     'L1_ffn_sWg': 4.915,
     'L1_ffn_sWu': 4.832,
     'L1_ffn_sWd': 4.848}
    for name, (base, spread) in spreads.items():
        noise = np.random.default_rng([zlib.crc32(name.encode()), seed]).standard_normal(out[name].shape)
        drawn = base * np.exp(spread * noise) if base else spread * noise
        out[name] = jnp.asarray(drawn.astype(out[name].dtype))
    for name, factor in factors.items():
        out[name] = (out[name] * factor).astype(out[name].dtype)
    return out
```

```python
from contextlib import ExitStack

import concourse.bass as bass
from concourse import mybir

F32 = mybir.dt.float32
F32R = mybir.dt.float32r
BF16 = mybir.dt.bfloat16
I32 = mybir.dt.int32
U32 = mybir.dt.uint32
ALU = mybir.AluOpType
ACT = mybir.ActivationFunctionType
AX = mybir.AxisListType

P = 128
TOKENS, D = 4096, 256
CHUNKS = TOKENS // P
BATCHES = 2
KD = D // P
LN_EPS = 1e-5
ROW = D + 2
H = 64
HP = 8
G = 8
Q = 64
CONV = 12
TILES = 16
GROUP = 256


def wait(engine, sem, value):
    if not isinstance(value, int) or value > 0:
        engine.wait_ge(sem, value)


def inside(i, per, k, end):
    return not isinstance(i, int) or 0 <= per * i + k < end


class Buffers:

    def __init__(self, nc, ctx, phase):
        self.nc, self.ctx, self.phase, self.sems = nc, ctx, phase, []

    def sb(self, name, shape, dt=F32):
        return self.ctx.enter_context(self.nc.sbuf_tensor(f"{self.phase}_{name}", shape, dt))

    def ps(self, name, shape, dt=F32):
        return self.ctx.enter_context(self.nc.psum_tensor(f"{self.phase}_{name}", shape, dt))

    def sem(self, name):
        self.sems.append(self.nc.alloc_semaphore(f"{self.phase}_{name}"))
        return self.sems[-1]

    def clear(self):
        self.nc.clear_and_free_semaphores(self.sems)
        self.nc.all_engine_barrier()


def product3(nc, out, l_hi, l_lo, r_hi, r_lo, first, last):
    nc.tensor.matmul(out, l_hi, r_hi, start=first, stop=False)
    nc.tensor.matmul(out, l_hi, r_lo, start=False, stop=False)
    return nc.tensor.matmul(out, l_lo, r_hi, start=False, stop=last)


class Chain:

    def __init__(self, engine, sem, n=0):
        self.engine, self.sem, self.n = engine, sem, n

    def __call__(self, instruction):
        self.n = self.n + 1
        instruction.then_inc(self.sem, 1)
        self.engine.wait_ge(self.sem, self.n)


def first_guess(nc, link, v, y, t):
    link(nc.vector.tensor_scalar(t.bitcast(I32), v.bitcast(I32), 1, None, ALU.logical_shift_right))
    link(nc.vector.tensor_scalar(y.bitcast(I32), t.bitcast(I32), -1.0, float(0x5F3759DF), ALU.mult, ALU.add))


def newton_step(nc, link, v, y, t):
    link(nc.vector.scalar_tensor_tensor(t, y, -0.5, y, ALU.mult, ALU.mult))
    link(nc.vector.tensor_tensor(t, t, v, ALU.mult))
    link(nc.vector.scalar_tensor_tensor(y, t, 1.5, y, ALU.add, ALU.mult))


def inverse_deviation(nc, link, v, y, t):
    first_guess(nc, link, v, y, t)
    for _ in range(4):
        newton_step(nc, link, v, y, t)


def steps_phase(nc, ins, keep, scratch):
    with ExitStack() as ctx:
        b = Buffers(nc, ctx, "steps")
        xT = b.sb("xT", [P, 2, KD, 512])
        w_step = b.sb("w_step", [P, KD, H])
        d_row = b.sb("d_row", [P, H])
        neg_tri = b.sb("neg_tri", [P, P])
        W = 4 * H
        e, w1, magnitude, r, lg = (b.sb(n, [P, W]) for n in ("e", "w1", "magnitude", "r", "lg"))
        steps = b.sb("steps", [P, 2, 4, 2, H])
        parts = b.sb("parts", [H, 2, 4, 3, P], BF16)
        rest = b.sb("rest", [H, 512])
        w_raw = b.sb("w_raw", [P, KD, 2048])
        wo_raw = b.sb("wo_raw", [P, 4, D])
        a_log = b.ps("a_log", [P, 2, 512])
        sums = b.ps("sums", [P, 2, 512])
        x_in = [b.sem(f"x_in{k}") for k in range(2)]
        const_in, w_in, out_done = b.sem("const_in"), b.sem("w_in"), b.sem("out_done")
        log_done, abs_ready, exp_done, one_plus_ready = (b.sem(n) for n in ("log_done", "abs_ready", "exp_done", "one_plus_ready"))
        ln_done, dt_ready, sum_done, parts_ready = (b.sem(n) for n in ("ln_done", "dt_ready", "sum_done", "parts_ready"))
        dd_ready, dve_chain, hi_ready, lo_ready = (b.sem(n) for n in ("dd_ready", "dve_chain", "hi_ready", "lo_ready"))
        halved = b.sem("halved")
        NG = TOKENS // 512
        x_src = ins["xT"].rearrange("(k p) t -> p k t", p=P)
        ctx.callback(b.clear)
        block = ctx.enter_context(nc.Block())

        @block.sync
        def _(sp):
            sp.dma_start(w_step[:], ins["w_stepT"].rearrange("(k p) h -> p k h", p=P)).then_inc(const_in, 16)
            sp.dma_start(d_row[:], ins["d_rows"]).then_inc(const_in, 16)
            sp.dma_start(neg_tri[:], ins["neg_tri"]).then_inc(const_in, 16)
            for g in range(NG):
                if g >= 2:
                    sp.wait_ge(log_done, g - 1)
                sp.dma_start(xT[:, g % 2], x_src[:, :, g * 512:(g + 1) * 512]).then_inc(x_in[g % 2], 16)
                if g >= 1:
                    sp.wait_ge(parts_ready, g)
                    sp.dma_start(scratch["parts"][4 * g - 4:4 * g].rearrange("c h k s -> h c k s"),
                                 parts[:, (g - 1) % 2]).then_inc(out_done, 16)
                    sp.dma_start(scratch["steps"][4 * g - 4:4 * g].rearrange("c p k h -> p c k h"),
                                 steps[:, (g - 1) % 2]).then_inc(out_done, 16)
            sp.wait_ge(parts_ready, NG)
            g = NG
            sp.dma_start(scratch["parts"][4 * g - 4:4 * g].rearrange("c h k s -> h c k s"),
                         parts[:, (g - 1) % 2]).then_inc(out_done, 16)
            sp.dma_start(scratch["steps"][4 * g - 4:4 * g].rearrange("c p k h -> p c k h"),
                         steps[:, (g - 1) % 2]).then_inc(out_done, 16)
            sp.wait_ge(out_done, 32 * NG)

        @block.tensor
        def _(pe):
            pe.wait_ge(const_in, 48)

            def logs(g):
                pe.wait_ge(x_in[g % 2], 16 * (g // 2 + 1))
                if g >= 2:
                    pe.wait_ge(dt_ready, g - 1)
                for c in range(4):
                    for k in range(KD):
                        m = nc.tensor.matmul(a_log[:, g % 2, c * H:(c + 1) * H], xT[:, g % 2, k, c * P:(c + 1) * P],
                                             w_step[:, k, :], start=(k == 0), stop=(k == KD - 1))
                m.then_inc(log_done, 1)

            logs(0)
            for g in range(NG):
                if g + 1 < NG:
                    logs(g + 1)
                pe.wait_ge(dt_ready, g + 1)
                if g >= 2:
                    pe.wait_ge(parts_ready, g - 1)
                for c in range(4):
                    m = nc.tensor.matmul(sums[0:H, g % 2, c * P:(c + 1) * P],
                                         steps[:, g % 2, c, 0, :], neg_tri[:, :], start=True, stop=True)
                m.then_inc(sum_done, 1)

        @block.scalar
        def _(act):
            act.dma_start(w_raw[:], ins["w_projT"].rearrange("(k p) c -> p k c", p=P)).then_inc(w_in, 16)
            act.dma_start(wo_raw[:], ins["w_outT"].rearrange("(k p) c -> p k c", p=P)).then_inc(w_in, 16)
            act.dma_start(keep["conv_w"][:], ins["conv_w"].rearrange("(t p) k -> p t k", p=P)).then_inc(w_in, 16)
            act.dma_start(keep["conv_b"][:], ins["conv_b"]).then_inc(w_in, 16)
            act.dma_start(keep["z_b"][:], ins["z_b"]).then_inc(w_in, 16)
            nc.scalar.preload_act_table_set("natural_log_exp_and_others")
            for g in range(NG):
                act.wait_ge(abs_ready, g + 1)
                nc.scalar.activation(e[:], magnitude[:], ACT.Exp, scale=-1.0).then_inc(exp_done, 1)
                act.wait_ge(one_plus_ready, g + 1)
                nc.scalar.activation(lg[:], w1[:], ACT.Ln).then_inc(ln_done, 1)
                if g == 0:
                    act.wait_ge(w_in, 80)
                    nc.scalar.activation(keep["w_hi"][:], w_raw[:], ACT.Copy).then_inc(hi_ready, 1)
                    nc.scalar.activation(keep["wo_hi"][:], wo_raw[:], ACT.Copy).then_inc(hi_ready, 1)

        @block.gpsimd
        def _(pool):
            pool.wait_ge(w_in, 80)
            for t in (keep["conv_w"], keep["conv_b"], keep["z_b"]):
                nc.gpsimd.tensor_scalar(t[:], t[:], 0.5, None, ALU.mult).then_inc(halved, 1)
            pool.wait_ge(hi_ready, 2)
            nc.gpsimd.tensor_tensor(keep["w_lo"][:], w_raw[:], keep["w_hi"][:].bitcast(F32), ALU.subtract).then_inc(lo_ready, 1)
            nc.gpsimd.tensor_tensor(keep["wo_lo"][:], wo_raw[:], keep["wo_hi"][:].bitcast(F32), ALU.subtract).then_inc(lo_ready, 1)
            pool.wait_ge(lo_ready, 2)
            pool.wait_ge(halved, 3)

        @block.vector
        def _(v):
            link = Chain(v, dve_chain)
            v.wait_ge(const_in, 48)
            for g in range(NG):
                a = a_log[:, g % 2, 0:W]
                a4 = a.rearrange("p (c h) -> p c h", c=4)
                dtg, ddg = steps[:, g % 2, :, 0, :], steps[:, g % 2, :, 1, :]
                v.wait_ge(log_done, g + 1)
                link(nc.vector.tensor_scalar(r[:], a, -1.0, None, ALU.mult))
                nc.vector.tensor_tensor(magnitude[:], a, r[:], ALU.max).then_inc(abs_ready, 1)
                v.wait_ge(exp_done, g + 1)
                link(nc.vector.tensor_scalar(magnitude[:], a, 0.0, None, ALU.max))
                nc.vector.tensor_scalar(w1[:], e[:], 1.0, None, ALU.add).then_inc(one_plus_ready, 1)
                v.wait_ge(one_plus_ready, g + 1)
                link(nc.vector.tensor_scalar(r[:], w1[:], -1.0, 2.0 ** -23, ALU.add, ALU.max))
                link(nc.vector.reciprocal(r[:], r[:]))
                v.wait_ge(ln_done, g + 1)
                link(nc.vector.tensor_tensor(lg[:], lg[:], r[:], ALU.mult))
                link(nc.vector.scalar_tensor_tensor(w1[:], w1[:], 1.0, lg[:], ALU.is_equal, ALU.max))
                link(nc.vector.tensor_tensor(e[:], e[:], w1[:], ALU.mult))
                if g >= 2:
                    v.wait_ge(out_done, 32 * (g - 1))
                four = lambda t: t[:].rearrange("p (c h) -> p c h", c=4)
                nc.vector.tensor_tensor(dtg, four(magnitude), four(e), ALU.add).then_inc(dt_ready, 1)
                v.wait_ge(dt_ready, g + 1)
                nc.vector.reciprocal(ddg, dtg).then_inc(dd_ready, 1)
                v.wait_ge(dd_ready, g + 1)
                link(nc.vector.tensor_tensor(ddg, ddg, d_row[:, None, :].broadcast_to([P, 4, H]), ALU.mult))
                v.wait_ge(sum_done, g + 1)
                s = sums[0:H, g % 2, :].rearrange("h (c s) -> h c s", c=4)
                hi, mid, lo = (parts[:, g % 2, :, k, :] for k in range(3))
                rs = rest[:, :].rearrange("h (c s) -> h c s", c=4)
                link(nc.vector.tensor_copy(hi, s))
                link(nc.vector.tensor_tensor(rs, s, hi, ALU.subtract))
                link(nc.vector.tensor_copy(mid, rs))
                nc.vector.tensor_tensor(lo, rs, mid, ALU.subtract).then_inc(parts_ready, 1)




def mixer_phase(nc, ins, keep, scratch, u):
    with ExitStack() as ctx:
        b = Buffers(nc, ctx, "mix")
        ident = b.sb("ident", [P, P])
        sum_masks = b.sb("sum_masks", [P, 4, P])
        keep_rows = b.sb("keep_rows", [P, 9])
        x_raw = b.sb("x_raw", [P, KD, GROUP])
        x_hi = b.sb("x_hi", [P, 2, KD, GROUP], F32R)
        x_lo = b.sb("x_lo", [P, 2, KD, GROUP], F32R)
        raw = b.sb("raw", [P, CONV, 3 + GROUP])
        xbc = b.sb("xbc", [P, 2, CONV, GROUP])
        gate = b.sb("gate", [P, 2, 4, GROUP])
        th = b.sb("th", [P, 2, GROUP])
        zt = b.sb("zt", [P, 2, GROUP])
        mov = b.sb("mov", [94, 2, H * Q], BF16)
        stat = b.sb("stat", [94, 2, G, P], BF16)
        decay = b.sb("decay", [P, 2, 2, 512])
        cb = b.sb("cb", [P, 2, G, Q])
        sums = b.sb("sums", [P, 2, 4, H])
        steps = b.sb("steps", [P, 2, 2, H])
        x_blocks = b.sb("x_blocks", [P, 2, H, 2, HP])
        x_dec = b.sb("x_dec", [P, H, HP])
        y = b.sb("y", [P, 2, H, HP])
        tmp = b.sb("tmp", [P, H, HP])
        b_tok = b.sb("b_tok", [P, 512])
        state = b.sb("state", [P, 4, 2, Q])
        yg = b.sb("yg", [P, 4, P])
        yg_hi = b.sb("yg_hi", [P, 4, P], F32R)
        yg_lo = b.sb("yg_lo", [P, 4, P], F32R)
        x_res = b.sb("x_res", [P, 2, ROW])
        bn, bn_copy = b.sb("bn", [P, 6]), b.sb("bn_copy", [P, 1])
        ps_proj = b.ps("ps_proj", [P, 2, GROUP])
        ps_off = b.ps("ps_off", [P, H, HP])
        ps_decay = b.ps("ps_decay", [P, 2, 512])
        ps_diag = b.ps("ps_diag", [P, 2, 512])
        ps_turn = b.ps("ps_turn", [P, 512])
        ps_misc = b.ps("ps_misc", [P, 512])
        (const_in, x_in, init, x_hi_ready, x_lo_ready, proj_done, raw_ready, taps, th_ready, final, halo_ready,
         decay_done, exp_done, g_ready, diag_done, assembled, sums_done, sums_ready, xt_done, blocks_ready, xdec_ready,
         du_ready, bt_done, btok_ready, cb_done, cb_ready, off_done, st_done, state_ready, reset_ready, off_read,
         y_ready, yt_done, gated, yg_hi_ready, yg_lo_ready, out_done, res_done, bn_done, stat_done) = (b.sem(n) for n in (
            "const_in x_in init x_hi_ready x_lo_ready proj_done raw_ready taps th_ready final halo_ready "
            "decay_done exp_done g_ready diag_done assembled sums_done sums_ready xt_done blocks_ready xdec_ready "
            "du_ready bt_done btok_ready cb_done cb_ready off_done st_done state_ready reset_ready off_read "
            "y_ready yt_done gated yg_hi_ready yg_lo_ready out_done res_done bn_done stat_done").split())
        steps_in = [b.sem(f"steps_in{k}") for k in range(2)]
        parts_in = [b.sem(f"parts_in{k}") for k in range(2)]
        res_in = [b.sem(f"res_in{k}") for k in range(2)]
        kept = [b.sem(f"kept{k}") for k in range(2)]
        ctx.callback(b.clear)
        block = ctx.enter_context(nc.Block())
        NCONST = 5 + 2 * 2
        w_hi, w_lo, wo_hi, wo_lo = keep["w_hi"], keep["w_lo"], keep["wo_hi"], keep["wo_lo"]
        conv_w, conv_b, z_b = keep["conv_w"], keep["conv_b"], keep["z_b"]
        xT_src = ins["xT"].rearrange("(k p) t -> p k t", p=P)

        def run(engine, body):
            body(-1)
            body(0)
            with engine.Fori(1, 7) as i:
                body(i)
            body(7)
            body(8)

        def pair(i, m):
            k = m + 10
            return 2 * i + k // 8, k % 8, (k // 8) % 2

        def in_group(q):
            return (q // 2) % 2, (q % 2) * P

        @block.sync
        def _(sp):
            sp.dma_start(ident[:], ins["identity"]).then_inc(const_in, 16)
            sp.dma_start(sum_masks[:], ins["sum_masks"]).then_inc(const_in, 16)
            sp.dma_start(keep_rows[:], ins["keep_rows"]).then_inc(const_in, 16)
            for k in range(2):
                sp.dma_start(mov[:, k], ins["mov_const"]).then_inc(const_in, 16)
                sp.dma_start(stat[:, k], ins["stat_const"]).then_inc(const_in, 16)
            sp.wait_ge(const_in, 16 * 7)

            def body(i):
                for q in range(4):
                    if q % 2 == 0 and inside(i, 2, 2 + q // 2, 16):
                        g = 2 * i + 2 + q // 2
                        wait(sp, x_lo_ready, g)
                        sp.dma_start(x_raw[:], xT_src[:, :, bass.ds(g * GROUP, GROUP)]).then_inc(x_in, 16)
                    if inside(i, 4, q + 2, CHUNKS):
                        wait(sp, du_ready, 4 * i + q + 1)
                        sp.dma_start(steps[:, q % 2], scratch["steps"][bass.ds(4 * i + q + 2, 1)].rearrange(
                            "c p k h -> (c p) k h")).then_inc(steps_in[q % 2], 16)
                    if inside(i, 4, q + 1, CHUNKS):
                        k = (q + 1) % 2
                        wait(sp, decay_done, 4 * (4 * i + q))
                        src = scratch["parts"][bass.ds(4 * i + q + 1, 1)]
                        for part in range(3):
                            rows = src[:, :, part, :]
                            for blk in range(2):
                                r = Q + 2 * part + blk
                                sp.dma_start(mov[r:r + 1, k].rearrange("o (h s) -> o h s", s=Q),
                                             rows[:, :, blk * Q:(blk + 1) * Q]).then_inc(parts_in[k], 16)
                            r = 70 + 8 * part
                            sp.dma_start(stat[r:r + 8, k], rows.rearrange("c (g j) z -> (c j) g z", g=G)).then_inc(parts_in[k], 16)
                    if inside(i, 4, q - 2, CHUNKS):
                        wait(sp, stat_done, 4 * i + q - 1)
                        sp.dma_start(u[:, bass.ds(4 * i + q - 2, 1), :], x_res[:, q % 2, None, :]).then_inc(kept[q % 2], 16)
                    if inside(i, 4, q, CHUNKS):
                        wait(sp, kept[q % 2], 16 * (2 * i + q // 2))
                        sp.dma_start(x_res[:, q % 2, 0:D], ins["x"][bass.ds((4 * i + q) * P, P), :]).then_inc(res_in[q % 2], 16)

            run(sp, body)
            for k in range(2):
                sp.wait_ge(kept[k], 16 * CHUNKS // 2)

        @block.tensor
        def _(pe):
            pe.wait_ge(const_in, 16 * 7)
            pe.wait_ge(init, 6)

            def body(i):
                for m in range(16 if not (isinstance(i, int) and i == 8) else 4):
                    q, s = m // 4, m % 4
                    n = 16 * i + m
                    c = 4 * i + q
                    if inside(i, 16, m + 1, 128):
                        k = ((m + 1) // 4) % 2
                        if s == 3:
                            pe.wait_ge(parts_in[k], 144 * ((4 * i + q + 1 - k) // 2 + 1) if isinstance(i, int)
                                       else 144 * (2 * i + (q + 1) // 2 + 1))
                        wait(pe, exp_done, n + 1)
                        for t in range(2):
                            g = 2 * ((s + 1) % 4) + t
                            mm = nc.tensor.matmul(ps_decay[:, t, :], stat[:, k, g, :], mov[:, k, g * 512:(g + 1) * 512],
                                                  start=True, stop=True)
                        mm.then_inc(decay_done, 1)
                    if inside(i, 16, m + 10, 128):
                        g, p, slot = pair(i, m)
                        if p == 0:
                            pe.wait_ge(x_lo_ready, g + 1)
                        wait(pe, raw_ready, n + 10)
                        for t in range(2):
                            cols = slice((2 * p + t) * P, (2 * p + t + 1) * P)
                            for k in range(KD):
                                mm = product3(nc, ps_proj[:, t, :], w_hi[:, k, cols], w_lo[:, k, cols],
                                              x_hi[:, slot, k, :], x_lo[:, slot, k, :], k == 0, k == KD - 1)
                        mm.then_inc(proj_done, 1)
                    if inside(i, 4, q + 1, CHUNKS):
                        slot, t0 = in_group(q + 1)
                        tok = slice(t0, t0 + P)
                        grp = 2 * i + (q + 1) // 2
                        sl = (q + 1) % 2
                        if s == 0:
                            pe.wait_ge(steps_in[sl], 16 * ((4 * i + q + 1) // 2 + 1) if isinstance(i, int)
                                       else 16 * (2 * i + (q + 1) // 2 + 1))
                            wait(pe, cb_ready, 2 * (c + 1))
                            for k in range(4):
                                mm = nc.tensor.matmul(ps_misc[:, k * H:(k + 1) * H], sum_masks[:, k, :],
                                                      steps[:, sl, 0, :], start=True, stop=True)
                            mm.then_inc(sums_done, 1)
                            pe.wait_ge(final, 8 * grp + 2)
                            wait(pe, state_ready, 8 * (c + 1))
                            for k in range(4):
                                mm = nc.tensor.transpose(ps_turn[:, k * P:(k + 1) * P], xbc[:, slot, k, tok], ident[:])
                            mm.then_inc(xt_done, 1)
                        if s == 1:
                            pe.wait_ge(final, 8 * grp + 6)
                            pe.wait_ge(sums_ready, c + 2)
                            pe.wait_ge(du_ready, c + 2)
                            for k in range(4):
                                mm = nc.tensor.transpose(ps_turn[:, k * P:(k + 1) * P], xbc[:, slot, 4 + k, tok], ident[:])
                            mm.then_inc(bt_done, 1)
                            scores(slot, t0, 0)
                        if s == 2:
                            wait(pe, off_read, c + 1)
                            wait(pe, state_ready, 8 * (c + 1))
                            pe.wait_ge(reset_ready, (4 * i + q + 1) // 4 + 1 if isinstance(i, int) else i + (q + 1) // 4 + 1)
                            pe.wait_ge(cb_ready, 2 * c + 3)
                            from_state(slot, t0, 0)
                            scores(slot, t0, 1)
                            pe.wait_ge(btok_ready, c + 2)
                            to_state(0)
                        if s == 3:
                            pe.wait_ge(state_ready, 8 * (c + 1) + 4)
                            from_state(slot, t0, 1)
                            to_state(1)
                    if inside(i, 4, q - 1, CHUNKS):
                        if s == 0:
                            pe.wait_ge(assembled, 8 * c)
                            for k in range(4):
                                mm = nc.tensor.transpose(ps_diag[:, 1, k * P:(k + 1) * P],
                                                         y[:, (q - 1) % 2].rearrange("t h p -> t (h p)")[:, k * P:(k + 1) * P], ident[:])
                            mm.then_inc(yt_done, 1)
                        if s == 1:
                            pe.wait_ge(yg_lo_ready, c)
                            for k in range(4):
                                mm = product3(nc, ps_diag[:, 1, 0:D], yg_hi[:, k, :], yg_lo[:, k, :],
                                              wo_hi[:, k, :], wo_lo[:, k, :], k == 0, k == 3)
                            mm.then_inc(out_done, 1)
                    if inside(i, 4, q, CHUNKS):
                        pe.wait_ge(g_ready, n + 1)
                        if s == 0:
                            pe.wait_ge(blocks_ready, 2 * c + 2)
                            wait(pe, assembled, 8 * c)
                        if s == 2:
                            wait(pe, res_done, c)
                        for t in range(2):
                            for k in range(4):
                                h = 8 * (2 * s + t) + 2 * k
                                col = (2 * (s % 2) + t) * P + k * 32
                                mm = nc.tensor.matmul(ps_diag[:, s // 2, col:col + 32], decay[:, m % 2, t, k * P:(k + 1) * P],
                                                      x_blocks[:, q % 2, h:h + 2].rearrange("z h b p -> z (h b p)"),
                                                      start=True, stop=True)
                        mm.then_inc(diag_done, 1)

            def scores(slot, t0, odd):
                rows = slice(64 * odd, 64 * odd + 64)
                for k in range(4):
                    for blk in range(2):
                        toks = slice(t0 + Q * blk, t0 + Q * blk + Q)
                        mm = nc.tensor.matmul(ps_misc[Q * blk:Q * blk + Q, (4 * odd + k) * Q:(4 * odd + k + 1) * Q],
                                              xbc[rows, slot, 4 + k, toks], xbc[rows, slot, 8 + k, toks], start=True, stop=True)
                mm.then_inc(cb_done, 1)

            def from_state(slot, t0, blk):
                toks = slice(t0 + Q * blk, t0 + Q * blk + Q)
                out = ps_off[Q * blk:Q * blk + Q].rearrange("t h p -> t (h p)")
                for k in range(4):
                    mm = nc.tensor.matmul(out[:, k * P:(k + 1) * P], xbc[:, slot, 8 + k, toks],
                                          state[:, k].rearrange("n a c -> n (a c)"), start=True, stop=True)
                mm.then_inc(off_done, 1)

            def to_state(blk):
                rows = slice(Q * blk, Q * blk + Q)
                xd = x_dec[rows].rearrange("t h p -> t (h p)")
                for k in range(4):
                    mm = nc.tensor.matmul(ps_turn[:, k * P:(k + 1) * P], b_tok[rows, k * P:(k + 1) * P],
                                          xd[:, k * P:(k + 1) * P], start=True, stop=True)
                mm.then_inc(st_done, 1)

            run(pe, body)

        @block.scalar
        def _(act):
            act.wait_ge(init, 6)

            def body(i):
                for m in range(16 if not (isinstance(i, int) and i == 8) else 4):
                    q, s = m // 4, m % 4
                    n = 16 * i + m
                    c = 4 * i + q
                    if inside(i, 16, m + 1, 128):
                        act.wait_ge(decay_done, n + 2)
                        wait(act, diag_done, n)
                        nc.scalar.activation(decay[:, (m + 1) % 2], ps_decay[:], ACT.Exp).then_inc(exp_done, 1)
                    if inside(i, 16, m + 9, 128) and (m + 9) % 8 < 6:
                        g, p, slot = pair(i, m - 1)
                        conv = 6 * g + p
                        act.wait_ge(taps, 8 * (conv + 1))
                        wait(act, final, n + 9)
                        nc.scalar.activation(th[:], xbc[:, slot, 2 * p:2 * p + 2, :], ACT.Tanh).then_inc(th_ready, 1)
                    if inside(i, 16, m + 10, 128):
                        g, p, slot = pair(i, m)
                        act.wait_ge(proj_done, n + 11)
                        if p < 6:
                            if p == 0:
                                act.wait_ge(halo_ready, g + 1)
                            nc.scalar.activation(raw[:, 2 * p:2 * p + 2, 3:], ps_proj[:], ACT.Copy).then_inc(raw_ready, 1)
                        else:
                            wait(act, final, n + 10)
                            wait(act, gated, 2 * g - 2)
                            for t in range(2):
                                j = 2 * (p - 6) + t
                                nc.scalar.activation(zt[:, t], ps_proj[:, t], ACT.Tanh, bias=z_b[:, j:j + 1], scale=0.5)
                                mm = nc.scalar.activation(gate[:, slot, j], ps_proj[:, t], ACT.Identity,
                                                          bias=z_b[:, j:j + 1], scale=0.5)
                            mm.then_inc(raw_ready, 1)
                    if inside(i, 4, q + 1, CHUNKS):
                        sl = (q + 1) % 2
                        if s == 0:
                            act.wait_ge(sums_done, c + 2)
                            wait(act, off_read, c)
                            nc.scalar.activation(sums[:, sl].rearrange("p a h -> p (a h)"), ps_misc[:, 0:4 * H],
                                                 ACT.Exp).then_inc(sums_ready, 1)
                            act.wait_ge(xt_done, c + 2)
                            wait(act, diag_done, 4 * c)
                            for blk in range(2):
                                rows = slice(Q * blk, Q * blk + Q)
                                nc.scalar.activation(x_blocks[rows, sl, :, blk, :],
                                                     ps_turn[rows].rearrange("t (h p) -> t h p", p=HP), ACT.Copy)\
                                    .then_inc(blocks_ready, 1)
                        if s == 1:
                            act.wait_ge(bt_done, c + 2)
                            wait(act, st_done, 2 * (c + 1))
                            nc.scalar.activation(b_tok[:], ps_turn[:], ACT.Copy).then_inc(btok_ready, 1)
                        if s in (1, 2):
                            odd = s - 1
                            act.wait_ge(cb_done, 2 * c + 3 + odd)
                            wait(act, g_ready, 4 * c)
                            nc.scalar.activation(cb[:, sl].rearrange("z (k a) s -> z k a s", a=2)[:, :, odd],
                                                 ps_misc[:, odd * 256:odd * 256 + 256].rearrange("z (k s) -> z k s", k=4),
                                                 ACT.Copy).then_inc(cb_ready, 1)
                    if inside(i, 4, q - 1, CHUNKS) and s == 0:
                        act.wait_ge(gated, c)
                        wait(act, out_done, c - 1)
                        nc.scalar.activation(yg_hi[:], yg[:], ACT.Copy).then_inc(yg_hi_ready, 1)
                    if (m + 11) % 8 == 0 and inside(i, 2, (m + 11) // 8, 16):
                        g = 2 * i + (m + 11) // 8
                        act.wait_ge(x_in, 16 * (g + 1))
                        wait(act, proj_done, 8 * (g - 1))
                        nc.scalar.activation(x_hi[:, ((m + 11) // 8) % 2], x_raw[:], ACT.Copy).then_inc(x_hi_ready, 1)

            run(act, body)

        @block.vector
        def _(v):
            nc.vector.memset(state[:], 0.0).then_inc(reset_ready, 1)
            nc.vector.memset(x_blocks[:], 0.0).then_inc(init, 6)
            nc.vector.memset(raw[:, :, 0:3], 0.0).then_inc(halo_ready, 1)
            v.wait_ge(const_in, 16 * 7)

            def body(i):
                for m in range(16 if not (isinstance(i, int) and i == 8) else 4):
                    q, s = m // 4, m % 4
                    n = 16 * i + m
                    c = 4 * i + q
                    if inside(i, 16, m + 1, 128):
                        sc, sq = (m + 1) // 4, (m + 1) % 4
                        v.wait_ge(exp_done, n + 2)
                        v.wait_ge(cb_ready, 2 * (4 * i + sc) + 2)
                        d4 = decay[:, (m + 1) % 2].rearrange("z g (h s) -> z g h s", s=Q)
                        for t in range(2):
                            g = 2 * sq + t
                            mm = nc.vector.tensor_tensor(d4[:, t], d4[:, t],
                                                         cb[:, sc % 2, g:g + 1, :].broadcast_to([P, 8, Q]), ALU.mult)
                        mm.then_inc(g_ready, 1)
                    if inside(i, 16, m + 9, 128):
                        g, p, slot = pair(i, m - 1)
                        if p < 6:
                            v.wait_ge(th_ready, 6 * g + p + 1)
                            to, by = xbc[:, slot, 2 * p:2 * p + 2, :], th
                        else:
                            v.wait_ge(raw_ready, n + 10)
                            to, by = gate[:, slot, 2 * (p - 6):2 * (p - 6) + 2, :], zt
                        nc.vector.scalar_tensor_tensor(to, by[:], 1.0, to, ALU.add, ALU.mult).then_inc(final, 1)
                    if inside(i, 16, m + 10, 128):
                        g, p, slot = pair(i, m)
                        if p < 6:
                            base = 8 * (6 * g + p)
                            v.wait_ge(raw_ready, n + 11)
                            if p == 0:
                                wait(v, off_done, 2 * (2 * g - 2))
                            for k in range(4):
                                for t in range(2):
                                    j = 2 * p + t
                                    to = xbc[:, slot, j, :]
                                    if k == 0:
                                        nc.vector.tensor_scalar(to, raw[:, j, 3:], conv_w[:, j, 3:4], conv_b[:, j:j + 1],
                                                                ALU.mult, ALU.add).then_inc(taps, 1)
                                    else:
                                        v.wait_ge(taps, base + 2 * k + t - 1)
                                        nc.vector.scalar_tensor_tensor(to, raw[:, j, 3 - k:3 - k + GROUP], conv_w[:, j, 3 - k:4 - k],
                                                                       to, ALU.mult, ALU.add).then_inc(taps, 1)
                            if p == 5:
                                v.wait_ge(taps, base + 8)
                                if (m + 10) // 8 % 2 == 1:
                                    kr = keep_rows[:, bass.ds(i + ((m + 10) // 8 + 1) // 2, 1)]
                                    nc.vector.tensor_scalar(raw[:, :, 0:3], raw[:, :, GROUP:], kr, None, ALU.mult).then_inc(halo_ready, 1)
                                else:
                                    nc.vector.tensor_copy(raw[:, :, 0:3], raw[:, :, GROUP:]).then_inc(halo_ready, 1)
                    if inside(i, 4, q - 1, CHUNKS) and s == 0:
                        v.wait_ge(diag_done, n)
                        assemble((q - 1) % 2, 1)
                    if inside(i, 4, q + 1, CHUNKS):
                        sl = (q + 1) % 2
                        turned = ps_turn[:].rearrange("t (h p) -> t h p", p=HP)
                        if s == 0:
                            v.wait_ge(sums_ready, c + 2)
                            v.wait_ge(blocks_ready, 2 * (c + 1) + 2)
                            wait(v, st_done, 2 * (c + 1))
                            nc.vector.tensor_tensor(x_dec[:], turned, sums[:, sl, 1, :, None].broadcast_to([P, H, HP]),
                                                    ALU.mult).then_inc(xdec_ready, 1)
                            wait(v, yt_done, c)
                            nc.vector.tensor_tensor(y[:, sl], turned, steps[:, sl, 1, :, None].broadcast_to([P, H, HP]),
                                                    ALU.mult).then_inc(du_ready, 1)
                        if s >= 2:
                            blk = s - 2
                            base = 8 * (c + 1) + 4 * blk
                            v.wait_ge(off_done, 2 * (c + 1) + blk + 1)
                            for a in range(2):
                                rows = slice(64 * a, 64 * a + 64)
                                st = state[rows, :, a, :].rearrange("n k (h p) -> n k h p", p=HP)
                                el = sums[rows, sl, 2 + blk, :].rearrange("n (k a h) -> n k a h", k=4, a=2)[:, :, a, :, None]
                                nc.vector.tensor_tensor(st, st, el.broadcast_to([64, 4, 8, HP]), ALU.mult).then_inc(state_ready, 1)
                            v.wait_ge(st_done, 2 * (c + 1) + blk + 1)
                            for a in range(2):
                                rows = slice(64 * a, 64 * a + 64)
                                v.wait_ge(state_ready, base + a + 1)
                                new = ps_turn[rows].rearrange("n (k a c) -> n k a c", k=4, a=2)[:, :, a]
                                nc.vector.tensor_tensor(state[rows, :, a, :], state[rows, :, a, :], new, ALU.add).then_inc(state_ready, 1)
                            if blk == 1:
                                if q == 2:
                                    v.wait_ge(state_ready, base + 4)
                                    kr = keep_rows[:, bass.ds(i + 1, 1)]
                                    st = state[:].rearrange("n k a c -> n (k a c)")
                                    nc.vector.tensor_scalar(st, st, kr, None, ALU.mult).then_inc(reset_ready, 1)
                                nc.vector.tensor_tensor(tmp[:], ps_off[:], sums[:, sl, 0, :, None].broadcast_to([P, H, HP]),
                                                        ALU.mult).then_inc(off_read, 1)
                                v.wait_ge(off_read, c + 2)
                                nc.vector.tensor_tensor(y[:, sl], y[:, sl], tmp[:], ALU.add).then_inc(y_ready, 1)
                    if inside(i, 4, q, CHUNKS) and s == 2:
                        v.wait_ge(diag_done, n)
                        v.wait_ge(y_ready, c + 1)
                        assemble(q % 2, 0)
                    if inside(i, 4, q - 1, CHUNKS):
                        if s == 0:
                            slot, t0 = in_group(q - 1)
                            v.wait_ge(final, 8 * (2 * i + (q - 1) // 2) + 8)
                            v.wait_ge(yt_done, c)
                            wait(v, yg_lo_ready, c - 1)
                            wait(v, yg_hi_ready, c - 1)
                            nc.vector.tensor_tensor(yg[:], ps_diag[:, 1].rearrange("p (k t) -> p k t", k=4),
                                                    gate[:, slot, :, t0:t0 + P], ALU.mult).then_inc(gated, 1)
                        if s == 1:
                            v.wait_ge(yg_hi_ready, c)
                            wait(v, out_done, c - 1)
                            nc.vector.tensor_tensor(yg_lo[:], yg[:], yg_hi[:].bitcast(F32), ALU.subtract).then_inc(yg_lo_ready, 1)
                            v.wait_ge(out_done, c)
                            v.wait_ge(res_in[(q - 1) % 2], 16 * ((4 * i + q - 1) // 2 + 1) if isinstance(i, int)
                                      else 16 * (2 * i + (q - 1) // 2 + 1))
                            row = x_res[:, (q - 1) % 2]
                            nc.vector.tensor_tensor(row[:, 0:D], ps_diag[:, 1, 0:D], row[:, 0:D], ALU.add).then_inc(res_done, 1)
                            v.wait_ge(res_done, c)
                            nc.vector.bn_stats(bn[:], row[:, 0:D]).then_inc(bn_done, 1)
                            v.wait_ge(bn_done, c)
                            nc.vector.tensor_copy(bn_copy[:], bn[:, 0:1])
                            nc.vector.bn_aggr(row[:, D:ROW], bn[:]).then_inc(stat_done, 1)
                    if (m + 11) % 8 == 0 and inside(i, 2, (m + 11) // 8, 16):
                        g = 2 * i + (m + 11) // 8
                        k = ((m + 11) // 8) % 2
                        v.wait_ge(x_hi_ready, g + 1)
                        nc.vector.tensor_tensor(x_lo[:, k], x_raw[:], x_hi[:, k].bitcast(F32), ALU.subtract).then_inc(x_lo_ready, 1)

            def assemble(slot, half):
                pairs = ps_diag[:, half].rearrange("r (k a b p) -> r k a b p", k=16, a=2, b=2)
                yh = y[:, slot].rearrange("t (f k a) p -> t f k a p", f=2, a=2)[:, half]
                for blk in range(2):
                    for a in range(2):
                        to = yh[Q * blk:Q * blk + Q, :, a, :]
                        nc.vector.tensor_tensor(to, to, pairs[Q * a:Q * a + Q, :, a, blk, :], ALU.add).then_inc(assembled, 1)

            run(v, body)
            v.wait_ge(stat_done, CHUNKS)


HIDDEN, FT = 704, 6
NG = TOKENS // 512


def run_pairs(engine, body, last=NG // 2 - 1):
    body(0)
    with engine.Fori(1, last) as i:
        body(i)
    body(last)


class Normalizer:

    def __init__(self, nc, b, u):
        self.nc, self.u = nc, u
        self.var, self.scale, self.t = (b.sb(f"norm_{n}", [P, CHUNKS]) for n in ("var", "scale", "t"))
        self.chain = b.sem("norm_chain")

    def scales(self, v):
        nc = self.nc
        link = Chain(v, self.chain)
        link(nc.vector.tensor_scalar(self.var[:], self.u[:, :, D + 1], LN_EPS, None, ALU.add))
        inverse_deviation(nc, link, self.var[:], self.scale[:], self.t[:])

    def rows(self, out, c):
        one = lambda t: t.rearrange("p c d -> p (c d)")
        row = self.u[:, bass.ds(c, 1)]
        return self.nc.vector.tensor_scalar(out, one(row[:, :, 0:D]), one(row[:, :, D:D + 1]),
                                            self.scale[:, bass.ds(c, 1)], ALU.subtract, ALU.mult)


def ffn_phase(nc, ins, u):
    with ExitStack() as ctx:
        b = Buffers(nc, ctx, "ffn")
        ident, ones = b.sb("ident", [P, P]), b.sb("ones", [P, P])
        w_raw = b.sb("w_raw", [P, 3, KD * FT * P])
        w_q = b.sb("w_q", [P, 3, KD * FT * P], F32R)
        below = b.sb("below", [P, KD * FT * P])
        mags, limit, neg_limit = b.sb("mags", [P, 3]), b.sb("limit", [P, 3]), b.sb("neg_limit", [P, 3])
        norm = Normalizer(nc, b, u)
        xn = b.sb("xn", [P, 2, 4, D])
        x_hi, x_lo = b.sb("x_hi", [P, 2, KD, 512], F32R), b.sb("x_lo", [P, 2, KD, 512], F32R)
        sig, h = b.sb("sig", [P, 2, 512]), b.sb("h", [P, 2, 512])
        h_hi, h_lo = b.sb("h_hi", [P, FT, 512], F32R), b.sb("h_lo", [P, FT, 512], F32R)
        row = b.sb("row", [P, 2, ROW])
        bn, bn_copy = b.sb("bn", [P, 6]), b.sb("bn_copy", [P, 1])
        ps_gate, ps_up = b.ps("ps_gate", [P, 2, 512]), b.ps("ps_up", [P, 2, 512])
        ps_turn, ps_out = b.ps("ps_turn", [P, KD, 512]), b.ps("ps_out", [P, 2, 512])
        (const_in, w_in, mags_ready, mags_done, quantized, xn_ready, turned, x_hi_ready, x_lo_ready, up_done, sig_ready, h_ready,
         h_hi_ready, h_lo_ready, out_done, res_done, bn_done, stat_done) = (b.sem(n) for n in (
            "const_in w_in mags_ready mags_done quantized xn_ready turned x_hi_ready x_lo_ready up_done sig_ready h_ready "
            "h_hi_ready h_lo_ready out_done res_done bn_done stat_done").split())
        kept = [b.sem(f"kept{k}") for k in range(2)]
        w1, w2 = (w_q[:, k].rearrange("p (k c) -> p k c", k=KD) for k in range(2))
        w3 = w_q[:, 2].rearrange("p (f c) -> p f c", f=FT)
        ctx.callback(b.clear)
        block = ctx.enter_context(nc.Block())

        @block.sync
        def _(sp):
            for k, name in enumerate(("w1T", "w2T")):
                sp.dma_start(w_raw[:, k].rearrange("p (k c) -> p k c", k=KD),
                             ins[name].rearrange("(k p) c -> p k c", p=P)).then_inc(w_in, 16)
            sp.dma_start(w_raw[:, 2].rearrange("p (f c) -> p f c", f=FT),
                         ins["w3T"].rearrange("(f p) c -> p f c", p=P)).then_inc(w_in, 16)
            sp.dma_start(ident[:], ins["identity"]).then_inc(const_in, 16)

            def body(i):
                for k in range(2):
                    for c in range(4):
                        ci = 8 * i + 4 * k + c
                        sp.wait_ge(stat_done, ci + 1)
                        sp.dma_start(u[:, bass.ds(ci, 1), :], row[:, c % 2, None, :]).then_inc(kept[c % 2], 16)

            run_pairs(sp, body)
            for k in range(2):
                sp.wait_ge(kept[k], 16 * CHUNKS // 2)

        @block.tensor
        def _(pe):
            pe.wait_ge(mags_ready, 4)
            nc.tensor.matmul(ps_out[:, 0, 0:3], ones[:], mags[:], start=True, stop=True).then_inc(mags_done, 1)
            pe.wait_ge(const_in, 16)

            def turn(g, slot):
                pe.wait_ge(xn_ready, 4 * g + 4)
                wait(pe, x_lo_ready, g)
                for c in range(4):
                    for k in range(KD):
                        m = nc.tensor.transpose(ps_turn[:, k, c * P:(c + 1) * P], xn[:, slot, c, k * P:(k + 1) * P], ident[:])
                m.then_inc(turned, 1)

            def body(i):
                for k in range(2):
                    g = 2 * i + k
                    pe.wait_ge(x_lo_ready, g + 1)
                    for f in range(FT):
                        wait(pe, h_ready, FT * g + f - 1)
                        cols = slice(f * P, (f + 1) * P)
                        for w, out in ((w1, ps_gate), (w2, ps_up)):
                            for d in range(KD):
                                nc.tensor.matmul(out[:, f % 2], w[:, d, cols], x_hi[:, k, d], start=(d == 0), stop=False)
                                m = nc.tensor.matmul(out[:, f % 2], w[:, d, cols], x_lo[:, k, d], start=False, stop=(d == KD - 1))
                        m.then_inc(up_done, 1)
                    if inside(i, 2, k + 1, NG):
                        turn(g + 1, (k + 1) % 2)
                    for c in range(4):
                        if c == 0:
                            pe.wait_ge(h_lo_ready, FT * (g + 1))
                        wait(pe, res_done, 4 * g + c - 1)
                        toks = slice(c * P, (c + 1) * P)
                        for f in range(FT):
                            nc.tensor.matmul(ps_out[:, c % 2, 0:D], h_hi[:, f, toks], w3[:, f], start=(f == 0), stop=False)
                            m = nc.tensor.matmul(ps_out[:, c % 2, 0:D], h_lo[:, f, toks], w3[:, f], start=False, stop=(f == FT - 1))
                        m.then_inc(out_done, 1)

            turn(0, 0)
            pe.wait_ge(quantized, 6)
            run_pairs(pe, body)

        @block.scalar
        def _(act):
            def high(g, slot):
                act.wait_ge(turned, g + 1)
                nc.scalar.activation(x_hi[:, slot], ps_turn[:], ACT.Copy).then_inc(x_hi_ready, 1)

            def h_high(g, f):
                act.wait_ge(h_ready, FT * g + f + 1)
                if f == 0:
                    wait(act, out_done, 4 * g)
                nc.scalar.activation(h_hi[:, f], h[:, f % 2], ACT.Copy).then_inc(h_hi_ready, 1)

            def body(i):
                for k in range(2):
                    g = 2 * i + k
                    for f in range(FT):
                        act.wait_ge(up_done, FT * g + f + 1)
                        wait(act, h_ready, FT * g + f - 1)
                        nc.scalar.activation(sig[:, f % 2], ps_gate[:, f % 2], ACT.Sigmoid).then_inc(sig_ready, 1)
                        if f:
                            h_high(g, f - 1)
                    h_high(g, FT - 1)
                    if inside(i, 2, k + 1, NG):
                        high(g + 1, (k + 1) % 2)

            high(0, 0)
            run_pairs(act, body)

        @block.vector
        def _(v):
            nc.vector.memset(ones[:], 1.0).then_inc(mags_ready, 1)
            v.wait_ge(w_in, 48)
            for k in range(3):
                nc.vector.tensor_reduce(mags[:, k:k + 1], w_raw[:, k], AX.X, ALU.add, apply_absolute_value=True).then_inc(mags_ready, 1)
            norm.scales(v)

            def rows(g, slot):
                for c in range(4):
                    if c == 0:
                        wait(v, turned, g - 1)
                    norm.rows(xn[:, slot, c], 4 * g + c).then_inc(xn_ready, 1)

            def low(g, slot):
                v.wait_ge(x_hi_ready, g + 1)
                nc.vector.tensor_tensor(x_lo[:, slot], ps_turn[:], x_hi[:, slot].bitcast(F32), ALU.subtract).then_inc(x_lo_ready, 1)

            rows(0, 0)
            v.wait_ge(mags_done, 1)
            for t, sign in ((limit, 0.5), (neg_limit, -0.5)):
                nc.vector.tensor_scalar(t[:], ps_out[:, 0, 0:3], sign / (HIDDEN * D), sign * 1e-8, ALU.mult, ALU.add).then_inc(mags_ready, 1)
            v.wait_ge(mags_ready, 6)
            for k in range(3):
                wait(v, quantized, 2 * k)
                nc.vector.tensor_scalar(below[:], w_raw[:, k], neg_limit[:, k:k + 1], None, ALU.is_lt).then_inc(quantized, 1)
                v.wait_ge(quantized, 2 * k + 1)
                nc.vector.scalar_tensor_tensor(w_q[:, k], w_raw[:, k], limit[:, k:k + 1], below[:],
                                               ALU.is_gt, ALU.subtract).then_inc(quantized, 1)
            low(0, 0)

            def h_low(g, f):
                v.wait_ge(h_hi_ready, FT * g + f + 1)
                nc.vector.tensor_tensor(h_lo[:, f], h[:, f % 2], h_hi[:, f].bitcast(F32), ALU.subtract).then_inc(h_lo_ready, 1)

            def body(i):
                for k in range(2):
                    g = 2 * i + k
                    if inside(i, 2, k + 1, NG):
                        rows(g + 1, (k + 1) % 2)
                    for f in range(FT):
                        v.wait_ge(sig_ready, FT * g + f + 1)
                        wait(v, h_lo_ready, FT * g + f - 1)
                        nc.vector.tensor_tensor(h[:, f % 2], ps_up[:, f % 2], sig[:, f % 2], ALU.mult).then_inc(h_ready, 1)
                        if f:
                            h_low(g, f - 1)
                    h_low(g, FT - 1)
                    if inside(i, 2, k + 1, NG):
                        low(g + 1, (k + 1) % 2)
                    for c in range(4):
                        ci = 8 * i + 4 * k + c
                        v.wait_ge(out_done, ci + 1)
                        wait(v, kept[c % 2], 16 * (4 * i + 2 * k + c // 2))
                        nc.vector.tensor_tensor(row[:, c % 2, 0:D], ps_out[:, c % 2, 0:D], xn[:, k, c], ALU.add).then_inc(res_done, 1)
                        v.wait_ge(res_done, ci + 1)
                        nc.vector.bn_stats(bn[:], row[:, c % 2, 0:D]).then_inc(bn_done, 1)
                        v.wait_ge(bn_done, ci + 1)
                        nc.vector.tensor_copy(bn_copy[:], bn[:, 0:1])
                        nc.vector.bn_aggr(row[:, c % 2, D:ROW], bn[:]).then_inc(stat_done, 1)

            run_pairs(v, body)


NH, HD, NM = 16, 16, 4
VW = HD + 1
ATT_EPS = 1e-6


def attention_phase(nc, ins, u):
    with ExitStack() as ctx:
        b = Buffers(nc, ctx, "att")
        ctx.callback(b.clear)
        kept = {
            "phi_q": b.sb("phi_q", [P, NG, 2, 512]),
            "local": b.sb("local", [P, CHUNKS, D]),
            "q_sums": b.sb("q_sums", [P, NG, 2]),
            "w_hi": b.sb("w_hi", [P, KD, D], F32R), "w_lo": b.sb("w_lo", [P, KD, D], F32R),
            "mem": b.sb("mem", [P, 2, NM + 1, 8 * VW]),
            "coef": b.sb("coef", [P, NG // 2, NM + 1, NH]),
            "head_gate": b.sb("head_gate", [P, NH]),
        }
        norm = Normalizer(nc, b, u)
        causal_pass(nc, ins, u, norm, kept)
        memory_weights(nc, ins, kept)
        memory_pass(nc, ins, u, norm, kept)


def causal_pass(nc, ins, u, norm, kept):
    with ExitStack() as ctx:
        b = Buffers(nc, ctx, "causal")
        ident = b.sb("ident", [P, P])
        mask = b.sb("mask", [P, P])
        head_blocks = b.sb("head_blocks", [P, 2, 8 * VW])
        parity = b.sb("parity", [P, 2])
        keep_rows = b.sb("keep_rows", [P, NG // 2 + 1])
        w_raw = b.sb("w_raw", [P, 4, KD, D])
        w_hi, w_lo = b.sb("w_hi", [P, KD, 3 * D], F32R), b.sb("w_lo", [P, KD, 3 * D], F32R)
        xn = b.sb("xn", [P, 4, D])
        x_hi, x_lo = b.sb("x_hi", [P, 2, KD, 512], F32R), b.sb("x_lo", [P, 2, KD, 512], F32R)
        e, r = b.sb("e", [P, 2, 512]), b.sb("r", [P, 2, 512])
        pq, pk = b.sb("pq", [P, 2, 2, 512]), b.sb("pk", [P, 2, 2, 512])
        pq_half = b.sb("pq_half", [P, 2, 2, 2, 512])
        ek, rk = b.sb("ek", [P, D]), b.sb("rk", [P, D])
        k_tok = b.sb("k_tok", [P, 2, D])
        v_tok = b.sb("v_tok", [P, 2, NH, VW])
        sc = b.sb("sc", [P, 4, 2, 2, P])
        acc = b.sb("acc", [P, 2 * 8 * VW])
        state = b.sb("state", [P, 2 * 8 * VW])
        den, zero = b.sb("den", [P, NH]), b.sb("zero", [P, 2])
        red = b.sb("red", [P, 2])
        ps_turn, ps_proj = b.ps("ps_turn", [P, 512]), b.ps("ps_proj", [P, 512])
        ps_sc = b.ps("ps_sc", [P, 4, 2, 2, P])
        ps_num, ps_state = b.ps("ps_num", [P, 512]), b.ps("ps_state", [P, 512])
        (const_in, w_in, w_ready, w_lo_ready, zeroed, xn_ready, turned, x_hi_ready, x_lo_ready, kv_done, kv_read, k_ready, qk_done,
         qk_read, phi_ready, half_ready, sc_done, sc_ready, num_done, num_read, den_ready, st_done, acc_ready, state_ready,
         red_ready, sum_kept) = (b.sem(n) for n in (
            "const_in w_in w_ready w_lo_ready zeroed xn_ready turned x_hi_ready x_lo_ready kv_done kv_read k_ready qk_done "
            "qk_read phi_ready half_ready sc_done sc_ready num_done num_read den_ready st_done acc_ready state_ready "
            "red_ready sum_kept").split())
        phi_kept = [b.sem(f"phi_kept{k}") for k in range(2)]
        ctx.callback(b.clear)
        block = ctx.enter_context(nc.Block())

        def run(engine, body):
            body(-1)
            body(0)
            with engine.Fori(1, NG // 2 - 1) as i:
                body(i)
            body(NG // 2 - 1)

        def next_group(i, j):
            k = j // 4 + 1
            return (2 * i + k, k % 2) if inside(i, 2, k, NG) else (None, None)

        @block.sync
        def _(sp):
            for k, name in enumerate(("wqT", "wkT", "wvT", "woT")):
                sp.dma_start(w_raw[:, k], ins[name].rearrange("(k p) c -> p k c", p=P)).then_inc(w_in, 16)
            for t, name in ((ident, "identity"), (mask, "upper_ones"), (head_blocks, "head_blocks"), (parity, "parity"),
                            (keep_rows, "keep_batches")):
                sp.dma_start(t[:], ins[name]).then_inc(const_in, 16)

            def body(i):
                for j in (1, 5):
                    g, slot = next_group(i, j)
                    if g is not None:
                        sp.wait_ge(phi_ready, 4 * g + 2)
                        sp.dma_start(kept["phi_q"][:, bass.ds(g, 1)], pq[:, slot:slot + 1]).then_inc(phi_kept[slot], 16)

            run(sp, body)
            for k in range(2):
                sp.wait_ge(phi_kept[k], 16 * NG // 2)

        @block.tensor
        def _(pe):
            pe.wait_ge(const_in, 80)
            pe.wait_ge(w_lo_ready, 4)

            def project(out, w0, w1, g_slot, toks=None):
                for k in range(KD):
                    w = (w_hi[:, k, w0:w1], w_lo[:, k, w0:w1])
                    if toks is None:
                        m = product3(nc, out, *w, x_hi[:, g_slot, k], x_lo[:, g_slot, k], k == 0, k == KD - 1)
                    else:
                        m = product3(nc, out, x_hi[:, g_slot, k, toks], x_lo[:, g_slot, k, toks], *w, k == 0, k == KD - 1)
                return m

            def body(i):
                for j in range(8):
                    ci, c = 8 * i + j, j % 4
                    nxt = ((j + 1) // 4) % 2
                    toks = slice(((j + 1) % 4) * P, ((j + 1) % 4 + 1) * P)
                    if inside(i, 8, j + 1, CHUNKS):
                        wait(pe, kv_read, ci + 1)
                        begun = 0 if next_group(i, j)[0] is None else (0, 0, 2, 4)[c]
                        wait(pe, qk_read, 4 * (2 * i + j // 4) + 4 + begun)
                        project(ps_proj[:], D, 3 * D, nxt, toks).then_inc(kv_done, 1)
                    g, slot = next_group(i, j)
                    if g is not None:
                        if c == 0:
                            pe.wait_ge(xn_ready, 4 * g + 4)
                            for k in range(KD):
                                wait(pe, x_lo_ready, 2 * g + k)
                                for t in range(4):
                                    m = nc.tensor.transpose(ps_turn[:, t * P:(t + 1) * P], xn[:, t, k * P:(k + 1) * P], ident[:])
                                m.then_inc(turned, 1)
                        if c in (1, 2):
                            pe.wait_ge(x_lo_ready, 2 * g + 2)
                            if inside(i, 8, j + 1, CHUNKS):
                                wait(pe, kv_read, ci + 2)
                            for t in range(2):
                                n = 2 * (c - 1) + t
                                wait(pe, qk_read, 4 * g + n)
                                w0 = (c - 1) * D + t * P
                                project(ps_proj[:], w0, w0 + P, slot).then_inc(qk_done, 1)
                    if inside(i, 8, j, CHUNKS):
                        now = (j // 4) % 2
                        ts = slice(c * P, (c + 1) * P)
                        wait(pe, num_read, ci)
                        pe.wait_ge(state_ready, ci + 1)
                        pe.wait_ge(k_ready, ci + 1)
                        pe.wait_ge(sc_ready, 4 * (ci + 1))
                        for t in range(2):
                            nc.tensor.matmul(ps_num[:, t * 8 * VW:(t + 1) * 8 * VW], pq[:, now, t, ts],
                                             state[:, t * 8 * VW:(t + 1) * 8 * VW], start=(t == 0), stop=False, skip_group_check=True)
                        for h in range(NH):
                            t, rt, par = h // 8, (h % 8) // 2, h % 2
                            m = nc.tensor.matmul(ps_num[:, h * VW:(h + 1) * VW], sc[:, rt, t, par], v_tok[:, j % 2, h],
                                                 start=False, stop=(h == NH - 1), skip_group_check=True)
                        m.then_inc(num_done, 1)
                        wait(pe, acc_ready, ci)
                        for t in range(2):
                            m = nc.tensor.matmul(ps_state[:, t * 8 * VW:(t + 1) * 8 * VW], k_tok[:, j % 2, t * P:(t + 1) * P],
                                                 v_tok[:, j % 2, 8 * t:8 * t + 8].rearrange("p h e -> p (h e)"), start=True, stop=True)
                        m.then_inc(st_done, 1)
                    if inside(i, 8, j + 1, CHUNKS):
                        gn = 2 * i + (j + 1) // 4
                        pe.wait_ge(half_ready, 4 * gn + 4)
                        pe.wait_ge(phi_ready, 4 * gn + 4)
                        wait(pe, sc_ready, 4 * (ci + 1))
                        for t in range(2):
                            for rt in range(4):
                                rows = slice(32 * rt, 32 * rt + 32)
                                m = nc.tensor.matmul(ps_sc[:, rt, t], pk[rows, nxt, t, toks], pq_half[rows, nxt, t, :, toks],
                                                     start=True, stop=True, tile_position=(32 * rt, 0))
                        m.then_inc(sc_done, 1)

            run(pe, body)

        @block.scalar
        def _(act):
            act.wait_ge(w_in, 64)
            for k in range(3):
                nc.scalar.activation(w_hi[:, :, k * D:(k + 1) * D], w_raw[:, k], ACT.Copy).then_inc(w_ready, 1)
            nc.scalar.activation(kept["w_hi"][:], w_raw[:, 3], ACT.Copy).then_inc(w_ready, 1)
            act.wait_ge(zeroed, 1)

            def body(i):
                for j in range(8):
                    ci, c = 8 * i + j, j % 4
                    if inside(i, 8, j + 1, CHUNKS):
                        act.wait_ge(kv_done, ci + 2)
                        wait(act, k_ready, ci + 1)
                        wait(act, st_done, ci)
                        nc.scalar.activation(ek[:], ps_proj[:, 0:D], ACT.Exp)
                        nc.scalar.activation(rk[:], ps_proj[:, 0:D], ACT.Relu)
                        nc.scalar.activation(v_tok[:, (j + 1) % 2, :, 0:HD], ps_proj[:, D:2 * D].rearrange("p (h e) -> p h e", e=HD),
                                             ACT.Copy).then_inc(kv_read, 1)
                    g, slot = next_group(i, j)
                    if g is not None:
                        if c == 0:
                            for k in range(KD):
                                act.wait_ge(turned, 2 * g + k + 1)
                                nc.scalar.activation(x_hi[:, slot, k], ps_turn[:], ACT.Copy).then_inc(x_hi_ready, 1)
                        if c in (1, 2):
                            for t in range(2):
                                n = 4 * g + 2 * (c - 1) + t
                                act.wait_ge(qk_done, n + 1)
                                wait(act, phi_ready, n - 1)
                                nc.scalar.activation(e[:, t], ps_proj[:], ACT.Exp)
                                nc.scalar.activation(r[:, t], ps_proj[:], ACT.Relu).then_inc(qk_read, 1)

            run(act, body)

        @block.gpsimd
        def _(pool):
            for k in range(4):
                pool.wait_ge(w_ready, k + 1)
                hi, lo = ((w_hi[:, :, k * D:(k + 1) * D], w_lo[:, :, k * D:(k + 1) * D]) if k < 3 else (kept["w_hi"][:], kept["w_lo"][:]))
                nc.gpsimd.tensor_tensor(lo, w_raw[:, k], hi.bitcast(F32), ALU.subtract).then_inc(w_lo_ready, 1)

            def body(i):
                for j in (1, 5):
                    g, slot = next_group(i, j)
                    if g is not None:
                        wait(pool, sc_done, 4 * (g - 1))
                        for t in range(2):
                            pool.wait_ge(phi_ready, 4 * g + t + 1)
                            for par in range(2):
                                nc.gpsimd.tensor_tensor(pq_half[:, slot, t, par], pq[:, slot, t],
                                                        parity[:, par:par + 1].broadcast_to([P, 512]), ALU.mult).then_inc(half_ready, 1)

            run(pool, body)

        @block.vector
        def _(v):
            nc.vector.memset(v_tok[:], 1.0).then_inc(zeroed, 1)
            nc.vector.memset(acc[:], 0.0).then_inc(zeroed, 1)
            nc.vector.memset(zero[:], 0.0).then_inc(zeroed, 1)
            nc.vector.memset(state[:], 0.0).then_inc(state_ready, 1)
            v.wait_ge(zeroed, 3)
            v.wait_ge(const_in, 80)
            norm.scales(v)

            def body(i):
                for j in range(8):
                    ci, c = 8 * i + j, j % 4
                    if inside(i, 8, j, CHUNKS):
                        v.wait_ge(sc_done, ci + 1)
                        wait(v, num_done, ci)
                        for rt in range(4):
                            nc.vector.tensor_tensor(sc[:, rt].rearrange("p t a i -> p (t a) i"), ps_sc[:, rt].rearrange("p t a i -> p (t a) i"),
                                                    mask[:, None, :].broadcast_to([P, 4, P]), ALU.mult).then_inc(sc_ready, 1)
                    g, slot = next_group(i, j)
                    if g is not None:
                        if c == 0:
                            wait(v, turned, 2 * g)
                            for t in range(4):
                                norm.rows(xn[:, t], 4 * g + t).then_inc(xn_ready, 1)
                            for k in range(KD):
                                v.wait_ge(x_hi_ready, 2 * g + k + 1)
                                nc.vector.tensor_tensor(x_lo[:, slot, k], ps_turn[:], x_hi[:, slot, k].bitcast(F32), ALU.subtract)\
                                    .then_inc(x_lo_ready, 1)
                        if c in (1, 2):
                            to = (pq, pk)[c - 1]
                            if c == 1:
                                wait(v, num_done, 4 * (g - 1))
                                wait(v, half_ready, 4 * (g - 1))
                                wait(v, phi_kept[slot], 16 * (i + (j // 4 + 1) // 2))
                                wait(v, red_ready, g - 1)
                            for t in range(2):
                                v.wait_ge(qk_read, 4 * g + 2 * (c - 1) + t + 1)
                                nc.vector.scalar_tensor_tensor(to[:, slot, t], e[:, t], 1.0, r[:, t], ALU.min, ALU.add).then_inc(phi_ready, 1)
                        if c == 3:
                            v.wait_ge(phi_ready, 4 * g + 2)
                            wait(v, sum_kept, g)
                            nc.vector.tensor_reduce(red[:], pq[:, slot], AX.X, ALU.add).then_inc(red_ready, 1)
                            v.wait_ge(red_ready, g + 1)
                            nc.vector.tensor_tensor(kept["q_sums"][:, bass.ds(g, 1)].rearrange("p g t -> p (g t)"), red[:], zero[:],
                                                    ALU.add).then_inc(sum_kept, 1)
                    if inside(i, 8, j + 1, CHUNKS):
                        v.wait_ge(kv_read, ci + 2)
                        wait(v, st_done, ci)
                        nc.vector.scalar_tensor_tensor(k_tok[:, (j + 1) % 2], ek[:], 1.0, rk[:], ALU.min, ALU.add).then_inc(k_ready, 1)
                    if inside(i, 8, j, CHUNKS):
                        W2 = 2 * 8 * VW
                        v.wait_ge(st_done, ci + 1)
                        wait(v, state_ready, ci + 1)
                        old = keep_rows[:, bass.ds(i, 1)] if j == 0 else 1.0
                        new = keep_rows[:, bass.ds(i + 1, 1)] if j == 7 else 1.0
                        nc.vector.scalar_tensor_tensor(acc[:], acc[:], old, ps_state[:, 0:W2], ALU.mult, ALU.add).then_inc(acc_ready, 1)
                        v.wait_ge(acc_ready, ci + 1)
                        v.wait_ge(num_done, ci + 1)
                        nc.vector.scalar_tensor_tensor(state[:], acc[:], new, head_blocks[:].rearrange("p t c -> p (t c)"),
                                                       ALU.mult, ALU.mult).then_inc(state_ready, 1)
                        num = ps_num[:, 0:NH * VW].rearrange("p (h e) -> p h e", e=VW)
                        nc.vector.tensor_scalar(den[:], num[:, :, HD], ATT_EPS, None, ALU.max).then_inc(den_ready, 1)
                        v.wait_ge(den_ready, 2 * ci + 1)
                        nc.vector.reciprocal(den[:], den[:]).then_inc(den_ready, 1)
                        v.wait_ge(den_ready, 2 * ci + 2)
                        nc.vector.tensor_tensor(kept["local"][:, bass.ds(ci, 1)].rearrange("p c (h e) -> p (c h) e", e=HD), num[:, :, 0:HD],
                                                den[:, :, None].broadcast_to([P, NH, HD]), ALU.mult).then_inc(num_read, 1)

            run(v, body)
            v.wait_ge(num_read, CHUNKS)
            v.wait_ge(sum_kept, NG)


def memory_weights(nc, ins, kept):
    with ExitStack() as ctx:
        b = Buffers(nc, ctx, "memw")
        mem, coef = kept["mem"], kept["coef"]
        ones = b.sb("ones", [P, P])
        gate_raw = b.sb("gate_raw", [P, NH])
        mean = b.sb("mean", [P, BATCHES, 2])
        mean_rows = b.sb("mean_rows", [P, BATCHES, 2, P])
        norms = b.sb("norms", [P, NM])
        alive = b.sb("alive", [P, NM + 1])
        top, total = b.sb("top", [P, BATCHES * NH]), b.sb("total", [P, BATCHES * NH])
        rel = b.sb("rel", [P, NM, BATCHES * NH])
        ps_rel, ps_norms = b.ps("ps_rel", [P, BATCHES, 2, NM, 8]), b.ps("ps_norms", [P, 512])
        ld, step, pe_done, act_done = b.sem("ld"), b.sem("step"), b.sem("pe_done"), b.sem("act_done")
        ctx.callback(b.clear)
        block = ctx.enter_context(nc.Block())
        mem6 = mem[:].rearrange("p t m (h e) -> p t m h e", e=VW)

        @block.sync
        def _(sp):
            sp.dma_start(mem[:, :, 1:], ins["mem_blocks"]).then_inc(ld, 16)
            sp.dma_start(gate_raw[:], ins["gate_rows"]).then_inc(ld, 16)

        @block.tensor
        def _(pe):
            pe.wait_ge(step, STEPS_READY)
            nc.tensor.matmul(ps_norms[:, 0:NM], ones[:], norms[:], start=True, stop=True).then_inc(pe_done, 1)
            for s in range(BATCHES):
                for t in range(2):
                    m = nc.tensor.matmul(ps_rel[:, s, t].rearrange("p m h -> p (m h)"), mean_rows[:, s, t],
                                         mem6[:, t, 1:, :, HD],
                                         start=True, stop=True)
            m.then_inc(pe_done, 1)

        @block.scalar
        def _(act):
            act.wait_ge(ld, 32)
            nc.scalar.activation(kept["head_gate"][:], gate_raw[:], ACT.Sigmoid)
            act.wait_ge(step, EXP_READY)
            nc.scalar.activation(rel[:], rel[:], ACT.Exp).then_inc(act_done, 1)

        @block.vector
        def _(v):
            link = Chain(v, step)
            v.wait_ge(ld, 32)
            link(nc.vector.memset(ones[:], 1.0))
            link(nc.vector.tensor_tensor(mem[:, :, 0], mem[:, :, 1], mem[:, :, 2], ALU.add))
            link(nc.vector.tensor_tensor(mem[:, :, 0], mem[:, :, 0], mem[:, :, 3], ALU.add))
            link(nc.vector.tensor_tensor(mem[:, :, 0], mem[:, :, 0], mem[:, :, 4], ALU.add))
            for m in range(NM):
                link(nc.vector.tensor_reduce(norms[:, m:m + 1], mem6[:, :, m + 1, :, HD], AX.XY, ALU.add))
            gs = NG // BATCHES
            link(nc.vector.tensor_reduce(mean[:], kept["q_sums"][:].rearrange("p (s g) t -> p s t g", g=gs), AX.X, ALU.add))
            for s in range(BATCHES):
                for t in range(2):
                    link(nc.vector.tensor_scalar(mean_rows[:, s, t], ones[:], mean[:, s, t:t + 1], 1.0 / (TOKENS // BATCHES),
                                                 ALU.mult, ALU.mult))
            assert link.n == STEPS_READY
            v.wait_ge(pe_done, 2)
            link(nc.vector.tensor_scalar(alive[:, 1:], ps_norms[:, 0:NM], ATT_EPS, None, ALU.is_ge))
            link(nc.vector.tensor_reduce(alive[:, 0:1], ps_norms[:, 0:NM], AX.X, ALU.add))
            link(nc.vector.tensor_scalar(alive[:, 0:1], alive[:, 0:1], ATT_EPS, None, ALU.is_ge))
            for m in range(NM):
                link(nc.vector.tensor_copy(rel[:, m].rearrange("p (s t h) -> p s t h", s=BATCHES, t=2), ps_rel[:, :, :, m]))
            link(nc.vector.tensor_tensor(top[:], rel[:, 0], rel[:, 1], ALU.max))
            link(nc.vector.tensor_tensor(top[:], top[:], rel[:, 2], ALU.max))
            link(nc.vector.tensor_tensor(top[:], top[:], rel[:, 3], ALU.max))
            link(nc.vector.tensor_tensor(rel[:], rel[:], top[:, None, :].broadcast_to([P, NM, BATCHES * NH]), ALU.subtract))
            assert link.n == EXP_READY
            v.wait_ge(act_done, 1)
            link(nc.vector.tensor_tensor(total[:], rel[:, 0], rel[:, 1], ALU.add))
            link(nc.vector.tensor_tensor(total[:], total[:], rel[:, 2], ALU.add))
            link(nc.vector.tensor_tensor(total[:], total[:], rel[:, 3], ALU.add))
            link(nc.vector.reciprocal(total[:], total[:]))
            link(nc.vector.tensor_tensor(rel[:], rel[:], total[:, None, :].broadcast_to([P, NM, BATCHES * NH]), ALU.mult))
            link(nc.vector.memset(coef[:, :, 0], 1.0))
            link(nc.vector.tensor_scalar(coef[:, :, 0], coef[:, :, 0], alive[:, 0:1], None, ALU.mult))
            for it in range(NG // 2):
                s = it // (NG // 2 // BATCHES)
                for m in range(NM):
                    link(nc.vector.tensor_scalar(coef[:, it, m + 1], rel[:, m, s * NH:(s + 1) * NH], alive[:, m + 1:m + 2], None, ALU.mult))


STEPS_READY = 4 + NM + 1 + 2 * BATCHES
EXP_READY = STEPS_READY + 3 + NM + 4


def memory_pass(nc, ins, u, norm, kept):
    with ExitStack() as ctx:
        b = Buffers(nc, ctx, "mem")
        ident = b.sb("ident", [P, P])
        eg_w1, eg_b1 = b.sb("eg_w1", [P, KD, 64]), b.sb("eg_b1", [64, 1])
        eg_w2, eg_b2 = b.sb("eg_w2", [64, 1]), b.sb("eg_b2", [P, 1])
        pq = b.sb("pq", [P, 2, 2, P])
        den = b.sb("den", [P, 2, NM + 1, NH])
        prod = b.sb("prod", [P, 2, NM + 1, D])
        pair_sum, fine = b.sb("pair_sum", [P, 2, D]), b.sb("fine", [P, 2, D])
        c_T = b.sb("c_T", [P, 2, P])
        hidden = b.sb("hidden", [64, P])
        choice = b.sb("choice", [P, 2])
        mix = b.sb("mix", [P, 2, D])
        o_hi, o_lo = b.sb("o_hi", [P, KD, P], F32R), b.sb("o_lo", [P, KD, P], F32R)
        xn = b.sb("xn", [P, D])
        row = b.sb("row", [P, 2, ROW])
        bn, bn_copy = b.sb("bn", [P, 6]), b.sb("bn_copy", [P, 1])
        ps_a, ps_b = b.ps("ps_a", [P, 2, 512]), b.ps("ps_b", [P, 2, 512])
        ps_coarse, ps_hidden = b.ps("ps_coarse", [P, 512]), b.ps("ps_hidden", [P, 512])
        ps_turn, ps_out = b.ps("ps_turn", [P, 512]), b.ps("ps_out", [P, 512])
        (const_in, mem_done, den_ready, rden_ready, coef_ready, prod_ready, pair_ready, fine_ready, diff_ready, ct_done, ct_ready,
         hidden_done, hidden_ready, choice_done, choice_ready, mix_step, ot_done, o_hi_ready, o_lo_ready, out_done, xn_ready,
         res_done, bn_done, stat_done) = (b.sem(n) for n in (
            "const_in mem_done den_ready rden_ready coef_ready prod_ready pair_ready fine_ready diff_ready ct_done ct_ready "
            "hidden_done hidden_ready choice_done choice_ready mix_step ot_done o_hi_ready o_lo_ready out_done xn_ready "
            "res_done bn_done stat_done").split())
        pq_in = [b.sem(f"pq_in{k}") for k in range(2)]
        u_kept = [b.sem(f"u_kept{k}") for k in range(2)]
        ctx.callback(b.clear)
        block = ctx.enter_context(nc.Block())
        N8 = CHUNKS // 8

        def run(engine, body):
            body(0)
            with engine.Fori(1, N8 - 1) as i:
                body(i)
            body(N8 - 1)
            body(N8)

        def width(i):
            return 2 if isinstance(i, int) and i == N8 else 8

        @block.sync
        def _(sp):
            sp.dma_start(ident[:], ins["identity"]).then_inc(const_in, 16)
            sp.dma_start(eg_w1[:], ins["eg_w1T"].rearrange("(k p) c -> p k c", p=P)).then_inc(const_in, 16)
            for t, name in ((eg_b1, "eg_b1"), (eg_w2, "eg_w2T"), (eg_b2, "eg_b2_rows")):
                sp.dma_start(t[:], ins[name]).then_inc(const_in, 16)

            def body(i):
                for j in range(width(i)):
                    c = 8 * i + j
                    if inside(i, 8, j, CHUNKS):
                        wait(sp, mem_done, c - 1)
                        sp.dma_start(pq[:, j % 2, None], kept["phi_q"][:, bass.ds(2 * i + j // 4, 1), :, (j % 4) * P:(j % 4 + 1) * P])\
                            .then_inc(pq_in[j % 2], 16)
                    if inside(i, 8, j - 2, CHUNKS):
                        wait(sp, stat_done, c - 1)
                        sp.dma_start(u[:, bass.ds(c - 2, 1), :], row[:, j % 2, None, :]).then_inc(u_kept[j % 2], 16)

            run(sp, body)
            for k in range(2):
                sp.wait_ge(u_kept[k], 16 * CHUNKS // 2)

        @block.tensor
        def _(pe):
            pe.wait_ge(const_in, 80)

            def body(i):
                for j in range(width(i)):
                    c = 8 * i + j
                    if inside(i, 8, j, CHUNKS):
                        pe.wait_ge(pq_in[j % 2], 16 * (4 * i + j // 2 + 1))
                        wait(pe, prod_ready, 4 * c)
                        for t in range(2):
                            for out, m0, m1 in ((ps_a, 0, 3), (ps_b, 3, 5)):
                                m = nc.tensor.matmul(out[:, t, 0:(m1 - m0) * 8 * VW], pq[:, j % 2, t],
                                                     kept["mem"][:, t, m0:m1].rearrange("p m c -> p (m c)"), start=True, stop=True)
                        m.then_inc(mem_done, 1)
                    if inside(i, 8, j - 1, CHUNKS):
                        s = (j - 1) % 2
                        wait(pe, prod_ready, 4 * c)
                        wait(pe, ct_ready, c - 1)
                        for k in range(KD):
                            m = nc.tensor.transpose(ps_coarse[:, k * P:(k + 1) * P], prod[:, s, 0, k * P:(k + 1) * P], ident[:])
                        m.then_inc(ct_done, 1)
                        wait(pe, choice_ready, c - 1)
                        wait(pe, ct_ready, c)
                        for k in range(KD):
                            m = nc.tensor.matmul(ps_hidden[0:64, 0:P], eg_w1[:, k], c_T[:, k], start=(k == 0), stop=(k == KD - 1))
                        m.then_inc(hidden_done, 1)
                    if inside(i, 8, j - 2, CHUNKS):
                        wait(pe, mix_step, 4 * (c - 1))
                        wait(pe, o_lo_ready, c - 2)
                        for k in range(KD):
                            m = nc.tensor.transpose(ps_turn[:, k * P:(k + 1) * P], mix[:, j % 2, k * P:(k + 1) * P], ident[:])
                        m.then_inc(ot_done, 1)
                    if inside(i, 8, j - 1, CHUNKS):
                        wait(pe, hidden_ready, c)
                        nc.tensor.matmul(ps_hidden[:, 256:257], hidden[:], eg_w2[:], start=True, stop=True).then_inc(choice_done, 1)
                    if inside(i, 8, j - 2, CHUNKS):
                        wait(pe, res_done, c - 2)
                        wait(pe, o_lo_ready, c - 1)
                        for k in range(KD):
                            m = product3(nc, ps_out[:, 0:D], o_hi[:, k], o_lo[:, k], kept["w_hi"][:, k], kept["w_lo"][:, k],
                                         k == 0, k == KD - 1)
                        m.then_inc(out_done, 1)

            run(pe, body)

        @block.scalar
        def _(act):
            act.wait_ge(const_in, 80)

            def body(i):
                for j in range(width(i)):
                    c = 8 * i + j
                    if inside(i, 8, j - 1, CHUNKS):
                        wait(act, ct_done, c)
                        wait(act, hidden_done, c - 1)
                        nc.scalar.activation(c_T[:].rearrange("p k t -> p (k t)"), ps_coarse[:, 0:D], ACT.Copy).then_inc(ct_ready, 1)
                        wait(act, hidden_done, c)
                        wait(act, choice_done, c - 1)
                        nc.scalar.activation(hidden[:], ps_hidden[0:64, 0:P], ACT.Relu, bias=eg_b1[:]).then_inc(hidden_ready, 1)
                    if inside(i, 8, j - 2, CHUNKS):
                        wait(act, ot_done, c - 1)
                        wait(act, out_done, c - 2)
                        nc.scalar.activation(o_hi[:].rearrange("p k t -> p (k t)"), ps_turn[:, 0:D], ACT.Copy).then_inc(o_hi_ready, 1)
                    if inside(i, 8, j - 1, CHUNKS):
                        wait(act, choice_done, c)
                        wait(act, mix_step, 4 * (c - 2))
                        nc.scalar.activation(choice[:, (j - 1) % 2:(j - 1) % 2 + 1], ps_hidden[:, 256:257], ACT.Sigmoid,
                                             bias=eg_b2[:]).then_inc(choice_ready, 1)

            run(act, body)

        @block.gpsimd
        def _(pool):
            def body(i):
                for j in range(width(i)):
                    c = 8 * i + j
                    if inside(i, 8, j, CHUNKS):
                        s = j % 2
                        pool.wait_ge(prod_ready, 4 * (c + 1))
                        wait(pool, mix_step, 4 * (c - 1))
                        nc.gpsimd.tensor_tensor(pair_sum[:], prod[:, s, 1:3], prod[:, s, 3:5], ALU.add).then_inc(pair_ready, 1)
                        pool.wait_ge(pair_ready, c + 1)
                        nc.gpsimd.tensor_tensor(fine[:, s], pair_sum[:, 0], pair_sum[:, 1], ALU.add).then_inc(fine_ready, 1)
                        pool.wait_ge(fine_ready, c + 1)
                        nc.gpsimd.tensor_tensor(fine[:, s], fine[:, s], prod[:, s, 0], ALU.subtract).then_inc(diff_ready, 1)

            run(pool, body)

        @block.vector
        def _(v):
            def body(i):
                for j in range(width(i)):
                    c = 8 * i + j
                    if inside(i, 8, j, CHUNKS):
                        s = j % 2
                        v.wait_ge(mem_done, c + 1)
                        wait(v, mix_step, 4 * (c - 1))
                        wait(v, diff_ready, c - 1)
                        wait(v, ct_done, c - 1)
                        dn = den[:, s].rearrange("p m (t h) -> p m t h", t=2)
                        src = [(ps_a[:, t, 0:3 * 8 * VW].rearrange("p (m h e) -> p m h e", m=3, e=VW), 0, 3, t) for t in range(2)] + \
                              [(ps_b[:, t, 0:2 * 8 * VW].rearrange("p (m h e) -> p m h e", m=2, e=VW), 3, 5, t) for t in range(2)]
                        for ps, m0, m1, t in src:
                            nc.vector.tensor_scalar(dn[:, m0:m1, t], ps[:, :, :, HD], ATT_EPS, None, ALU.max).then_inc(den_ready, 1)
                        v.wait_ge(den_ready, 4 * c + 4)
                        nc.vector.reciprocal(den[:, s], den[:, s]).then_inc(rden_ready, 1)
                        v.wait_ge(rden_ready, c + 1)
                        nc.vector.tensor_tensor(den[:, s], den[:, s], kept["coef"][:, bass.ds(i, 1)].rearrange("p i m h -> p (i m) h"),
                                                ALU.mult).then_inc(coef_ready, 1)
                        v.wait_ge(coef_ready, c + 1)
                        pr = prod[:, s].rearrange("p m (t h e) -> p m t h e", t=2, e=HD)
                        for ps, m0, m1, t in src:
                            for_all = dn[:, m0:m1, t, :, None].broadcast_to([P, m1 - m0, 8, HD])
                            nc.vector.tensor_tensor(pr[:, m0:m1, t], ps[:, :, :, 0:HD], for_all, ALU.mult).then_inc(prod_ready, 1)
                    if inside(i, 8, j - 2, CHUNKS):
                        wait(v, o_hi_ready, c - 1)
                        wait(v, out_done, c - 2)
                        nc.vector.tensor_tensor(o_lo[:].rearrange("p k t -> p (k t)"), ps_turn[:, 0:D],
                                                o_hi[:].bitcast(F32).rearrange("p k t -> p (k t)"), ALU.subtract).then_inc(o_lo_ready, 1)
                        wait(v, res_done, c - 2)
                        norm.rows(xn[:], c - 2).then_inc(xn_ready, 1)
                    if inside(i, 8, j - 1, CHUNKS):
                        s = (j - 1) % 2
                        wait(v, diff_ready, c)
                        wait(v, choice_ready, c)
                        wait(v, ot_done, c - 2)
                        local = kept["local"][:, bass.ds(c - 1, 1)].rearrange("p c d -> p (c d)")
                        nc.vector.scalar_tensor_tensor(mix[:, s], fine[:, s], choice[:, s:s + 1], prod[:, s, 0],
                                                       ALU.mult, ALU.add).then_inc(mix_step, 1)
                        v.wait_ge(mix_step, 4 * (c - 1) + 1)
                        nc.vector.tensor_tensor(mix[:, s], mix[:, s], local, ALU.subtract).then_inc(mix_step, 1)
                        v.wait_ge(mix_step, 4 * (c - 1) + 2)
                        mh = mix[:, s].rearrange("p (h e) -> p h e", e=HD)
                        nc.vector.tensor_tensor(mh, mh, kept["head_gate"][:, :, None].broadcast_to([P, NH, HD]), ALU.mult).then_inc(mix_step, 1)
                        v.wait_ge(mix_step, 4 * (c - 1) + 3)
                        nc.vector.tensor_tensor(mix[:, s], mix[:, s], local, ALU.add).then_inc(mix_step, 1)
                    if inside(i, 8, j - 2, CHUNKS):
                        wait(v, out_done, c - 1)
                        wait(v, xn_ready, c - 1)
                        wait(v, u_kept[j % 2], 16 * ((8 * i + j - 2) // 2) if isinstance(i, int) else 16 * (4 * i + (j - 2) // 2))
                        nc.vector.tensor_tensor(row[:, j % 2, 0:D], ps_out[:, 0:D], xn[:], ALU.add).then_inc(res_done, 1)
                        wait(v, res_done, c - 1)
                        nc.vector.bn_stats(bn[:], row[:, j % 2, 0:D]).then_inc(bn_done, 1)
                        wait(v, bn_done, c - 1)
                        nc.vector.tensor_copy(bn_copy[:], bn[:, 0:1])
                        nc.vector.bn_aggr(row[:, j % 2, D:ROW], bn[:]).then_inc(stat_done, 1)

            run(v, body)


E, E1 = 16, 17
STEP = 64


def experts_phase(nc, ins, u, out):
    with ExitStack() as ctx:
        b = Buffers(nc, ctx, "moe")
        ident, ident_bf = b.sb("ident", [P, P]), b.sb("ident_bf", [P, P], BF16)
        pick = b.sb("pick", [STEP, E1, P], BF16)
        rank, r_bias = b.sb("rank", [P, E]), b.sb("r_bias", [P, E])
        wr_raw = b.sb("wr_raw", [P, KD, E])
        wr_hi, wr_lo = b.sb("wr_hi", [P, KD, E], F32R), b.sb("wr_lo", [P, KD, E], F32R)
        RAW = 4
        gu_raw, d_raw = b.sb("gu_raw", [P, RAW, KD, 2, P]), b.sb("d_raw", [P, RAW, D])
        gu_hi, gu_lo = b.sb("gu_hi", [P, E1, KD, 2, P], F32R), b.sb("gu_lo", [P, E1, KD, 2, P], F32R)
        d_hi, d_lo = b.sb("d_hi", [P, E1, D], F32R), b.sb("d_lo", [P, E1, D], F32R)
        norm = Normalizer(nc, b, u)
        xn = b.sb("xn", [P, 2, 4, D])
        x_hi, x_lo = b.sb("x_hi", [P, 2, KD, 512], F32R), b.sb("x_lo", [P, 2, KD, 512], F32R)
        logit, cand, first, second, rest = (b.sb(n, [P, 4, E]) for n in ("logit", "cand", "first", "second", "rest"))
        top, total, chosen = (b.sb(n, [P, 4]) for n in ("top", "total", "chosen"))
        weight, left = b.sb("weight", [P, 4, E1]), b.sb("left", [P, 4, E1])
        parts = b.sb("parts", [P, 4, STEP], BF16)
        w_T = b.sb("w_T", [STEP, 2, 512], BF16)
        sil, su, h = b.sb("sil", [P, 2, 512]), b.sb("su", [P, 512]), b.sb("h", [P, 2, 512])
        h_hi, h_lo = b.sb("h_hi", [P, 2, 512], F32R), b.sb("h_lo", [P, 2, 512], F32R)
        row = b.sb("row", [P, 4, D])
        bn, bn_copy, stats = b.sb("bn", [P, 4, 6]), b.sb("bn_copy", [P, 1]), b.sb("stats", [P, 4, 2])
        var, dev, dev_t = b.sb("var", [P, 4]), b.sb("dev", [P, 4]), b.sb("dev_t", [P, 4])
        ps_g, ps_u = b.ps("ps_g", [P, 2, 512]), b.ps("ps_u", [P, 2, 512])
        ps_w, ps_turn, ps_out = b.ps("ps_w", [P, 512]), b.ps("ps_turn", [P, 512]), b.ps("ps_out", [P, 4, D])
        (const_in, wr_ready, w_hi_ready, w_lo_ready, zeroed, xn_ready, turned, x_hi_ready, x_lo_ready, logits_done, route_step,
         exp_ready, wt_done, wt_ready, g_done, u_done, w_done, sil_ready, su_ready, h_ready, h_hi_ready, h_lo_ready, down_done,
         res_done, bn_done, stat_done, dev_step, row_ready, stored) = (b.sem(n) for n in (
            "const_in wr_ready w_hi_ready w_lo_ready zeroed xn_ready turned x_hi_ready x_lo_ready logits_done route_step "
            "exp_ready wt_done wt_ready g_done u_done w_done sil_ready su_ready h_ready h_hi_ready h_lo_ready down_done "
            "res_done bn_done stat_done dev_step row_ready stored").split())
        raw_in = [b.sem(f"raw_in{k}") for k in range(RAW)]
        out_rows = out.rearrange("(g c p) d -> p g c d", p=P, c=4)
        ROUTE, DEV = 25, 15
        ctx.callback(b.clear)
        block = ctx.enter_context(nc.Block())

        def run(engine, body):
            body(-1, 1)
            body(0, 0)
            body(0, 1)
            with engine.Fori(1, NG // 2 - 1) as i:
                body(i, 0)
                body(i, 1)
            body(NG // 2 - 1, 0)
            body(NG // 2 - 1, 1)
            body(NG // 2, 0)

        def exists(i, k):
            return tuple(inside(i, 2, k + d, NG) for d in (-1, 0, 1))

        def loaded(i, k, e):
            return e + 3 if isinstance(i, int) and i == 0 and k == 0 and e + 3 < E1 else None

        @block.sync
        def _(sp):
            consts = ((ident, "identity"), (ident_bf, "identity_bf"), (pick, "pick"), (rank, "rank"), (r_bias, "router_bias"))
            for t, name in consts:
                sp.dma_start(t[:], ins[name]).then_inc(const_in, 16)
            sp.dma_start(wr_raw[:], ins["router_T"].rearrange("(k p) e -> p k e", p=P)).then_inc(const_in, 16)
            for e in range(E1):
                wait(sp, w_lo_ready, e - RAW + 1)
                sp.dma_start(gu_raw[:, e % RAW].rearrange("p k w i -> p k (w i)"),
                             ins["w_gate_up"][e].rearrange("(k p) c -> p k c", p=P)).then_inc(raw_in[e % RAW], 16)
                sp.dma_start(d_raw[:, e % RAW], ins["w_down"][e]).then_inc(raw_in[e % RAW], 16)

            def body(i, k):
                if exists(i, k)[0]:
                    g = 2 * i + k - 1
                    sp.wait_ge(row_ready, 4 * (g + 1))
                    sp.dma_start(out_rows[:, bass.ds(g, 1)], row[:, None]).then_inc(stored, 16)

            run(sp, body)
            sp.wait_ge(stored, 16 * NG)

        @block.tensor
        def _(pe):
            def body(i, k):
                prev, cur, nxt = exists(i, k)
                g = 2 * i + k
                ns = (k + 1) % 2
                for e in range(E1):
                    n = E1 * g + e
                    s = (k + e) % 2
                    if cur:
                        if isinstance(i, int) and i == 0 and k == 0:
                            pe.wait_ge(w_lo_ready, e + 1)
                        if e == 0:
                            pe.wait_ge(x_lo_ready, 2 * (g + 1))
                            pe.wait_ge(wt_ready, g + 1)
                        for w, to, read, done in ((0, ps_g, sil_ready, g_done), (1, ps_u, su_ready, u_done)):
                            wait(pe, read, n - 1)
                            for d in range(KD):
                                m = product3(nc, to[:, s], gu_hi[:, e, d, w], gu_lo[:, e, d, w], x_hi[:, k, d], x_lo[:, k, d],
                                             d == 0, d == KD - 1)
                            m.then_inc(done, 1)
                        wait(pe, h_ready, n)
                        nc.tensor.matmul(ps_w[:], pick[:, e], w_T[:, k], start=True, stop=True).then_inc(w_done, 1)
                    if (cur if e >= 2 else prev):
                        ee = (e - 2) % E1
                        pe.wait_ge(h_lo_ready, n - 1)
                        if ee == 0:
                            wait(pe, res_done, 4 * g)
                        for c in range(4):
                            toks = slice(c * P, (c + 1) * P)
                            for j, (l, r) in enumerate(((h_hi, d_hi), (h_hi, d_lo), (h_lo, d_hi))):
                                m = nc.tensor.matmul(ps_out[:, c], l[:, s, toks], r[:, ee], start=(ee == 0 and c % 2 == 0 and j == 0),
                                                     stop=(ee == E1 - 1 and j == 2), skip_group_check=True)
                        m.then_inc(down_done, 1)
                    if nxt:
                        if e in (3, 5):
                            d = (e - 3) // 2
                            if e == 3:
                                pe.wait_ge(xn_ready, 4 * (g + 2))
                                wait(pe, wt_ready, g + 1)
                                if isinstance(i, int) and i < 0:
                                    pe.wait_ge(const_in, 96)
                                    pe.wait_ge(zeroed, 2)
                            else:
                                pe.wait_ge(x_lo_ready, 2 * (g + 1) + 1)
                            for c in range(4):
                                m = nc.tensor.transpose(ps_turn[:, c * P:(c + 1) * P], xn[:, ns, c, d * P:(d + 1) * P], ident[:])
                            m.then_inc(turned, 1)
                        if e == 7:
                            pe.wait_ge(x_lo_ready, 2 * (g + 2))
                            pe.wait_ge(wr_ready, 2)
                            for c in range(4):
                                toks = slice(c * P, (c + 1) * P)
                                for d in range(KD):
                                    m = product3(nc, ps_turn[:, c * E:(c + 1) * E], x_hi[:, ns, d, toks], x_lo[:, ns, d, toks],
                                                 wr_hi[:, d], wr_lo[:, d], d == 0, d == KD - 1)
                            m.then_inc(logits_done, 1)
                        if e == 15:
                            pe.wait_ge(route_step, ROUTE * (g + 2))
                            for c in range(4):
                                m = nc.tensor.matmul(ps_turn[0:STEP, c * P:(c + 1) * P], parts[:, c], ident_bf[:], start=True, stop=True)
                            m.then_inc(wt_done, 1)
                    if not (cur or nxt) and e == 1:
                        break

            run(pe, body)

        @block.scalar
        def _(act):
            act.wait_ge(const_in, 96)
            nc.scalar.activation(wr_hi[:], wr_raw[:], ACT.Copy).then_inc(wr_ready, 1)

            def weights(e):
                act.wait_ge(raw_in[e % RAW], 32 * (e // RAW + 1))
                nc.scalar.activation(gu_hi[:, e], gu_raw[:, e % RAW], ACT.Copy)
                nc.scalar.activation(d_hi[:, e], d_raw[:, e % RAW], ACT.Copy).then_inc(w_hi_ready, 1)

            def body(i, k):
                prev, cur, nxt = exists(i, k)
                g = 2 * i + k
                ns = (k + 1) % 2
                for e in range(E1):
                    n = E1 * g + e
                    s = (k + e) % 2
                    if cur:
                        act.wait_ge(g_done, n + 1)
                        wait(act, su_ready, n - 1)
                        nc.scalar.activation(sil[:, s], ps_g[:, s], ACT.Silu).then_inc(sil_ready, 1)
                    if (cur if e >= 1 else prev):
                        act.wait_ge(h_ready, n)
                        wait(act, down_done, n - 2)
                        nc.scalar.activation(h_hi[:, 1 - s], h[:, 1 - s], ACT.Copy).then_inc(h_hi_ready, 1)
                    if loaded(i, k, e):
                        weights(loaded(i, k, e))
                    if nxt:
                        if e in (3, 5):
                            act.wait_ge(turned, 2 * (g + 1) + (e - 3) // 2 + 1)
                            nc.scalar.activation(x_hi[:, ns, (e - 3) // 2], ps_turn[:], ACT.Copy).then_inc(x_hi_ready, 1)
                        if e == 9:
                            act.wait_ge(route_step, ROUTE * (g + 1) + 3)
                            nc.scalar.activation(rest[:], rest[:], ACT.Exp).then_inc(exp_ready, 1)
                        if e == 15:
                            act.wait_ge(wt_done, g + 2)
                            nc.scalar.activation(w_T[:, ns], ps_turn[0:STEP, :], ACT.Copy).then_inc(wt_ready, 1)
                    if not (cur or nxt) and e == 0:
                        break

            body(-1, 1)
            for e in range(3):
                weights(e)
            body(0, 0)
            body(0, 1)
            with act.Fori(1, NG // 2 - 1) as i:
                body(i, 0)
                body(i, 1)
            body(NG // 2 - 1, 0)
            body(NG // 2 - 1, 1)
            body(NG // 2, 0)

        @block.gpsimd
        def _(pool):
            pool.wait_ge(wr_ready, 1)
            nc.gpsimd.tensor_tensor(wr_lo[:], wr_raw[:], wr_hi[:].bitcast(F32), ALU.subtract).then_inc(wr_ready, 1)

            def weights(e):
                pool.wait_ge(w_hi_ready, e + 1)
                nc.gpsimd.tensor_tensor(gu_lo[:, e], gu_raw[:, e % RAW], gu_hi[:, e].bitcast(F32), ALU.subtract)
                nc.gpsimd.tensor_tensor(d_lo[:, e], d_raw[:, e % RAW], d_hi[:, e].bitcast(F32), ALU.subtract).then_inc(w_lo_ready, 1)

            def body(i, k):
                cur = exists(i, k)[1]
                for e in range(E1):
                    n = E1 * (2 * i + k) + e
                    s = (k + e) % 2
                    if cur:
                        pool.wait_ge(h_hi_ready, n + 1)
                        wait(pool, down_done, n - 1)
                        nc.gpsimd.tensor_tensor(h_lo[:, s], h[:, s], h_hi[:, s].bitcast(F32), ALU.subtract).then_inc(h_lo_ready, 1)
                    if loaded(i, k, e):
                        weights(loaded(i, k, e))

            for e in range(3):
                weights(e)
            run(pool, body)

        @block.vector
        def _(v):
            nc.vector.memset(parts[:], 0.0).then_inc(zeroed, 1)
            nc.vector.memset(weight[:], 1.0).then_inc(zeroed, 1)
            v.wait_ge(zeroed, 2)
            v.wait_ge(const_in, 96)
            norm.scales(v)

            def over(t, width):
                return t[:, :, None].broadcast_to([P, 4, width])

            def route(g, part):
                if part == 0:
                    link = Chain(v, route_step, ROUTE * g)
                    lg = ps_turn[:, 0:4 * E].rearrange("p (c e) -> p c e", e=E)
                    link(nc.vector.tensor_tensor(logit[:], lg, r_bias[:, None, :].broadcast_to([P, 4, E]), ALU.add))
                    link(nc.vector.tensor_reduce(top[:], logit[:], AX.X, ALU.max))
                    link(nc.vector.tensor_tensor(rest[:], logit[:], over(top, E), ALU.subtract))
                if part == 1:
                    link = Chain(v, route_step, ROUTE * g + 3)
                    link(nc.vector.tensor_tensor(cand[:], logit[:], over(top, E), ALU.is_equal))
                    link(nc.vector.tensor_tensor(cand[:], cand[:], rank[:, None, :].broadcast_to([P, 4, E]), ALU.mult))
                    link(nc.vector.tensor_reduce(top[:], cand[:], AX.X, ALU.max))
                    link(nc.vector.tensor_tensor(first[:], cand[:], over(top, E), ALU.is_equal))
                    link(nc.vector.scalar_tensor_tensor(logit[:], first[:], -1e30, logit[:], ALU.mult, ALU.add))
                if part == 2:
                    link = Chain(v, route_step, ROUTE * g + 8)
                    link(nc.vector.tensor_reduce(top[:], logit[:], AX.X, ALU.max))
                    link(nc.vector.tensor_tensor(cand[:], logit[:], over(top, E), ALU.is_equal))
                    link(nc.vector.tensor_tensor(cand[:], cand[:], rank[:, None, :].broadcast_to([P, 4, E]), ALU.mult))
                    link(nc.vector.tensor_reduce(top[:], cand[:], AX.X, ALU.max))
                    link(nc.vector.tensor_tensor(second[:], cand[:], over(top, E), ALU.is_equal))
                if part == 3:
                    link = Chain(v, route_step, ROUTE * g + 13)
                    v.wait_ge(exp_ready, g + 1)
                    link(nc.vector.tensor_tensor(first[:], first[:], second[:], ALU.add))
                    link(nc.vector.tensor_tensor(first[:], first[:], rest[:], ALU.mult))
                    link(nc.vector.tensor_reduce(total[:], rest[:], AX.X, ALU.add))
                    link(nc.vector.tensor_reduce(chosen[:], first[:], AX.X, ALU.add))
                    link(nc.vector.scalar_tensor_tensor(chosen[:], total[:], 1e-9, chosen[:], ALU.mult, ALU.add))
                if part == 4:
                    link = Chain(v, route_step, ROUTE * g + 18)
                    link(nc.vector.reciprocal(chosen[:], chosen[:]))
                    link(nc.vector.tensor_tensor(weight[:, :, 0:E], first[:], over(chosen, E), ALU.mult))
                    wait(v, wt_done, g)
                    hi, mid, lo = (parts[:, :, k * E1:(k + 1) * E1] for k in range(3))
                    link(nc.vector.tensor_copy(hi, weight[:]))
                    link(nc.vector.tensor_tensor(left[:], weight[:], hi, ALU.subtract))
                    link(nc.vector.tensor_copy(mid, left[:]))
                    link(nc.vector.tensor_tensor(left[:], left[:], mid, ALU.subtract))
                    link(nc.vector.tensor_copy(lo, left[:]))

            def deviation(g, part):
                link = Chain(v, dev_step, DEV * g + 3 * part)
                if part == 0:
                    link(nc.vector.tensor_scalar(var[:], stats[:, :, 1], LN_EPS, None, ALU.add))
                    first_guess(nc, link, var[:], dev[:], dev_t[:])
                else:
                    newton_step(nc, link, var[:], dev[:], dev_t[:])

            def body(i, k):
                prev, cur, nxt = exists(i, k)
                g = 2 * i + k
                ns = (k + 1) % 2
                for e in range(E1):
                    n = E1 * g + e
                    s = (k + e) % 2
                    if prev:
                        if e == 2:
                            v.wait_ge(down_done, E1 * g)
                            wait(v, stored, 16 * (g - 1))
                            for c in range(4):
                                nc.vector.tensor_tensor(row[:, c], ps_out[:, c], xn[:, ns, c], ALU.add).then_inc(res_done, 1)
                        if e == 3:
                            v.wait_ge(res_done, 4 * g)
                            for c in range(4):
                                nc.vector.bn_stats(bn[:, c], row[:, c]).then_inc(bn_done, 1)
                            v.wait_ge(bn_done, 4 * g)
                            nc.vector.tensor_copy(bn_copy[:], bn[:, 3, 0:1])
                            for c in range(4):
                                nc.vector.bn_aggr(stats[:, c], bn[:, c]).then_inc(stat_done, 1)
                        if e in (4, 5, 6, 7, 8):
                            if e == 4:
                                v.wait_ge(stat_done, 4 * g)
                            deviation(g - 1, e - 4)
                        if e == 9:
                            for c in range(4):
                                nc.vector.tensor_scalar(row[:, c], row[:, c], stats[:, c, 0:1], dev[:, c:c + 1],
                                                        ALU.subtract, ALU.mult).then_inc(row_ready, 1)
                    if cur:
                        v.wait_ge(sil_ready, n + 1)
                        v.wait_ge(u_done, n + 1)
                        wait(v, h_ready, n)
                        nc.vector.tensor_tensor(su[:], ps_u[:, s], sil[:, s], ALU.mult).then_inc(su_ready, 1)
                        v.wait_ge(su_ready, n + 1)
                        v.wait_ge(w_done, n + 1)
                        wait(v, h_lo_ready, n - 1)
                        nc.vector.tensor_tensor(h[:, s], ps_w[:], su[:], ALU.mult).then_inc(h_ready, 1)
                    if nxt:
                        if e == 2:
                            for c in range(4):
                                norm.rows(xn[:, ns, c], 4 * (g + 1) + c).then_inc(xn_ready, 1)
                        if e in (3, 5):
                            d = (e - 3) // 2
                            v.wait_ge(x_hi_ready, 2 * (g + 1) + d + 1)
                            nc.vector.tensor_tensor(x_lo[:, ns, d], ps_turn[:], x_hi[:, ns, d].bitcast(F32), ALU.subtract).then_inc(x_lo_ready, 1)
                        if e == 8:
                            v.wait_ge(logits_done, g + 2)
                        if e in (8, 9, 10, 11, 12):
                            route(g + 1, e - 8)
                    if not (cur or nxt) and e == 9:
                        break

            run(v, body)


def mixer_constants():
    import numpy as np

    t = np.arange(P)
    same = (t[:, None] // Q) == (t[None, :] // Q)
    upto = same & (t[:, None] <= t[None, :])
    after = same & (t[:, None] > t[None, :])
    first = np.repeat((t < Q)[:, None], P, 1)
    sums = -np.stack([upto, after, first, ~first], 1).astype(np.float32)
    stat = np.zeros((94, G, P), np.float32)
    stat[:Q] = np.where((t[None, :] % Q) > np.arange(Q)[:, None], -1e30, 0.0)[:, None, :]
    for k in range(3):
        for block in range(2):
            stat[Q + 2 * k + block] = (t // Q == block)
    mov = np.zeros((94, H, Q), np.float32)
    mov[:Q] = np.eye(Q)[:, None, :]
    for k in range(3):
        for j in range(8):
            mov[70 + 8 * k + j, j::8] = -1
    keep = np.ones((P, 9), np.float32)
    keep[:, 4] = 0
    bf = np.dtype("bfloat16")
    return {"neg_tri": np.ascontiguousarray(sums[:, 0]), "sum_masks": sums, "stat_const": stat.astype(bf),
            "mov_const": mov.reshape(94, H * Q).astype(bf), "keep_rows": keep, "identity": np.eye(P, dtype=np.float32)}


def layouts(x):
    import numpy as np

    c = np.ascontiguousarray
    tokens = c(x["L0_attn_input_"]).reshape(TOKENS, D)
    w_in = x["L0_attn_in_proj_w"]
    a = {
        "x": tokens, "xT": c(tokens.T), "w_projT": c(w_in[:2048].T), "w_stepT": c(w_in[2048:].T),
        "d_rows": c(np.broadcast_to(x["L0_attn_D"], (P, H))),
        "conv_w": c(x["L0_attn_conv1d_weight"].reshape(CONV * P, 4)),
        "conv_b": c(x["L0_attn_conv1d_bias"].reshape(CONV, P).T),
        "z_b": c(x["L0_attn_z_bias"].reshape(4, P).T),
        "w_outT": c(x["L0_attn_out_proj_w"].T),
        "w1T": np.pad(x["L0_ffn_w1"].T, ((0, 0), (0, FT * P - HIDDEN))),
        "w2T": np.pad(x["L0_ffn_w2"].T, ((0, 0), (0, FT * P - HIDDEN))),
        "w3T": np.pad(x["L0_ffn_w3"].T, ((0, FT * P - HIDDEN), (0, 0))),
    }
    for n in "qkvo":
        a[f"w{n}T"] = c(x[f"L1_attn_w_{n}"].T)
    mem = np.zeros((2, 8, HD, NM, 8, VW), np.float32)
    fine = x["L1_attn_fine_memories"].reshape(NM, 2, 8, HD, HD)
    norms = x["L1_attn_fine_memory_norms"].reshape(NM, 2, 8, HD)
    for h in range(8):
        mem[:, h, :, :, h, :HD] = fine[:, :, h].transpose(1, 2, 0, 3)
        mem[:, h, :, :, h, HD] = norms[:, :, h].transpose(1, 2, 0)
    a["mem_blocks"] = c(mem.reshape(2, P, NM, 8 * VW).transpose(1, 0, 2, 3))
    a["gate_rows"] = c(np.broadcast_to(x["L1_attn_memory_gate"], (P, NH)))
    a["eg_w1T"], a["eg_w2T"] = c(x["L1_attn_eg_w1"].T), c(x["L1_attn_eg_w2"].T)
    a["eg_b1"] = c(x["L1_attn_eg_b1"].reshape(64, 1))
    a["eg_b2_rows"] = c(np.broadcast_to(x["L1_attn_eg_b2"], (P, 1)))
    a.update(mixer_constants())
    ch = np.arange(P)
    blocks = (ch[:, None] // HD == np.arange(8)[None, :]).astype(np.float32)
    a["head_blocks"] = c(np.broadcast_to(np.repeat(blocks, VW, 1)[:, None], (P, 2, 8 * VW)))
    a["parity"] = np.stack([(ch // HD % 2 == k).astype(np.float32) for k in range(2)], 1)
    a["upper_ones"] = np.triu(np.ones((P, P), np.float32))
    kb = np.ones((P, NG // 2 + 1), np.float32)
    kb[:, 2] = 0
    a["keep_batches"] = kb
    stack = lambda n: np.concatenate([x[f"L1_ffn_{n}"], x[f"L1_ffn_s{n}"][None]])
    a["w_gate_up"], a["w_down"] = np.concatenate([stack("Wg"), stack("Wu")], 2), stack("Wd")
    a["router_T"], a["router_bias"] = c(x["L1_ffn_Wr"].T), c(np.broadcast_to(x["L1_ffn_bias"], (P, E)))
    a["rank"] = c(np.broadcast_to(np.arange(E, 0, -1, dtype=np.float32), (P, E)))
    pick = np.zeros((STEP, E1, P), np.float32)
    for k in range(3):
        for e in range(E1):
            pick[k * E1 + e, e] = 1
    a["pick"], a["identity_bf"] = pick.astype(a["stat_const"].dtype), a["identity"].astype(a["stat_const"].dtype)
    return a


def mixer_keep(nc, ctx):
    b = Buffers(nc, ctx, "keep")
    return {
        "w_hi": b.sb("w_hi", [P, KD, 2048], F32R), "w_lo": b.sb("w_lo", [P, KD, 2048], F32R),
        "wo_hi": b.sb("wo_hi", [P, 4, D], F32R), "wo_lo": b.sb("wo_lo", [P, 4, D], F32R),
        "conv_w": b.sb("conv_w", [P, CONV, 4]), "conv_b": b.sb("conv_b", [P, CONV]), "z_b": b.sb("z_b", [P, 4]),
    }


def build_program(nc, ins, out):
    with ExitStack() as ctx:
        u = Buffers(nc, ctx, "all").sb("u", [P, CHUNKS, ROW])
        scratch = {"steps": nc.dram_tensor("steps_scratch", [CHUNKS, P, 2, H], F32).ap(),
                   "parts": nc.dram_tensor("parts_scratch", [CHUNKS, H, 3, P], BF16).ap()}
        with ExitStack() as mixer_ctx:
            keep = mixer_keep(nc, mixer_ctx)
            steps_phase(nc, ins, keep, scratch)
            mixer_phase(nc, ins, keep, scratch, u)
        ffn_phase(nc, ins, u)
        attention_phase(nc, ins, u)
        experts_phase(nc, ins, u, out)


def kernel(**inputs):
    import numpy as np
    import concourse.bacc as bacc
    from concourse.bass_utils import run_bass_kernel_spmd

    nc = bacc.Bacc("TRN2", target_bir_lowering=False, num_devices=1)
    arrays = {name: np.ascontiguousarray(a) for name, a in layouts({k: np.asarray(a) for k, a in inputs.items()}).items()}
    ins = {name: nc.dram_tensor(name, list(a.shape), mybir.dt.from_np(a.dtype), kind="ExternalInput").ap()
           for name, a in arrays.items()}
    out = nc.dram_tensor("out", [TOKENS, D], F32, kind="ExternalOutput").ap()
    build_program(nc, ins, out)
    launched = run_bass_kernel_spmd(nc, [arrays], core_ids=[0])
    return launched.results[0]["out"].reshape(BATCHES, TOKENS // BATCHES, D)
```

```python
from contextlib import ExitStack

import concourse.bass as bass
from concourse import mybir

F32 = mybir.dt.float32
F32R = mybir.dt.float32r
BF16 = mybir.dt.bfloat16
I32 = mybir.dt.int32
U32 = mybir.dt.uint32
ALU = mybir.AluOpType
ACT = mybir.ActivationFunctionType
AX = mybir.AxisListType

P = 128
TOKENS, D = 4096, 256
CHUNKS = TOKENS // P
BATCHES = 2
KD = D // P
LN_EPS = 1e-5
ROW = D + 2
H = 64
HP = 8
G = 8
Q = 64
CONV = 12
TILES = 16
GROUP = 256


def wait(engine, sem, value):
    if not isinstance(value, int) or value > 0:
        engine.wait_ge(sem, value)


def inside(i, per, k, end):
    return not isinstance(i, int) or 0 <= per * i + k < end


class Buffers:

    def __init__(self, nc, ctx, phase):
        self.nc, self.ctx, self.phase, self.sems = nc, ctx, phase, []

    def sb(self, name, shape, dt=F32):
        return self.ctx.enter_context(self.nc.sbuf_tensor(f"{self.phase}_{name}", shape, dt))

    def ps(self, name, shape, dt=F32):
        return self.ctx.enter_context(self.nc.psum_tensor(f"{self.phase}_{name}", shape, dt))

    def sem(self, name):
        self.sems.append(self.nc.alloc_semaphore(f"{self.phase}_{name}"))
        return self.sems[-1]

    def clear(self):
        self.nc.clear_and_free_semaphores(self.sems)
        self.nc.all_engine_barrier()


def product3(nc, out, l_hi, l_lo, r_hi, r_lo, first, last):
    nc.tensor.matmul(out, l_hi, r_hi, start=first, stop=False)
    nc.tensor.matmul(out, l_hi, r_lo, start=False, stop=False)
    return nc.tensor.matmul(out, l_lo, r_hi, start=False, stop=last)


class Chain:

    def __init__(self, engine, sem, n=0):
        self.engine, self.sem, self.n = engine, sem, n

    def __call__(self, instruction):
        self.n = self.n + 1
        instruction.then_inc(self.sem, 1)
        self.engine.wait_ge(self.sem, self.n)


def first_guess(nc, link, v, y, t):
    link(nc.vector.tensor_scalar(t.bitcast(I32), v.bitcast(I32), 1, None, ALU.logical_shift_right))
    link(nc.vector.tensor_scalar(y.bitcast(I32), t.bitcast(I32), -1.0, float(0x5F3759DF), ALU.mult, ALU.add))


def newton_step(nc, link, v, y, t):
    link(nc.vector.scalar_tensor_tensor(t, y, -0.5, y, ALU.mult, ALU.mult))
    link(nc.vector.tensor_tensor(t, t, v, ALU.mult))
    link(nc.vector.scalar_tensor_tensor(y, t, 1.5, y, ALU.add, ALU.mult))


def inverse_deviation(nc, link, v, y, t):
    first_guess(nc, link, v, y, t)
    for _ in range(4):
        newton_step(nc, link, v, y, t)


def steps_phase(nc, ins, keep, scratch):
    with ExitStack() as ctx:
        b = Buffers(nc, ctx, "steps")
        xT = b.sb("xT", [P, 2, KD, 512])
        w_step = b.sb("w_step", [P, KD, H])
        d_row = b.sb("d_row", [P, H])
        neg_tri = b.sb("neg_tri", [P, P])
        W = 4 * H
        e, w1, magnitude, r, lg = (b.sb(n, [P, W]) for n in ("e", "w1", "magnitude", "r", "lg"))
        steps = b.sb("steps", [P, 2, 4, 2, H])
        parts = b.sb("parts", [H, 2, 4, 3, P], BF16)
        rest = b.sb("rest", [H, 512])
        w_raw = b.sb("w_raw", [P, KD, 2048])
        wo_raw = b.sb("wo_raw", [P, 4, D])
        a_log = b.ps("a_log", [P, 2, 512])
        sums = b.ps("sums", [P, 2, 512])
        x_in = [b.sem(f"x_in{k}") for k in range(2)]
        const_in, w_in, out_done = b.sem("const_in"), b.sem("w_in"), b.sem("out_done")
        log_done, abs_ready, exp_done, one_plus_ready = (b.sem(n) for n in ("log_done", "abs_ready", "exp_done", "one_plus_ready"))
        ln_done, dt_ready, sum_done, parts_ready = (b.sem(n) for n in ("ln_done", "dt_ready", "sum_done", "parts_ready"))
        dd_ready, dve_chain, hi_ready, lo_ready = (b.sem(n) for n in ("dd_ready", "dve_chain", "hi_ready", "lo_ready"))
        halved = b.sem("halved")
        NG = TOKENS // 512
        x_src = ins["xT"].rearrange("(k p) t -> p k t", p=P)
        ctx.callback(b.clear)
        block = ctx.enter_context(nc.Block())

        @block.sync
        def _(sp):
            sp.dma_start(w_step[:], ins["w_stepT"].rearrange("(k p) h -> p k h", p=P)).then_inc(const_in, 16)
            sp.dma_start(d_row[:], ins["d_rows"]).then_inc(const_in, 16)
            sp.dma_start(neg_tri[:], ins["neg_tri"]).then_inc(const_in, 16)
            for g in range(NG):
                if g >= 2:
                    sp.wait_ge(log_done, g - 1)
                sp.dma_start(xT[:, g % 2], x_src[:, :, g * 512:(g + 1) * 512]).then_inc(x_in[g % 2], 16)
                if g >= 1:
                    sp.wait_ge(parts_ready, g)
                    sp.dma_start(scratch["parts"][4 * g - 4:4 * g].rearrange("c h k s -> h c k s"),
                                 parts[:, (g - 1) % 2]).then_inc(out_done, 16)
                    sp.dma_start(scratch["steps"][4 * g - 4:4 * g].rearrange("c p k h -> p c k h"),
                                 steps[:, (g - 1) % 2]).then_inc(out_done, 16)
            sp.wait_ge(parts_ready, NG)
            g = NG
            sp.dma_start(scratch["parts"][4 * g - 4:4 * g].rearrange("c h k s -> h c k s"),
                         parts[:, (g - 1) % 2]).then_inc(out_done, 16)
            sp.dma_start(scratch["steps"][4 * g - 4:4 * g].rearrange("c p k h -> p c k h"),
                         steps[:, (g - 1) % 2]).then_inc(out_done, 16)
            sp.wait_ge(out_done, 32 * NG)

        @block.tensor
        def _(pe):
            pe.wait_ge(const_in, 48)

            def logs(g):
                pe.wait_ge(x_in[g % 2], 16 * (g // 2 + 1))
                if g >= 2:
                    pe.wait_ge(dt_ready, g - 1)
                for c in range(4):
                    for k in range(KD):
                        m = nc.tensor.matmul(a_log[:, g % 2, c * H:(c + 1) * H], xT[:, g % 2, k, c * P:(c + 1) * P],
                                             w_step[:, k, :], start=(k == 0), stop=(k == KD - 1))
                m.then_inc(log_done, 1)

            logs(0)
            for g in range(NG):
                if g + 1 < NG:
                    logs(g + 1)
                pe.wait_ge(dt_ready, g + 1)
                if g >= 2:
                    pe.wait_ge(parts_ready, g - 1)
                for c in range(4):
                    m = nc.tensor.matmul(sums[0:H, g % 2, c * P:(c + 1) * P],
                                         steps[:, g % 2, c, 0, :], neg_tri[:, :], start=True, stop=True)
                m.then_inc(sum_done, 1)

        @block.scalar
        def _(act):
            act.dma_start(w_raw[:], ins["w_projT"].rearrange("(k p) c -> p k c", p=P)).then_inc(w_in, 16)
            act.dma_start(wo_raw[:], ins["w_outT"].rearrange("(k p) c -> p k c", p=P)).then_inc(w_in, 16)
            act.dma_start(keep["conv_w"][:], ins["conv_w"].rearrange("(t p) k -> p t k", p=P)).then_inc(w_in, 16)
            act.dma_start(keep["conv_b"][:], ins["conv_b"]).then_inc(w_in, 16)
            act.dma_start(keep["z_b"][:], ins["z_b"]).then_inc(w_in, 16)
            nc.scalar.preload_act_table_set("natural_log_exp_and_others")
            for g in range(NG):
                act.wait_ge(abs_ready, g + 1)
                nc.scalar.activation(e[:], magnitude[:], ACT.Exp, scale=-1.0).then_inc(exp_done, 1)
                act.wait_ge(one_plus_ready, g + 1)
                nc.scalar.activation(lg[:], w1[:], ACT.Ln).then_inc(ln_done, 1)
                if g == 0:
                    act.wait_ge(w_in, 80)
                    nc.scalar.activation(keep["w_hi"][:], w_raw[:], ACT.Copy).then_inc(hi_ready, 1)
                    nc.scalar.activation(keep["wo_hi"][:], wo_raw[:], ACT.Copy).then_inc(hi_ready, 1)

        @block.gpsimd
        def _(pool):
            pool.wait_ge(w_in, 80)
            for t in (keep["conv_w"], keep["conv_b"], keep["z_b"]):
                nc.gpsimd.tensor_scalar(t[:], t[:], 0.5, None, ALU.mult).then_inc(halved, 1)
            pool.wait_ge(hi_ready, 2)
            nc.gpsimd.tensor_tensor(keep["w_lo"][:], w_raw[:], keep["w_hi"][:].bitcast(F32), ALU.subtract).then_inc(lo_ready, 1)
            nc.gpsimd.tensor_tensor(keep["wo_lo"][:], wo_raw[:], keep["wo_hi"][:].bitcast(F32), ALU.subtract).then_inc(lo_ready, 1)
            pool.wait_ge(lo_ready, 2)
            pool.wait_ge(halved, 3)

        @block.vector
        def _(v):
            link = Chain(v, dve_chain)
            v.wait_ge(const_in, 48)
            for g in range(NG):
                a = a_log[:, g % 2, 0:W]
                a4 = a.rearrange("p (c h) -> p c h", c=4)
                dtg, ddg = steps[:, g % 2, :, 0, :], steps[:, g % 2, :, 1, :]
                v.wait_ge(log_done, g + 1)
                link(nc.vector.tensor_scalar(r[:], a, -1.0, None, ALU.mult))
                nc.vector.tensor_tensor(magnitude[:], a, r[:], ALU.max).then_inc(abs_ready, 1)
                v.wait_ge(exp_done, g + 1)
                link(nc.vector.tensor_scalar(magnitude[:], a, 0.0, None, ALU.max))
                nc.vector.tensor_scalar(w1[:], e[:], 1.0, None, ALU.add).then_inc(one_plus_ready, 1)
                v.wait_ge(one_plus_ready, g + 1)
                link(nc.vector.tensor_scalar(r[:], w1[:], -1.0, 2.0 ** -23, ALU.add, ALU.max))
                link(nc.vector.reciprocal(r[:], r[:]))
                v.wait_ge(ln_done, g + 1)
                link(nc.vector.tensor_tensor(lg[:], lg[:], r[:], ALU.mult))
                link(nc.vector.scalar_tensor_tensor(w1[:], w1[:], 1.0, lg[:], ALU.is_equal, ALU.max))
                link(nc.vector.tensor_tensor(e[:], e[:], w1[:], ALU.mult))
                if g >= 2:
                    v.wait_ge(out_done, 32 * (g - 1))
                four = lambda t: t[:].rearrange("p (c h) -> p c h", c=4)
                nc.vector.tensor_tensor(dtg, four(magnitude), four(e), ALU.add).then_inc(dt_ready, 1)
                v.wait_ge(dt_ready, g + 1)
                nc.vector.reciprocal(ddg, dtg).then_inc(dd_ready, 1)
                v.wait_ge(dd_ready, g + 1)
                link(nc.vector.tensor_tensor(ddg, ddg, d_row[:, None, :].broadcast_to([P, 4, H]), ALU.mult))
                v.wait_ge(sum_done, g + 1)
                s = sums[0:H, g % 2, :].rearrange("h (c s) -> h c s", c=4)
                hi, mid, lo = (parts[:, g % 2, :, k, :] for k in range(3))
                rs = rest[:, :].rearrange("h (c s) -> h c s", c=4)
                link(nc.vector.tensor_copy(hi, s))
                link(nc.vector.tensor_tensor(rs, s, hi, ALU.subtract))
                link(nc.vector.tensor_copy(mid, rs))
                nc.vector.tensor_tensor(lo, rs, mid, ALU.subtract).then_inc(parts_ready, 1)




def mixer_phase(nc, ins, keep, scratch, u):
    with ExitStack() as ctx:
        b = Buffers(nc, ctx, "mix")
        ident = b.sb("ident", [P, P])
        sum_masks = b.sb("sum_masks", [P, 4, P])
        keep_rows = b.sb("keep_rows", [P, 9])
        x_raw = b.sb("x_raw", [P, KD, GROUP])
        x_hi = b.sb("x_hi", [P, 2, KD, GROUP], F32R)
        x_lo = b.sb("x_lo", [P, 2, KD, GROUP], F32R)
        raw = b.sb("raw", [P, CONV, 3 + GROUP])
        xbc = b.sb("xbc", [P, 2, CONV, GROUP])
        gate = b.sb("gate", [P, 2, 4, GROUP])
        th = b.sb("th", [P, 2, GROUP])
        zt = b.sb("zt", [P, 2, 2, GROUP])
        mov = b.sb("mov", [94, 2, H * Q], BF16)
        stat = b.sb("stat", [94, 2, G, P], BF16)
        decay = b.sb("decay", [P, 2, 2, 512])
        cb = b.sb("cb", [P, 2, G, Q])
        sums = b.sb("sums", [P, 2, 4, H])
        steps = b.sb("steps", [P, 2, 2, H])
        x_blocks = b.sb("x_blocks", [P, 2, H, 2, HP])
        x_dec = b.sb("x_dec", [P, H, HP])
        y = b.sb("y", [P, 2, H, HP])
        tmp = b.sb("tmp", [P, H, HP])
        b_tok = b.sb("b_tok", [P, 512])
        state = b.sb("state", [P, 4, 2, Q])
        yg = b.sb("yg", [P, 4, P])
        yg_hi = b.sb("yg_hi", [P, 4, P], F32R)
        yg_lo = b.sb("yg_lo", [P, 4, P], F32R)
        x_res = b.sb("x_res", [P, 2, ROW])
        bn, bn_copy = b.sb("bn", [P, 6]), b.sb("bn_copy", [P, 1])
        ps_proj = b.ps("ps_proj", [P, 2, GROUP])
        ps_off = b.ps("ps_off", [P, H, HP])
        ps_decay = b.ps("ps_decay", [P, 2, 512])
        ps_diag = b.ps("ps_diag", [P, 2, 512])
        ps_turn = b.ps("ps_turn", [P, 512])
        ps_misc = b.ps("ps_misc", [P, 512])
        (const_in, x_in, init, x_hi_ready, x_lo_ready, proj_done, raw_ready, taps, th_ready, final, halo_ready,
         decay_done, exp_done, g_ready, diag_done, assembled, sums_done, sums_ready, xt_done, blocks_ready, xdec_ready,
         du_ready, bt_done, btok_ready, cb_done, cb_ready, off_done, st_done, state_ready, reset_ready, off_read,
         y_ready, yt_done, gated, yg_hi_ready, yg_lo_ready, out_done, res_done, bn_done, stat_done) = (b.sem(n) for n in (
            "const_in x_in init x_hi_ready x_lo_ready proj_done raw_ready taps th_ready final halo_ready "
            "decay_done exp_done g_ready diag_done assembled sums_done sums_ready xt_done blocks_ready xdec_ready "
            "du_ready bt_done btok_ready cb_done cb_ready off_done st_done state_ready reset_ready off_read "
            "y_ready yt_done gated yg_hi_ready yg_lo_ready out_done res_done bn_done stat_done").split())
        steps_in = [b.sem(f"steps_in{k}") for k in range(2)]
        parts_in = [b.sem(f"parts_in{k}") for k in range(2)]
        res_in = [b.sem(f"res_in{k}") for k in range(2)]
        kept = [b.sem(f"kept{k}") for k in range(2)]
        ctx.callback(b.clear)
        block = ctx.enter_context(nc.Block())
        NCONST = 5 + 2 * 2
        w_hi, w_lo, wo_hi, wo_lo = keep["w_hi"], keep["w_lo"], keep["wo_hi"], keep["wo_lo"]
        conv_w, conv_b, z_b = keep["conv_w"], keep["conv_b"], keep["z_b"]
        xT_src = ins["xT"].rearrange("(k p) t -> p k t", p=P)

        def run(engine, body):
            body(-1)
            body(0)
            with engine.Fori(1, 7) as i:
                body(i)
            body(7)
            body(8)

        def pair(i, m):
            k = m + 11
            return 2 * i + k // 8, k % 8, (k // 8) % 2

        def in_group(q):
            return (q // 2) % 2, (q % 2) * P

        @block.sync
        def _(sp):
            sp.dma_start(ident[:], ins["identity"]).then_inc(const_in, 16)
            sp.dma_start(sum_masks[:], ins["sum_masks"]).then_inc(const_in, 16)
            sp.dma_start(keep_rows[:], ins["keep_rows"]).then_inc(const_in, 16)
            for k in range(2):
                sp.dma_start(mov[:, k], ins["mov_const"]).then_inc(const_in, 16)
                sp.dma_start(stat[:, k], ins["stat_const"]).then_inc(const_in, 16)
            sp.wait_ge(const_in, 16 * 7)

            def body(i):
                for q in range(4):
                    if q % 2 == 0 and inside(i, 2, 2 + q // 2, 16):
                        g = 2 * i + 2 + q // 2
                        wait(sp, x_lo_ready, g)
                        sp.dma_start(x_raw[:], xT_src[:, :, bass.ds(g * GROUP, GROUP)]).then_inc(x_in, 16)
                    if inside(i, 4, q + 2, CHUNKS):
                        wait(sp, du_ready, 4 * i + q + 1)
                        sp.dma_start(steps[:, q % 2], scratch["steps"][bass.ds(4 * i + q + 2, 1)].rearrange(
                            "c p k h -> (c p) k h")).then_inc(steps_in[q % 2], 16)
                    if inside(i, 4, q + 1, CHUNKS):
                        k = (q + 1) % 2
                        wait(sp, decay_done, 4 * (4 * i + q))
                        src = scratch["parts"][bass.ds(4 * i + q + 1, 1)]
                        for part in range(3):
                            rows = src[:, :, part, :]
                            for blk in range(2):
                                r = Q + 2 * part + blk
                                sp.dma_start(mov[r:r + 1, k].rearrange("o (h s) -> o h s", s=Q),
                                             rows[:, :, blk * Q:(blk + 1) * Q]).then_inc(parts_in[k], 16)
                            r = 70 + 8 * part
                            sp.dma_start(stat[r:r + 8, k], rows.rearrange("c (g j) z -> (c j) g z", g=G)).then_inc(parts_in[k], 16)
                    if inside(i, 4, q - 2, CHUNKS):
                        wait(sp, stat_done, 4 * i + q - 1)
                        sp.dma_start(u[:, bass.ds(4 * i + q - 2, 1), :], x_res[:, q % 2, None, :]).then_inc(kept[q % 2], 16)
                    if inside(i, 4, q, CHUNKS):
                        wait(sp, kept[q % 2], 16 * (2 * i + q // 2))
                        sp.dma_start(x_res[:, q % 2, 0:D], ins["x"][bass.ds((4 * i + q) * P, P), :]).then_inc(res_in[q % 2], 16)

            run(sp, body)
            for k in range(2):
                sp.wait_ge(kept[k], 16 * CHUNKS // 2)

        @block.tensor
        def _(pe):
            pe.wait_ge(const_in, 16 * 7)
            pe.wait_ge(init, 6)

            def body(i):
                for m in range(16 if not (isinstance(i, int) and i == 8) else 4):
                    q, s = m // 4, m % 4
                    n = 16 * i + m
                    c = 4 * i + q
                    if inside(i, 16, m + 1, 128):
                        k = ((m + 1) // 4) % 2
                        if s == 3:
                            pe.wait_ge(parts_in[k], 144 * ((4 * i + q + 1 - k) // 2 + 1) if isinstance(i, int)
                                       else 144 * (2 * i + (q + 1) // 2 + 1))
                        wait(pe, exp_done, n + 1)
                        for t in range(2):
                            g = 2 * ((s + 1) % 4) + t
                            mm = nc.tensor.matmul(ps_decay[:, t, :], stat[:, k, g, :], mov[:, k, g * 512:(g + 1) * 512],
                                                  start=True, stop=True)
                        mm.then_inc(decay_done, 1)
                    if inside(i, 16, m + 11, 128):
                        g, p, slot = pair(i, m)
                        if p == 0:
                            pe.wait_ge(x_lo_ready, g + 1)
                        wait(pe, raw_ready, n + 11)
                        for t in range(2):
                            cols = slice((2 * p + t) * P, (2 * p + t + 1) * P)
                            for k in range(KD):
                                mm = product3(nc, ps_proj[:, t, :], w_hi[:, k, cols], w_lo[:, k, cols],
                                              x_hi[:, slot, k, :], x_lo[:, slot, k, :], k == 0, k == KD - 1)
                        mm.then_inc(proj_done, 1)
                    if inside(i, 4, q + 1, CHUNKS):
                        slot, t0 = in_group(q + 1)
                        tok = slice(t0, t0 + P)
                        grp = 2 * i + (q + 1) // 2
                        sl = (q + 1) % 2
                        if s == 0:
                            pe.wait_ge(steps_in[sl], 16 * ((4 * i + q + 1) // 2 + 1) if isinstance(i, int)
                                       else 16 * (2 * i + (q + 1) // 2 + 1))
                            wait(pe, cb_ready, 2 * (c + 1))
                            for k in range(4):
                                mm = nc.tensor.matmul(ps_misc[:, k * H:(k + 1) * H], sum_masks[:, k, :],
                                                      steps[:, sl, 0, :], start=True, stop=True)
                            mm.then_inc(sums_done, 1)
                            pe.wait_ge(final, 8 * grp + 2)
                            wait(pe, state_ready, 8 * (c + 1))
                            for k in range(4):
                                mm = nc.tensor.transpose(ps_turn[:, k * P:(k + 1) * P], xbc[:, slot, k, tok], ident[:])
                            mm.then_inc(xt_done, 1)
                        if s == 1:
                            pe.wait_ge(final, 8 * grp + 6)
                            pe.wait_ge(sums_ready, c + 2)
                            pe.wait_ge(du_ready, c + 2)
                            for k in range(4):
                                mm = nc.tensor.transpose(ps_turn[:, k * P:(k + 1) * P], xbc[:, slot, 4 + k, tok], ident[:])
                            mm.then_inc(bt_done, 1)
                            scores(slot, t0, 0)
                        if s == 2:
                            wait(pe, off_read, c + 1)
                            wait(pe, state_ready, 8 * (c + 1))
                            pe.wait_ge(reset_ready, (4 * i + q + 1) // 4 + 1 if isinstance(i, int) else i + (q + 1) // 4 + 1)
                            pe.wait_ge(cb_ready, 2 * c + 3)
                            from_state(slot, t0, 0)
                            scores(slot, t0, 1)
                            pe.wait_ge(btok_ready, c + 2)
                            to_state(0)
                        if s == 3:
                            pe.wait_ge(state_ready, 8 * (c + 1) + 4)
                            from_state(slot, t0, 1)
                            to_state(1)
                    if inside(i, 4, q - 1, CHUNKS):
                        if s == 0:
                            pe.wait_ge(assembled, 8 * c)
                            for k in range(4):
                                mm = nc.tensor.transpose(ps_diag[:, 1, k * P:(k + 1) * P],
                                                         y[:, (q - 1) % 2].rearrange("t h p -> t (h p)")[:, k * P:(k + 1) * P], ident[:])
                            mm.then_inc(yt_done, 1)
                        if s == 1:
                            pe.wait_ge(yg_lo_ready, c)
                            for k in range(4):
                                mm = product3(nc, ps_diag[:, 1, 0:D], yg_hi[:, k, :], yg_lo[:, k, :],
                                              wo_hi[:, k, :], wo_lo[:, k, :], k == 0, k == 3)
                            mm.then_inc(out_done, 1)
                    if inside(i, 4, q, CHUNKS):
                        pe.wait_ge(g_ready, n + 1)
                        if s == 0:
                            pe.wait_ge(blocks_ready, 2 * c + 2)
                            wait(pe, assembled, 8 * c)
                        if s == 2:
                            wait(pe, res_done, c)
                        for t in range(2):
                            for k in range(4):
                                h = 8 * (2 * s + t) + 2 * k
                                col = (2 * (s % 2) + t) * P + k * 32
                                mm = nc.tensor.matmul(ps_diag[:, s // 2, col:col + 32], decay[:, m % 2, t, k * P:(k + 1) * P],
                                                      x_blocks[:, q % 2, h:h + 2].rearrange("z h b p -> z (h b p)"),
                                                      start=True, stop=True)
                        mm.then_inc(diag_done, 1)

            def scores(slot, t0, odd):
                rows = slice(64 * odd, 64 * odd + 64)
                for k in range(4):
                    for blk in range(2):
                        toks = slice(t0 + Q * blk, t0 + Q * blk + Q)
                        mm = nc.tensor.matmul(ps_misc[Q * blk:Q * blk + Q, (4 * odd + k) * Q:(4 * odd + k + 1) * Q],
                                              xbc[rows, slot, 4 + k, toks], xbc[rows, slot, 8 + k, toks], start=True, stop=True)
                mm.then_inc(cb_done, 1)

            def from_state(slot, t0, blk):
                toks = slice(t0 + Q * blk, t0 + Q * blk + Q)
                out = ps_off[Q * blk:Q * blk + Q].rearrange("t h p -> t (h p)")
                for k in range(4):
                    mm = nc.tensor.matmul(out[:, k * P:(k + 1) * P], xbc[:, slot, 8 + k, toks],
                                          state[:, k].rearrange("n a c -> n (a c)"), start=True, stop=True)
                mm.then_inc(off_done, 1)

            def to_state(blk):
                rows = slice(Q * blk, Q * blk + Q)
                xd = x_dec[rows].rearrange("t h p -> t (h p)")
                for k in range(4):
                    mm = nc.tensor.matmul(ps_turn[:, k * P:(k + 1) * P], b_tok[rows, k * P:(k + 1) * P],
                                          xd[:, k * P:(k + 1) * P], start=True, stop=True)
                mm.then_inc(st_done, 1)

            run(pe, body)

        @block.scalar
        def _(act):
            act.wait_ge(init, 6)

            def body(i):
                for m in range(16 if not (isinstance(i, int) and i == 8) else 4):
                    q, s = m // 4, m % 4
                    n = 16 * i + m
                    c = 4 * i + q
                    if inside(i, 16, m + 1, 128):
                        act.wait_ge(decay_done, n + 2)
                        wait(act, diag_done, n)
                        nc.scalar.activation(decay[:, (m + 1) % 2], ps_decay[:], ACT.Exp).then_inc(exp_done, 1)
                    if inside(i, 16, m + 9, 128) and (m + 9) % 8 < 6:
                        g, p, slot = pair(i, m - 2)
                        conv = 6 * g + p
                        act.wait_ge(taps, 6 * (conv + 1))
                        wait(act, final, n + 9)
                        nc.scalar.activation(th[:], xbc[:, slot, 2 * p:2 * p + 2, :], ACT.Tanh).then_inc(th_ready, 1)
                    if inside(i, 16, m + 11, 128):
                        g, p, slot = pair(i, m)
                        act.wait_ge(proj_done, n + 12)
                        if p < 6:
                            if p == 0:
                                act.wait_ge(halo_ready, g + 1)
                                wait(act, off_done, 2 * (2 * g - 2))
                            nc.scalar.activation(raw[:, 2 * p:2 * p + 2, 3:], ps_proj[:], ACT.Copy)
                            for t in range(2):
                                j = 2 * p + t
                                mm = nc.scalar.activation(xbc[:, slot, j, :], ps_proj[:, t], ACT.Identity,
                                                          bias=conv_b[:, j:j + 1], scale=conv_w[:, j, 3:4])
                            mm.then_inc(raw_ready, 1)
                        else:
                            wait(act, final, n + 4)
                            wait(act, gated, 2 * g - 2)
                            for t in range(2):
                                j = 2 * (p - 6) + t
                                nc.scalar.activation(zt[:, p % 2, t], ps_proj[:, t], ACT.Tanh, bias=z_b[:, j:j + 1], scale=0.5)
                                mm = nc.scalar.activation(gate[:, slot, j], ps_proj[:, t], ACT.Identity,
                                                          bias=z_b[:, j:j + 1], scale=0.5)
                            mm.then_inc(raw_ready, 1)
                    if inside(i, 4, q + 1, CHUNKS):
                        sl = (q + 1) % 2
                        if s == 0:
                            act.wait_ge(sums_done, c + 2)
                            wait(act, off_read, c)
                            nc.scalar.activation(sums[:, sl].rearrange("p a h -> p (a h)"), ps_misc[:, 0:4 * H],
                                                 ACT.Exp).then_inc(sums_ready, 1)
                            act.wait_ge(xt_done, c + 2)
                            wait(act, diag_done, 4 * c)
                            for blk in range(2):
                                rows = slice(Q * blk, Q * blk + Q)
                                nc.scalar.activation(x_blocks[rows, sl, :, blk, :],
                                                     ps_turn[rows].rearrange("t (h p) -> t h p", p=HP), ACT.Copy)\
                                    .then_inc(blocks_ready, 1)
                        if s == 1:
                            act.wait_ge(bt_done, c + 2)
                            wait(act, st_done, 2 * (c + 1))
                            nc.scalar.activation(b_tok[:], ps_turn[:], ACT.Copy).then_inc(btok_ready, 1)
                        if s in (1, 2):
                            odd = s - 1
                            act.wait_ge(cb_done, 2 * c + 3 + odd)
                            wait(act, g_ready, 4 * c)
                            nc.scalar.activation(cb[:, sl].rearrange("z (k a) s -> z k a s", a=2)[:, :, odd],
                                                 ps_misc[:, odd * 256:odd * 256 + 256].rearrange("z (k s) -> z k s", k=4),
                                                 ACT.Copy).then_inc(cb_ready, 1)
                    if inside(i, 4, q - 1, CHUNKS) and s == 0:
                        act.wait_ge(gated, c)
                        wait(act, out_done, c - 1)
                        nc.scalar.activation(yg_hi[:], yg[:], ACT.Copy).then_inc(yg_hi_ready, 1)
                    if (m + 13) % 8 == 0 and inside(i, 2, (m + 13) // 8, 16):
                        g = 2 * i + (m + 13) // 8
                        act.wait_ge(x_in, 16 * (g + 1))
                        wait(act, proj_done, 8 * (g - 1))
                        nc.scalar.activation(x_hi[:, ((m + 13) // 8) % 2], x_raw[:], ACT.Copy).then_inc(x_hi_ready, 1)

            run(act, body)

        @block.gpsimd
        def _(pool):
            def body(i):
                for m in range(16 if not (isinstance(i, int) and i == 8) else 4):
                    q, s = m // 4, m % 4
                    n = 16 * i + m
                    c = 4 * i + q
                    if inside(i, 16, m + 1, 128):
                        sc, sq = (m + 1) // 4, (m + 1) % 4
                        pool.wait_ge(exp_done, n + 2)
                        pool.wait_ge(cb_ready, 2 * (4 * i + sc) + 2)
                        d4 = decay[:, (m + 1) % 2].rearrange("z g (h s) -> z g h s", s=Q)
                        for t in range(2):
                            g = 2 * sq + t
                            mm = nc.gpsimd.tensor_tensor(d4[:, t], d4[:, t],
                                                         cb[:, sc % 2, g:g + 1, :].broadcast_to([P, 8, Q]), ALU.mult)
                        mm.then_inc(g_ready, 1)
                    if inside(i, 4, q + 1, CHUNKS) and s == 3:
                        sl = (q + 1) % 2
                        pool.wait_ge(off_read, c + 2)
                        pool.wait_ge(du_ready, c + 2)
                        nc.gpsimd.tensor_tensor(y[:, sl], y[:, sl], tmp[:], ALU.add).then_inc(y_ready, 1)

            run(pool, body)

        @block.vector
        def _(v):
            nc.vector.memset(state[:], 0.0).then_inc(reset_ready, 1)
            nc.vector.memset(x_blocks[:], 0.0).then_inc(init, 6)
            nc.vector.memset(raw[:, :, 0:3], 0.0).then_inc(halo_ready, 1)
            v.wait_ge(const_in, 16 * 7)

            def body(i):
                for m in range(16 if not (isinstance(i, int) and i == 8) else 4):
                    q, s = m // 4, m % 4
                    n = 16 * i + m
                    c = 4 * i + q
                    if inside(i, 4, q - 1, CHUNKS) and s == 0:
                        v.wait_ge(diag_done, n)
                        assemble((q - 1) % 2, 1)
                    if inside(i, 4, q - 1, CHUNKS) and s == 1:
                        v.wait_ge(yg_hi_ready, c)
                        wait(v, out_done, c - 1)
                        nc.vector.tensor_tensor(yg_lo[:], yg[:], yg_hi[:].bitcast(F32), ALU.subtract).then_inc(yg_lo_ready, 1)
                    if inside(i, 4, q - 1, CHUNKS) and s == 2:
                        v.wait_ge(out_done, c)
                        v.wait_ge(res_in[(q - 1) % 2], 16 * ((4 * i + q - 1) // 2 + 1) if isinstance(i, int)
                                  else 16 * (2 * i + (q - 1) // 2 + 1))
                        row = x_res[:, (q - 1) % 2]
                        nc.vector.tensor_tensor(row[:, 0:D], ps_diag[:, 1, 0:D], row[:, 0:D], ALU.add).then_inc(res_done, 1)
                        v.wait_ge(res_done, c)
                        nc.vector.bn_stats(bn[:], row[:, 0:D]).then_inc(bn_done, 1)
                        v.wait_ge(bn_done, c)
                        nc.vector.tensor_copy(bn_copy[:], bn[:, 0:1])
                        nc.vector.bn_aggr(row[:, D:ROW], bn[:]).then_inc(stat_done, 1)
                    if inside(i, 16, m + 10, 128):
                        g, p, slot = pair(i, m - 1)
                        if p < 6:
                            base = 6 * (6 * g + p)
                            v.wait_ge(raw_ready, n + 11)
                            for k in range(1, 4):
                                for t in range(2):
                                    j = 2 * p + t
                                    to = xbc[:, slot, j, :]
                                    if k > 1:
                                        v.wait_ge(taps, base + 2 * (k - 2) + t + 1)
                                    nc.vector.scalar_tensor_tensor(to, raw[:, j, 3 - k:3 - k + GROUP], conv_w[:, j, 3 - k:4 - k],
                                                                   to, ALU.mult, ALU.add).then_inc(taps, 1)
                            if p == 5:
                                v.wait_ge(taps, base + 6)
                                if (m + 10) // 8 % 2 == 1:
                                    kr = keep_rows[:, bass.ds(i + ((m + 10) // 8 + 1) // 2, 1)]
                                    nc.vector.tensor_scalar(raw[:, :, 0:3], raw[:, :, GROUP:], kr, None, ALU.mult).then_inc(halo_ready, 1)
                                else:
                                    nc.vector.tensor_copy(raw[:, :, 0:3], raw[:, :, GROUP:]).then_inc(halo_ready, 1)
                    if inside(i, 16, m + 9, 128):
                        g, p, slot = pair(i, m - 2)
                        if p < 6:
                            v.wait_ge(th_ready, 6 * g + p + 1)
                            to, by = xbc[:, slot, 2 * p:2 * p + 2, :], th[:]
                        else:
                            v.wait_ge(raw_ready, n + 10)
                            to, by = gate[:, slot, 2 * (p - 6):2 * (p - 6) + 2, :], zt[:, p % 2]
                        nc.vector.scalar_tensor_tensor(to, by, 1.0, to, ALU.add, ALU.mult).then_inc(final, 1)
                    if inside(i, 4, q + 1, CHUNKS):
                        sl = (q + 1) % 2
                        turned = ps_turn[:].rearrange("t (h p) -> t h p", p=HP)
                        if s == 0:
                            v.wait_ge(sums_ready, c + 2)
                            v.wait_ge(blocks_ready, 2 * (c + 1) + 2)
                            wait(v, st_done, 2 * (c + 1))
                            nc.vector.tensor_tensor(x_dec[:], turned, sums[:, sl, 1, :, None].broadcast_to([P, H, HP]),
                                                    ALU.mult).then_inc(xdec_ready, 1)
                            wait(v, yt_done, c)
                            nc.vector.tensor_tensor(y[:, sl], turned, steps[:, sl, 1, :, None].broadcast_to([P, H, HP]),
                                                    ALU.mult).then_inc(du_ready, 1)
                        if s >= 2:
                            blk = s - 2
                            base = 8 * (c + 1) + 4 * blk
                            v.wait_ge(off_done, 2 * (c + 1) + blk + 1)
                            for a in range(2):
                                rows = slice(64 * a, 64 * a + 64)
                                st = state[rows, :, a, :].rearrange("n k (h p) -> n k h p", p=HP)
                                el = sums[rows, sl, 2 + blk, :].rearrange("n (k a h) -> n k a h", k=4, a=2)[:, :, a, :, None]
                                nc.vector.tensor_tensor(st, st, el.broadcast_to([64, 4, 8, HP]), ALU.mult).then_inc(state_ready, 1)
                            v.wait_ge(st_done, 2 * (c + 1) + blk + 1)
                            for a in range(2):
                                rows = slice(64 * a, 64 * a + 64)
                                v.wait_ge(state_ready, base + a + 1)
                                new = ps_turn[rows].rearrange("n (k a c) -> n k a c", k=4, a=2)[:, :, a]
                                nc.vector.tensor_tensor(state[rows, :, a, :], state[rows, :, a, :], new, ALU.add).then_inc(state_ready, 1)
                            if blk == 1:
                                if q == 2:
                                    v.wait_ge(state_ready, base + 4)
                                    kr = keep_rows[:, bass.ds(i + 1, 1)]
                                    st = state[:].rearrange("n k a c -> n (k a c)")
                                    nc.vector.tensor_scalar(st, st, kr, None, ALU.mult).then_inc(reset_ready, 1)
                                wait(v, y_ready, c + 1)
                                nc.vector.tensor_tensor(tmp[:], ps_off[:], sums[:, sl, 0, :, None].broadcast_to([P, H, HP]),
                                                        ALU.mult).then_inc(off_read, 1)
                    if inside(i, 4, q, CHUNKS) and s == 2:
                        v.wait_ge(diag_done, n)
                        v.wait_ge(y_ready, c + 1)
                        assemble(q % 2, 0)
                    if inside(i, 4, q - 1, CHUNKS):
                        if s == 0:
                            slot, t0 = in_group(q - 1)
                            v.wait_ge(final, 8 * (2 * i + (q - 1) // 2) + 8)
                            v.wait_ge(yt_done, c)
                            wait(v, yg_lo_ready, c - 1)
                            wait(v, yg_hi_ready, c - 1)
                            nc.vector.tensor_tensor(yg[:], ps_diag[:, 1].rearrange("p (k t) -> p k t", k=4),
                                                    gate[:, slot, :, t0:t0 + P], ALU.mult).then_inc(gated, 1)
                    if (m + 13) % 8 == 0 and inside(i, 2, (m + 13) // 8, 16):
                        g = 2 * i + (m + 13) // 8
                        k = ((m + 13) // 8) % 2
                        v.wait_ge(x_hi_ready, g + 1)
                        nc.vector.tensor_tensor(x_lo[:, k], x_raw[:], x_hi[:, k].bitcast(F32), ALU.subtract).then_inc(x_lo_ready, 1)

            def assemble(slot, half):
                pairs = ps_diag[:, half].rearrange("r (k a b p) -> r k a b p", k=16, a=2, b=2)
                yh = y[:, slot].rearrange("t (f k a) p -> t f k a p", f=2, a=2)[:, half]
                for blk in range(2):
                    for a in range(2):
                        to = yh[Q * blk:Q * blk + Q, :, a, :]
                        nc.vector.tensor_tensor(to, to, pairs[Q * a:Q * a + Q, :, a, blk, :], ALU.add).then_inc(assembled, 1)

            run(v, body)
            v.wait_ge(stat_done, CHUNKS)


HIDDEN, FT = 704, 6
NG = TOKENS // 512


def run_pairs(engine, body, last=NG // 2 - 1):
    body(0)
    with engine.Fori(1, last) as i:
        body(i)
    body(last)


class Normalizer:

    def __init__(self, nc, b, u):
        self.nc, self.u = nc, u
        self.var, self.scale, self.t = (b.sb(f"norm_{n}", [P, CHUNKS]) for n in ("var", "scale", "t"))
        self.chain = b.sem("norm_chain")

    def scales(self, v):
        nc = self.nc
        link = Chain(v, self.chain)
        link(nc.vector.tensor_scalar(self.var[:], self.u[:, :, D + 1], LN_EPS, None, ALU.add))
        inverse_deviation(nc, link, self.var[:], self.scale[:], self.t[:])

    def rows(self, out, c):
        one = lambda t: t.rearrange("p c d -> p (c d)")
        row = self.u[:, bass.ds(c, 1)]
        return self.nc.vector.tensor_scalar(out, one(row[:, :, 0:D]), one(row[:, :, D:D + 1]),
                                            self.scale[:, bass.ds(c, 1)], ALU.subtract, ALU.mult)


def ffn_phase(nc, ins, u):
    with ExitStack() as ctx:
        b = Buffers(nc, ctx, "ffn")
        ident, ones = b.sb("ident", [P, P]), b.sb("ones", [P, P])
        w_raw = b.sb("w_raw", [P, 3, KD * FT * P])
        w_q = b.sb("w_q", [P, 3, KD * FT * P], F32R)
        below = b.sb("below", [P, KD * FT * P])
        mags, limit, neg_limit = b.sb("mags", [P, 3]), b.sb("limit", [P, 3]), b.sb("neg_limit", [P, 3])
        norm = Normalizer(nc, b, u)
        xn = b.sb("xn", [P, 2, 4, D])
        x_hi, x_lo = b.sb("x_hi", [P, 2, KD, 512], F32R), b.sb("x_lo", [P, 2, KD, 512], F32R)
        sig, h = b.sb("sig", [P, 2, 512]), b.sb("h", [P, 2, 512])
        h_hi, h_lo = b.sb("h_hi", [P, FT, 512], F32R), b.sb("h_lo", [P, FT, 512], F32R)
        row = b.sb("row", [P, 2, ROW])
        bn, bn_copy = b.sb("bn", [P, 6]), b.sb("bn_copy", [P, 1])
        ps_gate, ps_up = b.ps("ps_gate", [P, 2, 512]), b.ps("ps_up", [P, 2, 512])
        ps_turn, ps_out = b.ps("ps_turn", [P, KD, 512]), b.ps("ps_out", [P, 2, 512])
        (const_in, w_in, mags_ready, mags_done, quantized, xn_ready, turned, x_hi_ready, x_lo_ready, up_done, sig_ready, h_ready,
         h_hi_ready, h_lo_ready, out_done, res_done, bn_done, stat_done) = (b.sem(n) for n in (
            "const_in w_in mags_ready mags_done quantized xn_ready turned x_hi_ready x_lo_ready up_done sig_ready h_ready "
            "h_hi_ready h_lo_ready out_done res_done bn_done stat_done").split())
        kept = [b.sem(f"kept{k}") for k in range(2)]
        w1, w2 = (w_q[:, k].rearrange("p (k c) -> p k c", k=KD) for k in range(2))
        w3 = w_q[:, 2].rearrange("p (f c) -> p f c", f=FT)
        ctx.callback(b.clear)
        block = ctx.enter_context(nc.Block())

        @block.sync
        def _(sp):
            for k, name in enumerate(("w1T", "w2T")):
                sp.dma_start(w_raw[:, k].rearrange("p (k c) -> p k c", k=KD),
                             ins[name].rearrange("(k p) c -> p k c", p=P)).then_inc(w_in, 16)
            sp.dma_start(w_raw[:, 2].rearrange("p (f c) -> p f c", f=FT),
                         ins["w3T"].rearrange("(f p) c -> p f c", p=P)).then_inc(w_in, 16)
            sp.dma_start(ident[:], ins["identity"]).then_inc(const_in, 16)

            def body(i):
                for k in range(2):
                    for c in range(4):
                        ci = 8 * i + 4 * k + c
                        sp.wait_ge(stat_done, ci + 1)
                        sp.dma_start(u[:, bass.ds(ci, 1), :], row[:, c % 2, None, :]).then_inc(kept[c % 2], 16)

            run_pairs(sp, body)
            for k in range(2):
                sp.wait_ge(kept[k], 16 * CHUNKS // 2)

        @block.tensor
        def _(pe):
            pe.wait_ge(mags_ready, 4)
            nc.tensor.matmul(ps_out[:, 0, 0:3], ones[:], mags[:], start=True, stop=True).then_inc(mags_done, 1)
            pe.wait_ge(const_in, 16)

            def turn(g, slot):
                pe.wait_ge(xn_ready, 4 * g + 4)
                wait(pe, x_lo_ready, g)
                for c in range(4):
                    for k in range(KD):
                        m = nc.tensor.transpose(ps_turn[:, k, c * P:(c + 1) * P], xn[:, slot, c, k * P:(k + 1) * P], ident[:])
                m.then_inc(turned, 1)

            def body(i):
                for k in range(2):
                    g = 2 * i + k
                    pe.wait_ge(x_lo_ready, g + 1)
                    for f in range(FT):
                        wait(pe, h_ready, FT * g + f - 1)
                        cols = slice(f * P, (f + 1) * P)
                        for w, out in ((w1, ps_gate), (w2, ps_up)):
                            for d in range(KD):
                                nc.tensor.matmul(out[:, f % 2], w[:, d, cols], x_hi[:, k, d], start=(d == 0), stop=False)
                                m = nc.tensor.matmul(out[:, f % 2], w[:, d, cols], x_lo[:, k, d], start=False, stop=(d == KD - 1))
                        m.then_inc(up_done, 1)
                    if inside(i, 2, k + 1, NG):
                        turn(g + 1, (k + 1) % 2)
                    for c in range(4):
                        if c == 0:
                            pe.wait_ge(h_lo_ready, FT * (g + 1))
                        wait(pe, res_done, 4 * g + c - 1)
                        toks = slice(c * P, (c + 1) * P)
                        for f in range(FT):
                            nc.tensor.matmul(ps_out[:, c % 2, 0:D], h_hi[:, f, toks], w3[:, f], start=(f == 0), stop=False)
                            m = nc.tensor.matmul(ps_out[:, c % 2, 0:D], h_lo[:, f, toks], w3[:, f], start=False, stop=(f == FT - 1))
                        m.then_inc(out_done, 1)

            turn(0, 0)
            pe.wait_ge(quantized, 6)
            run_pairs(pe, body)

        @block.scalar
        def _(act):
            def high(g, slot):
                act.wait_ge(turned, g + 1)
                nc.scalar.activation(x_hi[:, slot], ps_turn[:], ACT.Copy).then_inc(x_hi_ready, 1)

            def h_high(g, f):
                act.wait_ge(h_ready, FT * g + f + 1)
                if f == 0:
                    wait(act, out_done, 4 * g)
                nc.scalar.activation(h_hi[:, f], h[:, f % 2], ACT.Copy).then_inc(h_hi_ready, 1)

            def body(i):
                for k in range(2):
                    g = 2 * i + k
                    for f in range(FT):
                        act.wait_ge(up_done, FT * g + f + 1)
                        wait(act, h_ready, FT * g + f - 1)
                        nc.scalar.activation(sig[:, f % 2], ps_gate[:, f % 2], ACT.Sigmoid).then_inc(sig_ready, 1)
                        if f:
                            h_high(g, f - 1)
                    h_high(g, FT - 1)
                    if inside(i, 2, k + 1, NG):
                        high(g + 1, (k + 1) % 2)

            high(0, 0)
            run_pairs(act, body)

        @block.vector
        def _(v):
            nc.vector.memset(ones[:], 1.0).then_inc(mags_ready, 1)
            v.wait_ge(w_in, 48)
            for k in range(3):
                nc.vector.tensor_reduce(mags[:, k:k + 1], w_raw[:, k], AX.X, ALU.add, apply_absolute_value=True).then_inc(mags_ready, 1)
            norm.scales(v)

            def rows(g, slot):
                for c in range(4):
                    if c == 0:
                        wait(v, turned, g - 1)
                    norm.rows(xn[:, slot, c], 4 * g + c).then_inc(xn_ready, 1)

            def low(g, slot):
                v.wait_ge(x_hi_ready, g + 1)
                nc.vector.tensor_tensor(x_lo[:, slot], ps_turn[:], x_hi[:, slot].bitcast(F32), ALU.subtract).then_inc(x_lo_ready, 1)

            rows(0, 0)
            v.wait_ge(mags_done, 1)
            for t, sign in ((limit, 0.5), (neg_limit, -0.5)):
                nc.vector.tensor_scalar(t[:], ps_out[:, 0, 0:3], sign / (HIDDEN * D), sign * 1e-8, ALU.mult, ALU.add).then_inc(mags_ready, 1)
            v.wait_ge(mags_ready, 6)
            for k in range(3):
                wait(v, quantized, 2 * k)
                nc.vector.tensor_scalar(below[:], w_raw[:, k], neg_limit[:, k:k + 1], None, ALU.is_lt).then_inc(quantized, 1)
                v.wait_ge(quantized, 2 * k + 1)
                nc.vector.scalar_tensor_tensor(w_q[:, k], w_raw[:, k], limit[:, k:k + 1], below[:],
                                               ALU.is_gt, ALU.subtract).then_inc(quantized, 1)
            low(0, 0)

            def h_low(g, f):
                v.wait_ge(h_hi_ready, FT * g + f + 1)
                nc.vector.tensor_tensor(h_lo[:, f], h[:, f % 2], h_hi[:, f].bitcast(F32), ALU.subtract).then_inc(h_lo_ready, 1)

            def body(i):
                for k in range(2):
                    g = 2 * i + k
                    if inside(i, 2, k + 1, NG):
                        rows(g + 1, (k + 1) % 2)
                    for f in range(FT):
                        v.wait_ge(sig_ready, FT * g + f + 1)
                        wait(v, h_lo_ready, FT * g + f - 1)
                        nc.vector.tensor_tensor(h[:, f % 2], ps_up[:, f % 2], sig[:, f % 2], ALU.mult).then_inc(h_ready, 1)
                        if f:
                            h_low(g, f - 1)
                    h_low(g, FT - 1)
                    if inside(i, 2, k + 1, NG):
                        low(g + 1, (k + 1) % 2)
                    for c in range(4):
                        ci = 8 * i + 4 * k + c
                        v.wait_ge(out_done, ci + 1)
                        wait(v, kept[c % 2], 16 * (4 * i + 2 * k + c // 2))
                        nc.vector.tensor_tensor(row[:, c % 2, 0:D], ps_out[:, c % 2, 0:D], xn[:, k, c], ALU.add).then_inc(res_done, 1)
                        v.wait_ge(res_done, ci + 1)
                        nc.vector.bn_stats(bn[:], row[:, c % 2, 0:D]).then_inc(bn_done, 1)
                        v.wait_ge(bn_done, ci + 1)
                        nc.vector.tensor_copy(bn_copy[:], bn[:, 0:1])
                        nc.vector.bn_aggr(row[:, c % 2, D:ROW], bn[:]).then_inc(stat_done, 1)

            run_pairs(v, body)


NH, HD, NM = 16, 16, 4
VW = HD + 1
ATT_EPS = 1e-6


def attention_phase(nc, ins, u):
    with ExitStack() as ctx:
        b = Buffers(nc, ctx, "att")
        ctx.callback(b.clear)
        kept = {
            "phi_q": b.sb("phi_q", [P, NG, 2, 512]),
            "local": b.sb("local", [P, CHUNKS, D]),
            "q_sums": b.sb("q_sums", [P, NG, 2]),
            "w_hi": b.sb("w_hi", [P, KD, D], F32R), "w_lo": b.sb("w_lo", [P, KD, D], F32R),
            "mem": b.sb("mem", [P, 2, NM + 1, 8 * VW]),
            "coef": b.sb("coef", [P, NG // 2, NM + 1, NH]),
            "head_gate": b.sb("head_gate", [P, NH]),
            "local_gate": b.sb("local_gate", [P, NH]),
        }
        norm = Normalizer(nc, b, u)
        causal_pass(nc, ins, u, norm, kept)
        memory_weights(nc, ins, kept)
        memory_pass(nc, ins, u, norm, kept)


def causal_pass(nc, ins, u, norm, kept):
    with ExitStack() as ctx:
        b = Buffers(nc, ctx, "causal")
        ident = b.sb("ident", [P, P])
        mask = b.sb("mask", [P, Q])
        head_blocks = b.sb("head_blocks", [P, 2, 8 * VW])
        parity = b.sb("parity", [P, 2])
        keep_rows = b.sb("keep_rows", [P, NG // 2 + 1])
        w_raw = b.sb("w_raw", [P, 4, KD, D])
        w_hi, w_lo = b.sb("w_hi", [P, KD, 3 * D], F32R), b.sb("w_lo", [P, KD, 3 * D], F32R)
        xn = b.sb("xn", [P, 4, D])
        x_hi, x_lo = b.sb("x_hi", [P, 2, KD, 512], F32R), b.sb("x_lo", [P, 2, KD, 512], F32R)
        e, r = (w_raw[:, 2 * k:2 * k + 2].rearrange("p t k c -> p t (k c)") for k in range(2))
        pq, pk = b.sb("pq", [P, 2, 2, 512]), b.sb("pk", [P, 2, 2, 512])
        pq_half = b.sb("pq_half", [P, 2, 2, 2, 512])
        ek, rk = b.sb("ek", [P, D]), b.sb("rk", [P, D])
        k_tok = b.sb("k_tok", [P, 2, D])
        v_blocks = b.sb("v_blocks", [P, 2, NH, 2, VW])
        sc = b.sb("sc", [P, 2, 4, 2, 2, Q])
        acc = b.sb("acc", [P, 2, 2 * 8 * VW])
        state = b.sb("state", [P, 2, 2, 2, 4, 2, VW])
        den, zero = b.sb("den", [P, NH]), b.sb("zero", [P, 2])
        red = b.sb("red", [P, 2])
        ps_turn, ps_proj = b.ps("ps_turn", [P, 512]), b.ps("ps_proj", [P, 512])
        ps_sc = b.ps("ps_sc", [P, 4, 512])
        ps_num, ps_state = b.ps("ps_num", [P, 512]), b.ps("ps_state", [P, 512])
        (const_in, w_in, w_ready, w_lo_ready, zeroed, xn_ready, turned, x_hi_ready, x_lo_ready, kv_done, kv_read, k_ready, qk_done,
         qk_read, phi_ready, half_ready, sc_done, sc_ready, num_done, num_read, den_ready, st_done, acc_ready, start_ready, mid_ready, reset_ready,
         red_ready, sum_kept) = (b.sem(n) for n in (
            "const_in w_in w_ready w_lo_ready zeroed xn_ready turned x_hi_ready x_lo_ready kv_done kv_read k_ready qk_done "
            "qk_read phi_ready half_ready sc_done sc_ready num_done num_read den_ready st_done acc_ready start_ready mid_ready reset_ready "
            "red_ready sum_kept").split())
        phi_kept = [b.sem(f"phi_kept{k}") for k in range(2)]
        ctx.callback(b.clear)
        block = ctx.enter_context(nc.Block())

        def run(engine, body):
            body(-1)
            body(0)
            with engine.Fori(1, NG // 2 - 1) as i:
                body(i)
            body(NG // 2 - 1)

        def next_group(i, j):
            k = j // 4 + 1
            return (2 * i + k, k % 2) if inside(i, 2, k, NG) else (None, None)

        @block.sync
        def _(sp):
            for k, name in enumerate(("wqT", "wkT", "wvT", "woT")):
                sp.dma_start(w_raw[:, k], ins[name].rearrange("(k p) c -> p k c", p=P)).then_inc(w_in, 16)
            for t, name in ((ident, "identity"), (mask, "upper_ones"), (head_blocks, "head_blocks"), (parity, "parity"),
                            (keep_rows, "keep_batches")):
                sp.dma_start(t[:], ins[name]).then_inc(const_in, 16)

            def body(i):
                for j in (1, 5):
                    g, slot = next_group(i, j)
                    if g is not None:
                        sp.wait_ge(phi_ready, 4 * g + 2)
                        sp.dma_start(kept["phi_q"][:, bass.ds(g, 1)], pq[:, slot:slot + 1]).then_inc(phi_kept[slot], 16)

            run(sp, body)
            for k in range(2):
                sp.wait_ge(phi_kept[k], 16 * NG // 2)

        @block.tensor
        def _(pe):
            pe.wait_ge(const_in, 80)
            pe.wait_ge(w_lo_ready, 4)

            def project(out, w0, w1, g_slot, toks=None):
                for k in range(KD):
                    w = (w_hi[:, k, w0:w1], w_lo[:, k, w0:w1])
                    if toks is None:
                        m = product3(nc, out, *w, x_hi[:, g_slot, k], x_lo[:, g_slot, k], k == 0, k == KD - 1)
                    else:
                        m = product3(nc, out, x_hi[:, g_slot, k, toks], x_lo[:, g_slot, k, toks], *w, k == 0, k == KD - 1)
                return m

            def half_of_next(i, j, h):
                g, slot = next_group(i, j)
                ci, c = 8 * i + j, j % 4
                if g is None or c == 3:
                    return
                if c == 0:
                    if h == 0:
                        pe.wait_ge(xn_ready, 4 * g + 4)
                        wait(pe, acc_ready, 2 * (ci + 1))
                    wait(pe, x_lo_ready, 2 * g + h)
                    for t in range(4):
                        m = nc.tensor.transpose(ps_turn[:, t * P:(t + 1) * P], xn[:, t, h * P:(h + 1) * P], ident[:])
                    m.then_inc(turned, 1)
                else:
                    if inside(i, 8, j + 1, CHUNKS):
                        wait(pe, kv_read, ci + 2)
                    pe.wait_ge(x_lo_ready, 2 * g + 2)
                    wait(pe, qk_read, 4 * g + 2 * (c - 1) + h)
                    w0 = (c - 1) * D + h * P
                    project(ps_proj[:], w0, w0 + P, slot).then_inc(qk_done, 1)

            def body(i):
                for j in range(8):
                    ci, c = 8 * i + j, j % 4
                    nxt = ((j + 1) // 4) % 2
                    toks = slice(((j + 1) % 4) * P, ((j + 1) % 4 + 1) * P)
                    if inside(i, 8, j + 1, CHUNKS):
                        wait(pe, kv_read, ci + 1)
                        begun = 0 if next_group(i, j)[0] is None else (0, 0, 2, 4)[c]
                        wait(pe, qk_read, 4 * (2 * i + j // 4) + 4 + begun)
                        project(ps_proj[:], D, 3 * D, nxt, toks).then_inc(kv_done, 1)
                    g, slot = next_group(i, j)
                    if inside(i, 8, j + 1, CHUNKS):
                        gn = 2 * i + (j + 1) // 4
                        pe.wait_ge(half_ready, 4 * gn + 4)
                        pe.wait_ge(phi_ready, 4 * gn + 4)
                        wait(pe, sc_ready, 4 * (ci + 1))
                        for t in range(2):
                            for blk in range(2):
                                for rt in range(4):
                                    rows = slice(32 * rt, 32 * rt + 32)
                                    ts = slice(toks.start + Q * blk, toks.start + Q * blk + Q)
                                    m = nc.tensor.matmul(ps_sc[Q * blk:Q * blk + Q, rt, t * P:(t + 1) * P], pk[rows, nxt, t, ts],
                                                         pq_half[rows, nxt, t, :, ts], start=True, stop=True,
                                                         tile_position=(32 * rt, Q * blk))
                        m.then_inc(sc_done, 1)
                    half_of_next(i, j, 0)
                    if inside(i, 8, j, CHUNKS):
                        now = (j // 4) % 2
                        wait(pe, num_read, 4 * ci)
                        wait(pe, start_ready, ci + 1)
                        wait(pe, mid_ready, ci + 1)
                        num = ps_num[:, 0:NH * VW].rearrange("q (k b e) -> q k b e", b=2, e=VW)
                        for t in range(2):
                            for blk in range(2):
                                for par in range(2):
                                    ts = slice(c * P + Q * blk, c * P + Q * blk + Q)
                                    nc.tensor.matmul(num[Q * par:Q * par + Q, 4 * t:4 * t + 4, blk], pq[:, now, t, ts],
                                                     state[:, j % 2, blk, t, :, par], start=(t == 0 and blk == 0), stop=False,
                                                     skip_group_check=True)
                        pe.wait_ge(sc_ready, 4 * (ci + 1))
                        for h in range(NH):
                            t, rt, par = h // 8, (h % 8) // 2, h % 2
                            m = nc.tensor.matmul(num[Q * par:Q * par + Q, h // 2].rearrange("q b e -> q (b e)"), sc[:, j % 2, rt, t, par],
                                                 v_blocks[:, j % 2, h].rearrange("j b e -> j (b e)"),
                                                 start=False, stop=(h >= NH - 2), skip_group_check=True)
                        m.then_inc(num_done, 1)
                    half_of_next(i, j, 1)
                    if inside(i, 8, j + 1, CHUNKS):
                        pe.wait_ge(k_ready, ci + 2)
                        pe.wait_ge(kv_read, ci + 2)
                        wait(pe, acc_ready, 2 * (ci + 1))
                        if g is not None and c == 0:
                            pe.wait_ge(x_lo_ready, 2 * g + 2)
                        for blk, out in enumerate((ps_state, ps_turn)):
                            rows = slice(Q * blk, Q * blk + Q)
                            for t in range(2):
                                m = nc.tensor.matmul(out[:, t * 8 * VW:(t + 1) * 8 * VW], k_tok[rows, (j + 1) % 2, t * P:(t + 1) * P],
                                                     v_blocks[rows, (j + 1) % 2, 8 * t:8 * t + 8, blk], start=True, stop=True)
                            m.then_inc(st_done, 1)

            run(pe, body)

        @block.scalar
        def _(act):
            act.wait_ge(w_in, 64)
            for k in range(3):
                nc.scalar.activation(w_hi[:, :, k * D:(k + 1) * D], w_raw[:, k], ACT.Copy).then_inc(w_ready, 1)
            nc.scalar.activation(kept["w_hi"][:], w_raw[:, 3], ACT.Copy).then_inc(w_ready, 1)
            act.wait_ge(zeroed, 5)

            def body(i):
                for j in range(8):
                    ci, c = 8 * i + j, j % 4
                    if inside(i, 8, j + 1, CHUNKS):
                        act.wait_ge(kv_done, ci + 2)
                        wait(act, k_ready, ci + 1)
                        wait(act, num_done, ci)
                        nc.scalar.activation(ek[:], ps_proj[:, 0:D], ACT.Exp)
                        nc.scalar.activation(rk[:], ps_proj[:, 0:D], ACT.Relu)
                        for blk in range(2):
                            rows = slice(Q * blk, Q * blk + Q)
                            m = nc.scalar.activation(v_blocks[rows, (j + 1) % 2, :, blk, 0:HD],
                                                     ps_proj[rows, D:2 * D].rearrange("p (h e) -> p h e", e=HD), ACT.Copy)
                        m.then_inc(kv_read, 1)
                    g, slot = next_group(i, j)
                    if g is not None:
                        if c == 0:
                            for k in range(KD):
                                act.wait_ge(turned, 2 * g + k + 1)
                                nc.scalar.activation(x_hi[:, slot, k], ps_turn[:], ACT.Copy).then_inc(x_hi_ready, 1)
                        if c in (1, 2):
                            for t in range(2):
                                n = 4 * g + 2 * (c - 1) + t
                                act.wait_ge(qk_done, n + 1)
                                wait(act, phi_ready, n - 1)
                                nc.scalar.activation(e[:, t], ps_proj[:], ACT.Exp)
                                nc.scalar.activation(r[:, t], ps_proj[:], ACT.Relu).then_inc(qk_read, 1)

            run(act, body)

        @block.gpsimd
        def _(pool):
            for k in range(4):
                pool.wait_ge(w_ready, k + 1)
                hi, lo = ((w_hi[:, :, k * D:(k + 1) * D], w_lo[:, :, k * D:(k + 1) * D]) if k < 3 else (kept["w_hi"][:], kept["w_lo"][:]))
                nc.gpsimd.tensor_tensor(lo, w_raw[:, k], hi.bitcast(F32), ALU.subtract).then_inc(w_lo_ready, 1)

            masks = head_blocks[:].rearrange("p t c -> p (t c)")
            view = lambda slot, blk: state[:, slot, blk].rearrange("p t k a e -> p (t k a e)")
            pool.wait_ge(const_in, 80)

            def body(i):
                for j in range(8):
                    ci = 8 * i + j
                    g, slot = next_group(i, j)
                    if g is not None and j % 4 == 1:
                        wait(pool, sc_done, 4 * (g - 1))
                        for t in range(2):
                            pool.wait_ge(phi_ready, 4 * g + t + 1)
                            for par in range(2):
                                nc.gpsimd.tensor_tensor(pq_half[:, slot, t, par], pq[:, slot, t],
                                                        parity[:, par:par + 1].broadcast_to([P, 512]), ALU.mult).then_inc(half_ready, 1)
                    if inside(i, 8, j + 1, CHUNKS):
                        pool.wait_ge(acc_ready, 2 * (ci + 1) + 1)
                        wait(pool, num_done, ci)
                        nc.gpsimd.tensor_tensor(view((j + 1) % 2, 1), acc[:, 0], masks, ALU.mult).then_inc(mid_ready, 1)
                        pool.wait_ge(acc_ready, 2 * (ci + 2))
                        if j == 6:
                            pool.wait_ge(reset_ready, i + 1)
                        wait(pool, num_done, ci + 1)
                        nc.gpsimd.tensor_tensor(view(j % 2, 0), acc[:, 1], masks, ALU.mult).then_inc(start_ready, 1)

            run(pool, body)

        @block.vector
        def _(v):
            nc.vector.memset(v_blocks[:], 0.0).then_inc(zeroed, 1)
            v.wait_ge(zeroed, 1)
            for blk in range(2):
                nc.vector.memset(v_blocks[Q * blk:Q * blk + Q, :, :, blk, HD:VW], 1.0).then_inc(zeroed, 1)
            nc.vector.memset(acc[:], 0.0).then_inc(zeroed, 1)
            nc.vector.memset(zero[:], 0.0).then_inc(zeroed, 1)
            nc.vector.memset(state[:], 0.0).then_inc(start_ready, 1)
            v.wait_ge(zeroed, 5)
            v.wait_ge(const_in, 80)
            norm.scales(v)

            def half_of_next(i, j, h):
                g, slot = next_group(i, j)
                c = j % 4
                if g is None:
                    return
                if c == 0:
                    v.wait_ge(x_hi_ready, 2 * g + h + 1)
                    nc.vector.tensor_tensor(x_lo[:, slot, h], ps_turn[:], x_hi[:, slot, h].bitcast(F32), ALU.subtract)\
                        .then_inc(x_lo_ready, 1)
                if c in (1, 2):
                    if c == 1 and h == 0:
                        wait(v, num_done, 4 * (g - 1))
                        wait(v, half_ready, 4 * (g - 1))
                        wait(v, phi_kept[slot], 16 * (i + (j // 4 + 1) // 2))
                        wait(v, red_ready, g - 1)
                    v.wait_ge(qk_read, 4 * g + 2 * (c - 1) + h + 1)
                    nc.vector.scalar_tensor_tensor((pq, pk)[c - 1][:, slot, h], e[:, h], 1.0, r[:, h], ALU.min, ALU.add).then_inc(phi_ready, 1)
                if c == 3 and h == 1:
                    v.wait_ge(phi_ready, 4 * g + 2)
                    wait(v, sum_kept, g)
                    nc.vector.tensor_reduce(red[:], pq[:, slot], AX.X, ALU.add).then_inc(red_ready, 1)
                    v.wait_ge(red_ready, g + 1)
                    nc.vector.tensor_tensor(kept["q_sums"][:, bass.ds(g, 1)].rearrange("p g t -> p (g t)"), red[:], zero[:],
                                            ALU.add).then_inc(sum_kept, 1)

            def body(i):
                for j in range(8):
                    ci, c = 8 * i + j, j % 4
                    if inside(i, 8, j + 1, CHUNKS):
                        v.wait_ge(kv_read, ci + 2)
                        wait(v, st_done, 2 * ci)
                        nc.vector.scalar_tensor_tensor(k_tok[:, (j + 1) % 2], ek[:], 1.0, rk[:], ALU.min, ALU.add).then_inc(k_ready, 1)
                    if next_group(i, j)[0] is not None and c == 0:
                        g = next_group(i, j)[0]
                        wait(v, turned, 2 * g)
                        for t in range(4):
                            norm.rows(xn[:, t], 4 * g + t).then_inc(xn_ready, 1)
                    if inside(i, 8, j + 1, CHUNKS):
                        v.wait_ge(sc_done, ci + 2)
                        wait(v, num_done, ci)
                        for rt in range(4):
                            nc.vector.tensor_tensor(sc[:, (j + 1) % 2, rt].rearrange("p t a i -> p (t a) i"),
                                                    ps_sc[:, rt, 0:4 * Q].rearrange("p (c i) -> p c i", i=Q),
                                                    mask[:, None, :].broadcast_to([P, 4, Q]), ALU.mult).then_inc(sc_ready, 1)
                    half_of_next(i, j, 0)
                    if inside(i, 8, j, CHUNKS):
                        num = ps_num[:, 0:NH * VW].rearrange("q (k b e) -> q k b e", b=2, e=VW)
                        v.wait_ge(num_done, ci + 1)
                        wait(v, num_read, 4 * ci)
                        dn = den[:].rearrange("q (k b) -> q k b", b=2)
                        nc.vector.tensor_scalar(dn, num[:, :, :, HD], ATT_EPS, None, ALU.max).then_inc(den_ready, 1)
                        v.wait_ge(den_ready, 2 * ci + 1)
                        nc.vector.reciprocal(den[:], den[:]).then_inc(den_ready, 1)
                        v.wait_ge(den_ready, 2 * ci + 2)
                        for blk in range(2):
                            out = kept["local"][Q * blk:Q * blk + Q, bass.ds(ci, 1)].rearrange("p c (k a e) -> p (c k) a e", a=2, e=HD)
                            for par in range(2):
                                rows = slice(Q * par, Q * par + Q)
                                nc.vector.tensor_tensor(out[:, :, par], num[rows, :, blk, 0:HD],
                                                        dn[rows, :, blk, None].broadcast_to([Q, 8, HD]), ALU.mult).then_inc(num_read, 1)
                    half_of_next(i, j, 1)
                    if inside(i, 8, j + 1, CHUNKS):
                        v.wait_ge(st_done, 2 * (ci + 1) + 1)
                        wait(v, acc_ready, 2 * (ci + 1))
                        wait(v, mid_ready, ci + 1)
                        wait(v, start_ready, ci + 2)
                        if j == 7:
                            wait(v, reset_ready, i + 1)
                        W2 = 2 * 8 * VW
                        nc.vector.tensor_tensor(acc[:, 0], acc[:, 1], ps_state[:, 0:W2], ALU.add).then_inc(acc_ready, 1)
                        v.wait_ge(st_done, 2 * (ci + 2))
                        v.wait_ge(acc_ready, 2 * (ci + 1) + 1)
                        nc.vector.tensor_tensor(acc[:, 1], acc[:, 0], ps_turn[:, 0:W2], ALU.add).then_inc(acc_ready, 1)
                        if j == 6:
                            v.wait_ge(acc_ready, 2 * (ci + 2))
                            nc.vector.tensor_scalar(acc[:, 1], acc[:, 1], keep_rows[:, bass.ds(i + 1, 1)], None, ALU.mult).then_inc(reset_ready, 1)

            run(v, body)
            v.wait_ge(num_read, 4 * CHUNKS)
            v.wait_ge(sum_kept, NG)


def memory_weights(nc, ins, kept):
    with ExitStack() as ctx:
        b = Buffers(nc, ctx, "memw")
        mem, coef = kept["mem"], kept["coef"]
        ones = b.sb("ones", [P, P])
        gate_raw = b.sb("gate_raw", [P, NH])
        mean = b.sb("mean", [P, BATCHES, 2])
        mean_rows = b.sb("mean_rows", [P, BATCHES, 2, P])
        norms = b.sb("norms", [P, NM])
        alive = b.sb("alive", [P, NM + 1])
        top, total = b.sb("top", [P, BATCHES * NH]), b.sb("total", [P, BATCHES * NH])
        rel = b.sb("rel", [P, NM, BATCHES * NH])
        ps_rel, ps_norms = b.ps("ps_rel", [P, BATCHES, 2, NM, 8]), b.ps("ps_norms", [P, 512])
        ld, step, pe_done, act_done = b.sem("ld"), b.sem("step"), b.sem("pe_done"), b.sem("act_done")
        ctx.callback(b.clear)
        block = ctx.enter_context(nc.Block())
        mem6 = mem[:].rearrange("p t m (h e) -> p t m h e", e=VW)

        @block.sync
        def _(sp):
            sp.dma_start(mem[:, :, 1:], ins["mem_blocks"]).then_inc(ld, 16)
            sp.dma_start(gate_raw[:], ins["gate_rows"]).then_inc(ld, 16)

        @block.tensor
        def _(pe):
            pe.wait_ge(step, STEPS_READY)
            nc.tensor.matmul(ps_norms[:, 0:NM], ones[:], norms[:], start=True, stop=True).then_inc(pe_done, 1)
            for s in range(BATCHES):
                for t in range(2):
                    m = nc.tensor.matmul(ps_rel[:, s, t].rearrange("p m h -> p (m h)"), mean_rows[:, s, t],
                                         mem6[:, t, 1:, :, HD],
                                         start=True, stop=True)
            m.then_inc(pe_done, 1)

        @block.scalar
        def _(act):
            act.wait_ge(ld, 32)
            nc.scalar.activation(kept["head_gate"][:], gate_raw[:], ACT.Sigmoid)
            nc.scalar.activation(kept["local_gate"][:], gate_raw[:], ACT.Sigmoid, scale=-1.0)
            act.wait_ge(step, EXP_READY)
            nc.scalar.activation(rel[:], rel[:], ACT.Exp).then_inc(act_done, 1)

        @block.vector
        def _(v):
            link = Chain(v, step)
            v.wait_ge(ld, 32)
            link(nc.vector.memset(ones[:], 1.0))
            link(nc.vector.tensor_tensor(mem[:, :, 0], mem[:, :, 1], mem[:, :, 2], ALU.add))
            link(nc.vector.tensor_tensor(mem[:, :, 0], mem[:, :, 0], mem[:, :, 3], ALU.add))
            link(nc.vector.tensor_tensor(mem[:, :, 0], mem[:, :, 0], mem[:, :, 4], ALU.add))
            for m in range(NM):
                link(nc.vector.tensor_reduce(norms[:, m:m + 1], mem6[:, :, m + 1, :, HD], AX.XY, ALU.add))
            gs = NG // BATCHES
            link(nc.vector.tensor_reduce(mean[:], kept["q_sums"][:].rearrange("p (s g) t -> p s t g", g=gs), AX.X, ALU.add))
            for s in range(BATCHES):
                for t in range(2):
                    link(nc.vector.tensor_scalar(mean_rows[:, s, t], ones[:], mean[:, s, t:t + 1], 1.0 / (TOKENS // BATCHES),
                                                 ALU.mult, ALU.mult))
            assert link.n == STEPS_READY
            v.wait_ge(pe_done, 2)
            link(nc.vector.tensor_scalar(alive[:, 1:], ps_norms[:, 0:NM], ATT_EPS, None, ALU.is_ge))
            link(nc.vector.tensor_reduce(alive[:, 0:1], ps_norms[:, 0:NM], AX.X, ALU.add))
            link(nc.vector.tensor_scalar(alive[:, 0:1], alive[:, 0:1], ATT_EPS, None, ALU.is_ge))
            for m in range(NM):
                link(nc.vector.tensor_copy(rel[:, m].rearrange("p (s t h) -> p s t h", s=BATCHES, t=2), ps_rel[:, :, :, m]))
            link(nc.vector.tensor_tensor(top[:], rel[:, 0], rel[:, 1], ALU.max))
            link(nc.vector.tensor_tensor(top[:], top[:], rel[:, 2], ALU.max))
            link(nc.vector.tensor_tensor(top[:], top[:], rel[:, 3], ALU.max))
            link(nc.vector.tensor_tensor(rel[:], rel[:], top[:, None, :].broadcast_to([P, NM, BATCHES * NH]), ALU.subtract))
            assert link.n == EXP_READY
            v.wait_ge(act_done, 1)
            link(nc.vector.tensor_tensor(total[:], rel[:, 0], rel[:, 1], ALU.add))
            link(nc.vector.tensor_tensor(total[:], total[:], rel[:, 2], ALU.add))
            link(nc.vector.tensor_tensor(total[:], total[:], rel[:, 3], ALU.add))
            link(nc.vector.reciprocal(total[:], total[:]))
            link(nc.vector.tensor_tensor(rel[:], rel[:], total[:, None, :].broadcast_to([P, NM, BATCHES * NH]), ALU.mult))
            link(nc.vector.memset(coef[:, :, 0], 1.0))
            link(nc.vector.tensor_scalar(coef[:, :, 0], coef[:, :, 0], alive[:, 0:1], None, ALU.mult))
            for it in range(NG // 2):
                s = it // (NG // 2 // BATCHES)
                for m in range(NM):
                    link(nc.vector.tensor_scalar(coef[:, it, m + 1], rel[:, m, s * NH:(s + 1) * NH], alive[:, m + 1:m + 2], None, ALU.mult))


STEPS_READY = 4 + NM + 1 + 2 * BATCHES
EXP_READY = STEPS_READY + 3 + NM + 4


def memory_pass(nc, ins, u, norm, kept):
    with ExitStack() as ctx:
        b = Buffers(nc, ctx, "mem")
        ident = b.sb("ident", [P, P])
        eg_w1, eg_b1 = b.sb("eg_w1", [P, KD, 64]), b.sb("eg_b1", [64, 1])
        eg_w2, eg_b2 = b.sb("eg_w2", [64, 1]), b.sb("eg_b2", [P, 1])
        pq = b.sb("pq", [P, 4, 2, P])
        den = b.sb("den", [P, 2, NM + 1, NH])
        prod = b.sb("prod", [P, 2, NM + 1, D])
        pair_sum, fine = b.sb("pair_sum", [P, 2, D]), b.sb("fine", [P, 2, D])
        local_part = b.sb("local_part", [P, 2, D])
        c_T = b.sb("c_T", [P, 2, P])
        hidden = b.sb("hidden", [64, P])
        choice = b.sb("choice", [P, 2])
        mix = b.sb("mix", [P, 2, D])
        o_hi, o_lo = b.sb("o_hi", [P, KD, P], F32R), b.sb("o_lo", [P, KD, P], F32R)
        xn = b.sb("xn", [P, D])
        row = b.sb("row", [P, 2, ROW])
        bn, bn_copy = b.sb("bn", [P, 6]), b.sb("bn_copy", [P, 1])
        ps_a, ps_b = b.ps("ps_a", [P, 2, 512]), b.ps("ps_b", [P, 2, 512])
        ps_coarse, ps_hidden = b.ps("ps_coarse", [P, 512]), b.ps("ps_hidden", [P, 512])
        ps_turn, ps_out = b.ps("ps_turn", [P, 512]), b.ps("ps_out", [P, 512])
        (const_in, mem_done, den_ready, rden_ready, coef_ready, prod_ready, pair_ready, fine_ready, diff_ready, ct_done, ct_ready,
         hidden_done, hidden_ready, choice_done, choice_ready, mix_step, ot_done, o_hi_ready, o_lo_ready, out_done, xn_ready, local_ready,
         res_done, bn_done, stat_done) = (b.sem(n) for n in (
            "const_in mem_done den_ready rden_ready coef_ready prod_ready pair_ready fine_ready diff_ready ct_done ct_ready "
            "hidden_done hidden_ready choice_done choice_ready mix_step ot_done o_hi_ready o_lo_ready out_done xn_ready local_ready "
            "res_done bn_done stat_done").split())
        pq_in = [b.sem(f"pq_in{k}") for k in range(4)]
        u_kept = [b.sem(f"u_kept{k}") for k in range(2)]
        ctx.callback(b.clear)
        block = ctx.enter_context(nc.Block())
        N8 = CHUNKS // 8

        def run(engine, body):
            body(0)
            with engine.Fori(1, N8 - 1) as i:
                body(i)
            body(N8 - 1)
            body(N8)

        def width(i):
            return 3 if isinstance(i, int) and i == N8 else 8

        @block.sync
        def _(sp):
            sp.dma_start(ident[:], ins["identity"]).then_inc(const_in, 16)
            sp.dma_start(eg_w1[:], ins["eg_w1T"].rearrange("(k p) c -> p k c", p=P)).then_inc(const_in, 16)
            for t, name in ((eg_b1, "eg_b1"), (eg_w2, "eg_w2T"), (eg_b2, "eg_b2_rows")):
                sp.dma_start(t[:], ins[name]).then_inc(const_in, 16)

            def load(i, j):
                wait(sp, mem_done, 8 * i + j - 3)
                group = kept["phi_q"][:, bass.ds(2 * i + j // 4, 1)]
                sp.dma_start(pq[:, j % 4, None], group[:, :, :, (j % 4) * P:(j % 4 + 1) * P]).then_inc(pq_in[j % 4], 16)

            load(0, 0)
            load(0, 1)

            def body(i):
                for j in range(width(i)):
                    c = 8 * i + j
                    if inside(i, 8, j + 2, CHUNKS):
                        load(i, j + 2)
                    if inside(i, 8, j - 3, CHUNKS):
                        wait(sp, stat_done, c - 2)
                        sp.dma_start(u[:, bass.ds(c - 3, 1), :], row[:, (j - 3) % 2, None, :]).then_inc(u_kept[(j - 3) % 2], 16)

            run(sp, body)
            for k in range(2):
                sp.wait_ge(u_kept[k], 16 * CHUNKS // 2)

        @block.tensor
        def _(pe):
            pe.wait_ge(const_in, 80)

            def body(i):
                for j in range(width(i)):
                    c = 8 * i + j
                    if inside(i, 8, j - 1, CHUNKS):
                        wait(pe, prod_ready, 4 * c)
                        wait(pe, ct_ready, c - 1)
                        for k in range(KD):
                            m = nc.tensor.transpose(ps_coarse[:, k * P:(k + 1) * P], prod[:, (j - 1) % 2, 0, k * P:(k + 1) * P], ident[:])
                        m.then_inc(ct_done, 1)
                    if inside(i, 8, j - 3, CHUNKS):
                        wait(pe, mix_step, 3 * (c - 2))
                        wait(pe, o_lo_ready, c - 3)
                        for k in range(KD):
                            m = nc.tensor.transpose(ps_turn[:, k * P:(k + 1) * P], mix[:, (j - 3) % 2, k * P:(k + 1) * P], ident[:])
                        m.then_inc(ot_done, 1)
                    if inside(i, 8, j, CHUNKS):
                        pe.wait_ge(pq_in[j % 4], 16 * (2 * i + j // 4 + 1))
                        wait(pe, prod_ready, 4 * c)
                        for t in range(2):
                            for out, m0, m1 in ((ps_a, 0, 3), (ps_b, 3, 5)):
                                m = nc.tensor.matmul(out[:, t, 0:(m1 - m0) * 8 * VW], pq[:, j % 4, t],
                                                     kept["mem"][:, t, m0:m1].rearrange("p m c -> p (m c)"), start=True, stop=True)
                        m.then_inc(mem_done, 1)
                    if inside(i, 8, j - 1, CHUNKS):
                        wait(pe, choice_ready, c - 1)
                        wait(pe, ct_ready, c)
                        for k in range(KD):
                            m = nc.tensor.matmul(ps_hidden[0:64, 0:P], eg_w1[:, k], c_T[:, k], start=(k == 0), stop=(k == KD - 1))
                        m.then_inc(hidden_done, 1)
                    if inside(i, 8, j - 3, CHUNKS):
                        wait(pe, res_done, c - 3)
                        wait(pe, o_lo_ready, c - 2)
                        for k in range(KD):
                            m = product3(nc, ps_out[:, 0:D], o_hi[:, k], o_lo[:, k], kept["w_hi"][:, k], kept["w_lo"][:, k],
                                         k == 0, k == KD - 1)
                        m.then_inc(out_done, 1)
                    if inside(i, 8, j - 1, CHUNKS):
                        wait(pe, hidden_ready, c)
                        nc.tensor.matmul(ps_hidden[:, 256:257], hidden[:], eg_w2[:], start=True, stop=True).then_inc(choice_done, 1)

            run(pe, body)

        @block.scalar
        def _(act):
            act.wait_ge(const_in, 80)

            def body(i):
                for j in range(width(i)):
                    c = 8 * i + j
                    if inside(i, 8, j - 1, CHUNKS):
                        wait(act, ct_done, c)
                        wait(act, hidden_done, c - 1)
                        nc.scalar.activation(c_T[:].rearrange("p k t -> p (k t)"), ps_coarse[:, 0:D], ACT.Copy).then_inc(ct_ready, 1)
                    if inside(i, 8, j - 3, CHUNKS):
                        wait(act, ot_done, c - 2)
                        wait(act, out_done, c - 3)
                        nc.scalar.activation(o_hi[:].rearrange("p k t -> p (k t)"), ps_turn[:, 0:D], ACT.Copy).then_inc(o_hi_ready, 1)
                    if inside(i, 8, j - 1, CHUNKS):
                        wait(act, hidden_done, c)
                        wait(act, choice_done, c - 1)
                        nc.scalar.activation(hidden[:], ps_hidden[0:64, 0:P], ACT.Relu, bias=eg_b1[:]).then_inc(hidden_ready, 1)
                        wait(act, choice_done, c)
                        wait(act, mix_step, 3 * (c - 2))
                        nc.scalar.activation(choice[:, (j - 1) % 2:(j - 1) % 2 + 1], ps_hidden[:, 256:257], ACT.Sigmoid,
                                             bias=eg_b2[:]).then_inc(choice_ready, 1)

            run(act, body)

        @block.gpsimd
        def _(pool):
            def body(i):
                for j in range(width(i)):
                    c = 8 * i + j
                    if inside(i, 8, j, CHUNKS):
                        s = j % 2
                        pool.wait_ge(prod_ready, 4 * (c + 1))
                        wait(pool, mix_step, 3 * (c - 1))
                        nc.gpsimd.tensor_tensor(pair_sum[:], prod[:, s, 1:3], prod[:, s, 3:5], ALU.add).then_inc(pair_ready, 1)
                        pool.wait_ge(pair_ready, c + 1)
                        nc.gpsimd.tensor_tensor(fine[:, s], pair_sum[:, 0], pair_sum[:, 1], ALU.add).then_inc(fine_ready, 1)
                        pool.wait_ge(fine_ready, c + 1)
                        nc.gpsimd.tensor_tensor(fine[:, s], fine[:, s], prod[:, s, 0], ALU.subtract).then_inc(diff_ready, 1)
                        nc.gpsimd.tensor_tensor(local_part[:, s].rearrange("p (h e) -> p h e", e=HD),
                                                kept["local"][:, bass.ds(c, 1)].rearrange("p c (h e) -> p (c h) e", e=HD),
                                                kept["local_gate"][:, :, None].broadcast_to([P, NH, HD]), ALU.mult).then_inc(local_ready, 1)

            run(pool, body)

        @block.vector
        def _(v):
            def body(i):
                for j in range(width(i)):
                    c = 8 * i + j
                    if inside(i, 8, j - 3, CHUNKS):
                        wait(v, o_hi_ready, c - 2)
                        wait(v, out_done, c - 3)
                        nc.vector.tensor_tensor(o_lo[:].rearrange("p k t -> p (k t)"), ps_turn[:, 0:D],
                                                o_hi[:].bitcast(F32).rearrange("p k t -> p (k t)"), ALU.subtract).then_inc(o_lo_ready, 1)
                    if inside(i, 8, j - 2, CHUNKS):
                        s = j % 2
                        wait(v, diff_ready, c - 1)
                        wait(v, choice_ready, c - 1)
                        wait(v, ot_done, c - 3)
                        nc.vector.scalar_tensor_tensor(mix[:, s], fine[:, s], choice[:, s:s + 1], prod[:, s, 0],
                                                       ALU.mult, ALU.add).then_inc(mix_step, 1)
                        v.wait_ge(mix_step, 3 * (c - 2) + 1)
                        mh = mix[:, s].rearrange("p (h e) -> p h e", e=HD)
                        nc.vector.tensor_tensor(mh, mh, kept["head_gate"][:, :, None].broadcast_to([P, NH, HD]), ALU.mult).then_inc(mix_step, 1)
                        v.wait_ge(mix_step, 3 * (c - 2) + 2)
                        wait(v, local_ready, c - 1)
                        nc.vector.tensor_tensor(mix[:, s], mix[:, s], local_part[:, s], ALU.add).then_inc(mix_step, 1)
                    if inside(i, 8, j, CHUNKS):
                        s = j % 2
                        v.wait_ge(mem_done, c + 1)
                        wait(v, mix_step, 3 * (c - 1))
                        wait(v, diff_ready, c - 1)
                        wait(v, ct_done, c - 1)
                        dn = den[:, s].rearrange("p m (t h) -> p m t h", t=2)
                        src = [(ps_a[:, t, 0:3 * 8 * VW].rearrange("p (m h e) -> p m h e", m=3, e=VW), 0, 3, t) for t in range(2)] + \
                              [(ps_b[:, t, 0:2 * 8 * VW].rearrange("p (m h e) -> p m h e", m=2, e=VW), 3, 5, t) for t in range(2)]
                        for ps, m0, m1, t in src:
                            nc.vector.tensor_scalar(dn[:, m0:m1, t], ps[:, :, :, HD], ATT_EPS, None, ALU.max).then_inc(den_ready, 1)
                        v.wait_ge(den_ready, 4 * c + 4)
                        nc.vector.reciprocal(den[:, s], den[:, s]).then_inc(rden_ready, 1)
                        v.wait_ge(rden_ready, c + 1)
                        nc.vector.tensor_tensor(den[:, s], den[:, s], kept["coef"][:, bass.ds(i, 1)].rearrange("p i m h -> p (i m) h"),
                                                ALU.mult).then_inc(coef_ready, 1)
                        v.wait_ge(coef_ready, c + 1)
                        pr = prod[:, s].rearrange("p m (t h e) -> p m t h e", t=2, e=HD)
                        for ps, m0, m1, t in src:
                            for_all = dn[:, m0:m1, t, :, None].broadcast_to([P, m1 - m0, 8, HD])
                            nc.vector.tensor_tensor(pr[:, m0:m1, t], ps[:, :, :, 0:HD], for_all, ALU.mult).then_inc(prod_ready, 1)
                    if inside(i, 8, j - 3, CHUNKS):
                        s = (j - 3) % 2
                        wait(v, res_done, c - 3)
                        norm.rows(xn[:], c - 3).then_inc(xn_ready, 1)
                        wait(v, out_done, c - 2)
                        wait(v, xn_ready, c - 2)
                        wait(v, u_kept[s], 16 * (4 * i + (j - 3) // 2))
                        nc.vector.tensor_tensor(row[:, s, 0:D], ps_out[:, 0:D], xn[:], ALU.add).then_inc(res_done, 1)
                        wait(v, res_done, c - 2)
                        nc.vector.bn_stats(bn[:], row[:, s, 0:D]).then_inc(bn_done, 1)
                        wait(v, bn_done, c - 2)
                        nc.vector.tensor_copy(bn_copy[:], bn[:, 0:1])
                        nc.vector.bn_aggr(row[:, s, D:ROW], bn[:]).then_inc(stat_done, 1)

            run(v, body)


E, E1 = 16, 17
STEP = 64


def experts_phase(nc, ins, u, out):
    with ExitStack() as ctx:
        b = Buffers(nc, ctx, "moe")
        ident, ident_bf = b.sb("ident", [P, P]), b.sb("ident_bf", [P, P], BF16)
        pick = b.sb("pick", [STEP, E1, P], BF16)
        rank, r_bias = b.sb("rank", [P, E]), b.sb("r_bias", [P, E])
        wr_raw = b.sb("wr_raw", [P, KD, E])
        wr_hi, wr_lo = b.sb("wr_hi", [P, KD, E], F32R), b.sb("wr_lo", [P, KD, E], F32R)
        RAW = 4
        gu_raw, d_raw = b.sb("gu_raw", [P, RAW, KD, 2, P]), b.sb("d_raw", [P, RAW, D])
        gu_hi, gu_lo = b.sb("gu_hi", [P, E1, KD, 2, P], F32R), b.sb("gu_lo", [P, E1, KD, 2, P], F32R)
        d_hi, d_lo = b.sb("d_hi", [P, E1, D], F32R), b.sb("d_lo", [P, E1, D], F32R)
        norm = Normalizer(nc, b, u)
        xn = b.sb("xn", [P, 2, 4, D])
        x_hi, x_lo = b.sb("x_hi", [P, 2, KD, 512], F32R), b.sb("x_lo", [P, 2, KD, 512], F32R)
        logit, cand, first, second, rest = (b.sb(n, [P, 4, E]) for n in ("logit", "cand", "first", "second", "rest"))
        top, total, chosen = (b.sb(n, [P, 4]) for n in ("top", "total", "chosen"))
        weight, left = b.sb("weight", [P, 4, E1]), b.sb("left", [P, 4, E1])
        parts = b.sb("parts", [P, 4, STEP], BF16)
        w_T = b.sb("w_T", [STEP, 2, 512], BF16)
        sil, su, h = b.sb("sil", [P, 2, 512]), b.sb("su", [P, 512]), b.sb("h", [P, 2, 512])
        h_hi, h_lo = b.sb("h_hi", [P, 2, 512], F32R), b.sb("h_lo", [P, 2, 512], F32R)
        row = b.sb("row", [P, 4, D])
        bn, bn_copy, stats = b.sb("bn", [P, 4, 6]), b.sb("bn_copy", [P, 1]), b.sb("stats", [P, 4, 2])
        var, dev, dev_t = b.sb("var", [P, 4]), b.sb("dev", [P, 4]), b.sb("dev_t", [P, 4])
        ps_g, ps_u = b.ps("ps_g", [P, 2, 512]), b.ps("ps_u", [P, 2, 512])
        ps_w, ps_turn, ps_out = b.ps("ps_w", [P, 512]), b.ps("ps_turn", [P, 512]), b.ps("ps_out", [P, 4, D])
        (const_in, wr_ready, w_hi_ready, w_lo_ready, zeroed, xn_ready, turned, x_hi_ready, x_lo_ready, logits_done, route_step,
         exp_ready, wt_done, wt_ready, g_done, u_done, w_done, sil_ready, su_ready, h_ready, h_hi_ready, h_lo_ready, down_done,
         res_done, bn_done, stat_done, dev_step, row_ready, stored) = (b.sem(n) for n in (
            "const_in wr_ready w_hi_ready w_lo_ready zeroed xn_ready turned x_hi_ready x_lo_ready logits_done route_step "
            "exp_ready wt_done wt_ready g_done u_done w_done sil_ready su_ready h_ready h_hi_ready h_lo_ready down_done "
            "res_done bn_done stat_done dev_step row_ready stored").split())
        raw_in = [b.sem(f"raw_in{k}") for k in range(RAW)]
        out_rows = out.rearrange("(g c p) d -> p g c d", p=P, c=4)
        ROUTE, DEV = 25, 15
        ctx.callback(b.clear)
        block = ctx.enter_context(nc.Block())

        def run(engine, body):
            body(-1, 1)
            body(0, 0)
            body(0, 1)
            with engine.Fori(1, NG // 2 - 1) as i:
                body(i, 0)
                body(i, 1)
            body(NG // 2 - 1, 0)
            body(NG // 2 - 1, 1)
            body(NG // 2, 0)

        def exists(i, k):
            return tuple(inside(i, 2, k + d, NG) for d in (-1, 0, 1))

        def loaded(i, k, e):
            return e + 3 if isinstance(i, int) and i == 0 and k == 0 and e + 3 < E1 else None

        @block.sync
        def _(sp):
            consts = ((ident, "identity"), (ident_bf, "identity_bf"), (pick, "pick"), (rank, "rank"), (r_bias, "router_bias"))
            for t, name in consts:
                sp.dma_start(t[:], ins[name]).then_inc(const_in, 16)
            sp.dma_start(wr_raw[:], ins["router_T"].rearrange("(k p) e -> p k e", p=P)).then_inc(const_in, 16)
            for e in range(E1):
                wait(sp, w_lo_ready, e - RAW + 1)
                sp.dma_start(gu_raw[:, e % RAW].rearrange("p k w i -> p k (w i)"),
                             ins["w_gate_up"][e].rearrange("(k p) c -> p k c", p=P)).then_inc(raw_in[e % RAW], 16)
                sp.dma_start(d_raw[:, e % RAW], ins["w_down"][e]).then_inc(raw_in[e % RAW], 16)

            def body(i, k):
                if exists(i, k)[0]:
                    g = 2 * i + k - 1
                    sp.wait_ge(row_ready, 4 * (g + 1))
                    sp.dma_start(out_rows[:, bass.ds(g, 1)], row[:, None]).then_inc(stored, 16)

            run(sp, body)
            sp.wait_ge(stored, 16 * NG)

        @block.tensor
        def _(pe):
            def body(i, k):
                prev, cur, nxt = exists(i, k)
                g = 2 * i + k
                ns = (k + 1) % 2
                for e in range(E1):
                    n = E1 * g + e
                    s = (k + e) % 2
                    if cur:
                        if isinstance(i, int) and i == 0 and k == 0:
                            pe.wait_ge(w_lo_ready, e + 1)
                        if e == 0:
                            pe.wait_ge(x_lo_ready, 2 * (g + 1))
                            pe.wait_ge(wt_ready, g + 1)
                        for w, to, read, done in ((0, ps_g, sil_ready, g_done), (1, ps_u, su_ready, u_done)):
                            wait(pe, read, n - 1)
                            for d in range(KD):
                                m = product3(nc, to[:, s], gu_hi[:, e, d, w], gu_lo[:, e, d, w], x_hi[:, k, d], x_lo[:, k, d],
                                             d == 0, d == KD - 1)
                            m.then_inc(done, 1)
                        wait(pe, h_ready, n)
                        nc.tensor.matmul(ps_w[:], pick[:, e], w_T[:, k], start=True, stop=True).then_inc(w_done, 1)
                    if (cur if e >= 2 else prev):
                        ee = (e - 2) % E1
                        pe.wait_ge(h_lo_ready, n - 1)
                        if ee == 0:
                            wait(pe, res_done, 4 * g)
                        for c in range(4):
                            toks = slice(c * P, (c + 1) * P)
                            for j, (l, r) in enumerate(((h_hi, d_hi), (h_hi, d_lo), (h_lo, d_hi))):
                                m = nc.tensor.matmul(ps_out[:, c], l[:, s, toks], r[:, ee], start=(ee == 0 and c % 2 == 0 and j == 0),
                                                     stop=(ee == E1 - 1 and j == 2), skip_group_check=True)
                        m.then_inc(down_done, 1)
                    if nxt:
                        if e in (3, 5):
                            d = (e - 3) // 2
                            if e == 3:
                                pe.wait_ge(xn_ready, 4 * (g + 2))
                                wait(pe, wt_ready, g + 1)
                                if isinstance(i, int) and i < 0:
                                    pe.wait_ge(const_in, 96)
                                    pe.wait_ge(zeroed, 2)
                            else:
                                pe.wait_ge(x_lo_ready, 2 * (g + 1) + 1)
                            for c in range(4):
                                m = nc.tensor.transpose(ps_turn[:, c * P:(c + 1) * P], xn[:, ns, c, d * P:(d + 1) * P], ident[:])
                            m.then_inc(turned, 1)
                        if e == 7:
                            pe.wait_ge(x_lo_ready, 2 * (g + 2))
                            pe.wait_ge(wr_ready, 2)
                            for c in range(4):
                                toks = slice(c * P, (c + 1) * P)
                                for d in range(KD):
                                    m = product3(nc, ps_turn[:, c * E:(c + 1) * E], x_hi[:, ns, d, toks], x_lo[:, ns, d, toks],
                                                 wr_hi[:, d], wr_lo[:, d], d == 0, d == KD - 1)
                            m.then_inc(logits_done, 1)
                        if e == 15:
                            pe.wait_ge(route_step, ROUTE * (g + 2))
                            for c in range(4):
                                m = nc.tensor.matmul(ps_turn[0:STEP, c * P:(c + 1) * P], parts[:, c], ident_bf[:], start=True, stop=True)
                            m.then_inc(wt_done, 1)
                    if not (cur or nxt) and e == 1:
                        break

            run(pe, body)

        @block.scalar
        def _(act):
            act.wait_ge(const_in, 96)
            nc.scalar.activation(wr_hi[:], wr_raw[:], ACT.Copy).then_inc(wr_ready, 1)

            def weights(e):
                act.wait_ge(raw_in[e % RAW], 32 * (e // RAW + 1))
                nc.scalar.activation(gu_hi[:, e], gu_raw[:, e % RAW], ACT.Copy)
                nc.scalar.activation(d_hi[:, e], d_raw[:, e % RAW], ACT.Copy).then_inc(w_hi_ready, 1)

            def body(i, k):
                prev, cur, nxt = exists(i, k)
                g = 2 * i + k
                ns = (k + 1) % 2
                for e in range(E1):
                    n = E1 * g + e
                    s = (k + e) % 2
                    if cur:
                        act.wait_ge(g_done, n + 1)
                        wait(act, su_ready, n - 1)
                        nc.scalar.activation(sil[:, s], ps_g[:, s], ACT.Silu).then_inc(sil_ready, 1)
                    if (cur if e >= 1 else prev):
                        act.wait_ge(h_ready, n)
                        wait(act, down_done, n - 2)
                        nc.scalar.activation(h_hi[:, 1 - s], h[:, 1 - s], ACT.Copy).then_inc(h_hi_ready, 1)
                    if loaded(i, k, e):
                        weights(loaded(i, k, e))
                    if nxt:
                        if e in (3, 5):
                            act.wait_ge(turned, 2 * (g + 1) + (e - 3) // 2 + 1)
                            nc.scalar.activation(x_hi[:, ns, (e - 3) // 2], ps_turn[:], ACT.Copy).then_inc(x_hi_ready, 1)
                        if e == 9:
                            act.wait_ge(route_step, ROUTE * (g + 1) + 3)
                            nc.scalar.activation(rest[:], rest[:], ACT.Exp).then_inc(exp_ready, 1)
                        if e == 15:
                            act.wait_ge(wt_done, g + 2)
                            nc.scalar.activation(w_T[:, ns], ps_turn[0:STEP, :], ACT.Copy).then_inc(wt_ready, 1)
                    if not (cur or nxt) and e == 0:
                        break

            body(-1, 1)
            for e in range(3):
                weights(e)
            body(0, 0)
            body(0, 1)
            with act.Fori(1, NG // 2 - 1) as i:
                body(i, 0)
                body(i, 1)
            body(NG // 2 - 1, 0)
            body(NG // 2 - 1, 1)
            body(NG // 2, 0)

        @block.gpsimd
        def _(pool):
            pool.wait_ge(wr_ready, 1)
            nc.gpsimd.tensor_tensor(wr_lo[:], wr_raw[:], wr_hi[:].bitcast(F32), ALU.subtract).then_inc(wr_ready, 1)

            def weights(e):
                pool.wait_ge(w_hi_ready, e + 1)
                nc.gpsimd.tensor_tensor(gu_lo[:, e], gu_raw[:, e % RAW], gu_hi[:, e].bitcast(F32), ALU.subtract)
                nc.gpsimd.tensor_tensor(d_lo[:, e], d_raw[:, e % RAW], d_hi[:, e].bitcast(F32), ALU.subtract).then_inc(w_lo_ready, 1)

            def body(i, k):
                cur = exists(i, k)[1]
                for e in range(E1):
                    n = E1 * (2 * i + k) + e
                    s = (k + e) % 2
                    if cur:
                        pool.wait_ge(h_hi_ready, n + 1)
                        wait(pool, down_done, n - 1)
                        nc.gpsimd.tensor_tensor(h_lo[:, s], h[:, s], h_hi[:, s].bitcast(F32), ALU.subtract).then_inc(h_lo_ready, 1)
                    if loaded(i, k, e):
                        weights(loaded(i, k, e))

            for e in range(3):
                weights(e)
            run(pool, body)

        @block.vector
        def _(v):
            nc.vector.memset(parts[:], 0.0).then_inc(zeroed, 1)
            nc.vector.memset(weight[:], 1.0).then_inc(zeroed, 1)
            v.wait_ge(zeroed, 2)
            v.wait_ge(const_in, 96)
            norm.scales(v)

            def over(t, width):
                return t[:, :, None].broadcast_to([P, 4, width])

            def route(g, part):
                if part == 0:
                    link = Chain(v, route_step, ROUTE * g)
                    lg = ps_turn[:, 0:4 * E].rearrange("p (c e) -> p c e", e=E)
                    link(nc.vector.tensor_tensor(logit[:], lg, r_bias[:, None, :].broadcast_to([P, 4, E]), ALU.add))
                    link(nc.vector.tensor_reduce(top[:], logit[:], AX.X, ALU.max))
                    link(nc.vector.tensor_tensor(rest[:], logit[:], over(top, E), ALU.subtract))
                if part == 1:
                    link = Chain(v, route_step, ROUTE * g + 3)
                    link(nc.vector.tensor_tensor(cand[:], logit[:], over(top, E), ALU.is_equal))
                    link(nc.vector.tensor_tensor(cand[:], cand[:], rank[:, None, :].broadcast_to([P, 4, E]), ALU.mult))
                    link(nc.vector.tensor_reduce(top[:], cand[:], AX.X, ALU.max))
                    link(nc.vector.tensor_tensor(first[:], cand[:], over(top, E), ALU.is_equal))
                    link(nc.vector.scalar_tensor_tensor(logit[:], first[:], -1e30, logit[:], ALU.mult, ALU.add))
                if part == 2:
                    link = Chain(v, route_step, ROUTE * g + 8)
                    link(nc.vector.tensor_reduce(top[:], logit[:], AX.X, ALU.max))
                    link(nc.vector.tensor_tensor(cand[:], logit[:], over(top, E), ALU.is_equal))
                    link(nc.vector.tensor_tensor(cand[:], cand[:], rank[:, None, :].broadcast_to([P, 4, E]), ALU.mult))
                    link(nc.vector.tensor_reduce(top[:], cand[:], AX.X, ALU.max))
                    link(nc.vector.tensor_tensor(second[:], cand[:], over(top, E), ALU.is_equal))
                if part == 3:
                    link = Chain(v, route_step, ROUTE * g + 13)
                    v.wait_ge(exp_ready, g + 1)
                    link(nc.vector.tensor_tensor(first[:], first[:], second[:], ALU.add))
                    link(nc.vector.tensor_tensor(first[:], first[:], rest[:], ALU.mult))
                    link(nc.vector.tensor_reduce(total[:], rest[:], AX.X, ALU.add))
                    link(nc.vector.tensor_reduce(chosen[:], first[:], AX.X, ALU.add))
                    link(nc.vector.scalar_tensor_tensor(chosen[:], total[:], 1e-9, chosen[:], ALU.mult, ALU.add))
                if part == 4:
                    link = Chain(v, route_step, ROUTE * g + 18)
                    link(nc.vector.reciprocal(chosen[:], chosen[:]))
                    link(nc.vector.tensor_tensor(weight[:, :, 0:E], first[:], over(chosen, E), ALU.mult))
                    wait(v, wt_done, g)
                    hi, mid, lo = (parts[:, :, k * E1:(k + 1) * E1] for k in range(3))
                    link(nc.vector.tensor_copy(hi, weight[:]))
                    link(nc.vector.tensor_tensor(left[:], weight[:], hi, ALU.subtract))
                    link(nc.vector.tensor_copy(mid, left[:]))
                    link(nc.vector.tensor_tensor(left[:], left[:], mid, ALU.subtract))
                    link(nc.vector.tensor_copy(lo, left[:]))

            def deviation(g, part):
                link = Chain(v, dev_step, DEV * g + 3 * part)
                if part == 0:
                    link(nc.vector.tensor_scalar(var[:], stats[:, :, 1], LN_EPS, None, ALU.add))
                    first_guess(nc, link, var[:], dev[:], dev_t[:])
                else:
                    newton_step(nc, link, var[:], dev[:], dev_t[:])

            def body(i, k):
                prev, cur, nxt = exists(i, k)
                g = 2 * i + k
                ns = (k + 1) % 2
                for e in range(E1):
                    n = E1 * g + e
                    s = (k + e) % 2
                    if prev:
                        if e == 2:
                            v.wait_ge(down_done, E1 * g)
                            wait(v, stored, 16 * (g - 1))
                            for c in range(4):
                                nc.vector.tensor_tensor(row[:, c], ps_out[:, c], xn[:, ns, c], ALU.add).then_inc(res_done, 1)
                        if e == 3:
                            v.wait_ge(res_done, 4 * g)
                            for c in range(4):
                                nc.vector.bn_stats(bn[:, c], row[:, c]).then_inc(bn_done, 1)
                            v.wait_ge(bn_done, 4 * g)
                            nc.vector.tensor_copy(bn_copy[:], bn[:, 3, 0:1])
                            for c in range(4):
                                nc.vector.bn_aggr(stats[:, c], bn[:, c]).then_inc(stat_done, 1)
                        if e in (4, 5, 6, 7, 8):
                            if e == 4:
                                v.wait_ge(stat_done, 4 * g)
                            deviation(g - 1, e - 4)
                        if e == 9:
                            for c in range(4):
                                nc.vector.tensor_scalar(row[:, c], row[:, c], stats[:, c, 0:1], dev[:, c:c + 1],
                                                        ALU.subtract, ALU.mult).then_inc(row_ready, 1)
                    if cur:
                        v.wait_ge(sil_ready, n + 1)
                        v.wait_ge(u_done, n + 1)
                        wait(v, h_ready, n)
                        nc.vector.tensor_tensor(su[:], ps_u[:, s], sil[:, s], ALU.mult).then_inc(su_ready, 1)
                        v.wait_ge(su_ready, n + 1)
                        v.wait_ge(w_done, n + 1)
                        wait(v, h_lo_ready, n - 1)
                        nc.vector.tensor_tensor(h[:, s], ps_w[:], su[:], ALU.mult).then_inc(h_ready, 1)
                    if nxt:
                        if e == 2:
                            for c in range(4):
                                norm.rows(xn[:, ns, c], 4 * (g + 1) + c).then_inc(xn_ready, 1)
                        if e in (3, 5):
                            d = (e - 3) // 2
                            v.wait_ge(x_hi_ready, 2 * (g + 1) + d + 1)
                            nc.vector.tensor_tensor(x_lo[:, ns, d], ps_turn[:], x_hi[:, ns, d].bitcast(F32), ALU.subtract).then_inc(x_lo_ready, 1)
                        if e == 8:
                            v.wait_ge(logits_done, g + 2)
                        if e in (8, 9, 10, 11, 12):
                            route(g + 1, e - 8)
                    if not (cur or nxt) and e == 9:
                        break

            run(v, body)


def mixer_constants():
    import numpy as np

    t = np.arange(P)
    same = (t[:, None] // Q) == (t[None, :] // Q)
    upto = same & (t[:, None] <= t[None, :])
    after = same & (t[:, None] > t[None, :])
    first = np.repeat((t < Q)[:, None], P, 1)
    sums = -np.stack([upto, after, first, ~first], 1).astype(np.float32)
    stat = np.zeros((94, G, P), np.float32)
    stat[:Q] = np.where((t[None, :] % Q) > np.arange(Q)[:, None], -1e30, 0.0)[:, None, :]
    for k in range(3):
        for block in range(2):
            stat[Q + 2 * k + block] = (t // Q == block)
    mov = np.zeros((94, H, Q), np.float32)
    mov[:Q] = np.eye(Q)[:, None, :]
    for k in range(3):
        for j in range(8):
            mov[70 + 8 * k + j, j::8] = -1
    keep = np.ones((P, 9), np.float32)
    keep[:, 4] = 0
    bf = np.dtype("bfloat16")
    return {"neg_tri": np.ascontiguousarray(sums[:, 0]), "sum_masks": sums, "stat_const": stat.astype(bf),
            "mov_const": mov.reshape(94, H * Q).astype(bf), "keep_rows": keep, "identity": np.eye(P, dtype=np.float32)}


def layouts(x):
    import numpy as np

    c = np.ascontiguousarray
    tokens = c(x["L0_attn_input_"]).reshape(TOKENS, D)
    w_in = x["L0_attn_in_proj_w"]
    a = {
        "x": tokens, "xT": c(tokens.T), "w_projT": c(w_in[:2048].T), "w_stepT": c(w_in[2048:].T),
        "d_rows": c(np.broadcast_to(x["L0_attn_D"], (P, H))),
        "conv_w": c(x["L0_attn_conv1d_weight"].reshape(CONV * P, 4)),
        "conv_b": c(x["L0_attn_conv1d_bias"].reshape(CONV, P).T),
        "z_b": c(x["L0_attn_z_bias"].reshape(4, P).T),
        "w_outT": c(x["L0_attn_out_proj_w"].T),
        "w1T": np.pad(x["L0_ffn_w1"].T, ((0, 0), (0, FT * P - HIDDEN))),
        "w2T": np.pad(x["L0_ffn_w2"].T, ((0, 0), (0, FT * P - HIDDEN))),
        "w3T": np.pad(x["L0_ffn_w3"].T, ((0, FT * P - HIDDEN), (0, 0))),
    }
    for n in "qkvo":
        a[f"w{n}T"] = c(x[f"L1_attn_w_{n}"].T)
    mem = np.zeros((2, 8, HD, NM, 8, VW), np.float32)
    fine = x["L1_attn_fine_memories"].reshape(NM, 2, 8, HD, HD)
    norms = x["L1_attn_fine_memory_norms"].reshape(NM, 2, 8, HD)
    for h in range(8):
        mem[:, h, :, :, h, :HD] = fine[:, :, h].transpose(1, 2, 0, 3)
        mem[:, h, :, :, h, HD] = norms[:, :, h].transpose(1, 2, 0)
    a["mem_blocks"] = c(mem.reshape(2, P, NM, 8 * VW).transpose(1, 0, 2, 3))
    a["gate_rows"] = c(np.broadcast_to(x["L1_attn_memory_gate"], (P, NH)))
    a["eg_w1T"], a["eg_w2T"] = c(x["L1_attn_eg_w1"].T), c(x["L1_attn_eg_w2"].T)
    a["eg_b1"] = c(x["L1_attn_eg_b1"].reshape(64, 1))
    a["eg_b2_rows"] = c(np.broadcast_to(x["L1_attn_eg_b2"], (P, 1)))
    a.update(mixer_constants())
    ch = np.arange(P)
    blocks = (ch[:, None] // HD == np.arange(8)[None, :]).astype(np.float32)
    a["head_blocks"] = c(np.broadcast_to(np.repeat(blocks, VW, 1)[:, None], (P, 2, 8 * VW)))
    a["parity"] = np.stack([(ch // HD % 2 == k).astype(np.float32) for k in range(2)], 1)
    a["upper_ones"] = np.tile(np.triu(np.ones((Q, Q), np.float32)), (P // Q, 1))
    kb = np.ones((P, NG // 2 + 1), np.float32)
    kb[:, 2] = 0
    a["keep_batches"] = kb
    stack = lambda n: np.concatenate([x[f"L1_ffn_{n}"], x[f"L1_ffn_s{n}"][None]])
    a["w_gate_up"], a["w_down"] = np.concatenate([stack("Wg"), stack("Wu")], 2), stack("Wd")
    a["router_T"], a["router_bias"] = c(x["L1_ffn_Wr"].T), c(np.broadcast_to(x["L1_ffn_bias"], (P, E)))
    a["rank"] = c(np.broadcast_to(np.arange(E, 0, -1, dtype=np.float32), (P, E)))
    pick = np.zeros((STEP, E1, P), np.float32)
    for k in range(3):
        for e in range(E1):
            pick[k * E1 + e, e] = 1
    a["pick"], a["identity_bf"] = pick.astype(a["stat_const"].dtype), a["identity"].astype(a["stat_const"].dtype)
    return a


def mixer_keep(nc, ctx):
    b = Buffers(nc, ctx, "keep")
    return {
        "w_hi": b.sb("w_hi", [P, KD, 2048], F32R), "w_lo": b.sb("w_lo", [P, KD, 2048], F32R),
        "wo_hi": b.sb("wo_hi", [P, 4, D], F32R), "wo_lo": b.sb("wo_lo", [P, 4, D], F32R),
        "conv_w": b.sb("conv_w", [P, CONV, 4]), "conv_b": b.sb("conv_b", [P, CONV]), "z_b": b.sb("z_b", [P, 4]),
    }


def build_program(nc, ins, out):
    with ExitStack() as ctx:
        u = Buffers(nc, ctx, "all").sb("u", [P, CHUNKS, ROW])
        scratch = {"steps": nc.dram_tensor("steps_scratch", [CHUNKS, P, 2, H], F32).ap(),
                   "parts": nc.dram_tensor("parts_scratch", [CHUNKS, H, 3, P], BF16).ap()}
        with ExitStack() as mixer_ctx:
            keep = mixer_keep(nc, mixer_ctx)
            steps_phase(nc, ins, keep, scratch)
            mixer_phase(nc, ins, keep, scratch, u)
        ffn_phase(nc, ins, u)
        attention_phase(nc, ins, u)
        experts_phase(nc, ins, u, out)


def kernel(**inputs):
    import numpy as np
    import concourse.bacc as bacc
    from concourse.bass_utils import run_bass_kernel_spmd

    nc = bacc.Bacc("TRN2", target_bir_lowering=False, num_devices=1)
    arrays = {name: np.ascontiguousarray(a) for name, a in layouts({k: np.asarray(a) for k, a in inputs.items()}).items()}
    ins = {name: nc.dram_tensor(name, list(a.shape), mybir.dt.from_np(a.dtype), kind="ExternalInput").ap()
           for name, a in arrays.items()}
    out = nc.dram_tensor("out", [TOKENS, D], F32, kind="ExternalOutput").ap()
    build_program(nc, ins, out)
    launched = run_bass_kernel_spmd(nc, [arrays], core_ids=[0])
    return launched.results[0]["out"].reshape(BATCHES, TOKENS // BATCHES, D)
```

```python
from contextlib import ExitStack

import concourse.bass as bass
from concourse import mybir

F32 = mybir.dt.float32
F32R = mybir.dt.float32r
BF16 = mybir.dt.bfloat16
I32 = mybir.dt.int32
U32 = mybir.dt.uint32
ALU = mybir.AluOpType
ACT = mybir.ActivationFunctionType
AX = mybir.AxisListType

P = 128
TOKENS, D = 4096, 256
CHUNKS = TOKENS // P
BATCHES = 2
KD = D // P
LN_EPS = 1e-5
ROW = D + 2
H = 64
HP = 8
G = 8
Q = 64
CONV = 12
TILES = 16
GROUP = 256


def wait(engine, sem, value):
    if not isinstance(value, int) or value > 0:
        engine.wait_ge(sem, value)


def inside(i, per, k, end):
    return not isinstance(i, int) or 0 <= per * i + k < end


class Buffers:

    def __init__(self, nc, ctx, phase):
        self.nc, self.ctx, self.phase, self.sems = nc, ctx, phase, []

    def sb(self, name, shape, dt=F32):
        return self.ctx.enter_context(self.nc.sbuf_tensor(f"{self.phase}_{name}", shape, dt))

    def ps(self, name, shape, dt=F32):
        return self.ctx.enter_context(self.nc.psum_tensor(f"{self.phase}_{name}", shape, dt))

    def sem(self, name):
        self.sems.append(self.nc.alloc_semaphore(f"{self.phase}_{name}"))
        return self.sems[-1]

    def clear(self):
        self.nc.clear_and_free_semaphores(self.sems)
        self.nc.all_engine_barrier()


def product3(nc, out, l_hi, l_lo, r_hi, r_lo, first, last):
    nc.tensor.matmul(out, l_hi, r_hi, start=first, stop=False)
    nc.tensor.matmul(out, l_hi, r_lo, start=False, stop=False)
    return nc.tensor.matmul(out, l_lo, r_hi, start=False, stop=last)


class Chain:

    def __init__(self, engine, sem, n=0):
        self.engine, self.sem, self.n = engine, sem, n

    def __call__(self, instruction):
        self.n = self.n + 1
        instruction.then_inc(self.sem, 1)
        self.engine.wait_ge(self.sem, self.n)

    def beside(self, instruction):
        self.n = self.n + 1
        instruction.then_inc(self.sem, 1)


def first_guess(nc, link, v, y):
    link(nc.vector.tensor_scalar(y.bitcast(I32), v.bitcast(I32), -0.5, float(0x5F3759DF), ALU.mult, ALU.add))


def newton_step(nc, link, v, y, t):
    link(nc.vector.scalar_tensor_tensor(t, y, -0.5, y, ALU.mult, ALU.mult))
    link(nc.vector.tensor_tensor(t, t, v, ALU.mult))
    link(nc.vector.scalar_tensor_tensor(y, t, 1.5, y, ALU.add, ALU.mult))


def inverse_deviation(nc, link, v, y, t):
    first_guess(nc, link, v, y)
    for _ in range(3):
        newton_step(nc, link, v, y, t)


def steps_phase(nc, ins, keep, scratch):
    with ExitStack() as ctx:
        b = Buffers(nc, ctx, "steps")
        C8, N = 8, 8 * P
        xT = b.sb("xT", [P, TOKENS // N, KD, N])
        w_step = b.sb("w_step", [P, KD, H])
        d_row = b.sb("d_row", [P, H])
        neg_tri = b.sb("neg_tri", [P, P])
        W = C8 * H
        w1, magnitude, negative, r, lg = (b.sb(n, [P, W]) for n in ("w1", "magnitude", "negative", "r", "lg"))
        positive = b.sb("positive", [P, 2, W])
        e = b.sb("e", [P, 2, W])
        steps = b.sb("steps", [P, 2, C8, 2, H])
        parts = b.sb("parts", [H, 2, C8, 3, P], BF16)
        sum_copy = b.sb("sum_copy", [H, 2, N])
        rest = b.sb("rest", [H, 2, N])
        w_raw = b.sb("w_raw", [P, KD, 2048])
        wo_raw = b.sb("wo_raw", [P, 4, D])
        a_log = b.ps("a_log", [P, 2, 512])
        sums = b.ps("sums", [P, 2, N])
        x_in = [b.sem(f"x_in{k}") for k in range(TOKENS // N)]
        w_step_in, const_in, w_in, out_done = b.sem("w_step_in"), b.sem("const_in"), b.sem("w_in"), [b.sem(f"out_done{k}") for k in range(2)]
        mixer_in = b.sem("mixer_in")
        log_done, abs_ready, exp_done, one_plus_ready = (b.sem(n) for n in ("log_done", "abs_ready", "exp_done", "one_plus_ready"))
        ln_done, dt_ready, sum_done = (b.sem(n) for n in ("ln_done", "dt_ready", "sum_done"))
        parts_ready, rest_ready, mid_ready = ([b.sem(f"{n}{k}") for k in range(2)] for n in ("parts_ready", "rest_ready", "mid_ready"))
        dd_ready, dd_done, dve_chain, hi_ready, lo_ready = (b.sem(n) for n in ("dd_ready", "dd_done", "dve_chain", "hi_ready", "lo_ready"))
        halved, positive_ready, high_ready = b.sem("halved"), b.sem("positive_ready"), b.sem("high_ready")
        groups = TOKENS // N
        x_src = ins["xT"].rearrange("(k p) t -> p k t", p=P)
        ctx.callback(b.clear)
        block = ctx.enter_context(nc.Block())

        def split(engine, ops, g):
            k = g % 2
            engine.wait_ge(high_ready, g + 1)
            s, rs = (x[:, k].rearrange("h (c s) -> h c s", c=C8) for x in (sum_copy, rest))
            hi, mid, lo = (parts[:, k, :, n, :] for n in range(3))
            ops.tensor_tensor(rs, s, hi, ALU.subtract).then_inc(rest_ready[k], 1)
            engine.wait_ge(rest_ready[k], g // 2 + 1)
            ops.tensor_copy(mid, rs).then_inc(mid_ready[k], 1)
            engine.wait_ge(mid_ready[k], g // 2 + 1)
            ops.tensor_tensor(lo, rs, mid, ALU.subtract).then_inc(parts_ready[k], 1)

        @block.sync
        def _(sp):
            sp.dma_start(w_step[:], ins["w_stepT"].rearrange("(k p) h -> p k h", p=P)).then_inc(w_step_in, 16)
            for g in range(groups):
                sp.dma_start(xT[:, g], x_src[:, :, g * N:(g + 1) * N]).then_inc(x_in[g], 16)
                if g == 0:
                    sp.dma_start(neg_tri[:], ins["neg_tri"]).then_inc(const_in, 16)
                    sp.dma_start(d_row[:], ins["d_rows"]).then_inc(const_in, 16)
            for t, name in ((keep["ident"][:], "identity"), (keep["sum_masks"][:], "sum_masks"), (keep["keep_rows"][:], "keep_rows")):
                sp.dma_start(t, ins[name]).then_inc(mixer_in, 16)
            for k in range(2):
                sp.dma_start(keep["mov"][:, k], ins["mov_const"]).then_inc(mixer_in, 16)
                sp.dma_start(keep["stat"][:, k], ins["stat_const"]).then_inc(mixer_in, 16)
            for g in range(groups):
                sp.wait_ge(parts_ready[g % 2], g // 2 + 1)
                sp.wait_ge(dd_done, g + 1)
                sp.dma_start(scratch["parts"][C8 * g:C8 * (g + 1)].rearrange("c h k s -> h c k s"),
                             parts[:, g % 2]).then_inc(out_done[g % 2], 16)
                sp.dma_start(scratch["steps"][C8 * g:C8 * (g + 1)].rearrange("c p k h -> p c k h"),
                             steps[:, g % 2]).then_inc(out_done[g % 2], 16)
            sp.wait_ge(mixer_in, 16 * 7)
            for k in range(2):
                sp.wait_ge(out_done[k], 32 * (groups // 2))

        @block.tensor
        def _(pe):
            def logs(g):
                pe.wait_ge(x_in[g], 16)
                if g >= 2:
                    pe.wait_ge(positive_ready, g - 1)
                for c in range(C8):
                    for k in range(KD):
                        m = nc.tensor.matmul(a_log[:, g % 2, c * H:(c + 1) * H], xT[:, g, k, c * P:(c + 1) * P],
                                             w_step[:, k, :], start=(k == 0), stop=(k == KD - 1))
                m.then_inc(log_done, 1)

            pe.wait_ge(w_step_in, 16)
            logs(0)
            logs(1)
            pe.wait_ge(const_in, 32)
            for g in range(groups):
                pe.wait_ge(dt_ready, g + 1)
                if g >= 2:
                    pe.wait_ge(high_ready, g - 1)
                for c in range(C8):
                    m = nc.tensor.matmul(sums[0:H, g % 2, c * P:(c + 1) * P],
                                         steps[:, g % 2, c, 0, :], neg_tri[:, :], start=True, stop=True)
                m.then_inc(sum_done, 1)
                if g + 2 < groups:
                    logs(g + 2)

        @block.scalar
        def _(act):
            act.wait_ge(x_in[0], 16)
            act.dma_start(w_raw[:], ins["w_projT"].rearrange("(k p) c -> p k c", p=P)).then_inc(w_in, 16)
            act.dma_start(wo_raw[:], ins["w_outT"].rearrange("(k p) c -> p k c", p=P)).then_inc(w_in, 16)
            act.dma_start(keep["conv_w"][:], ins["conv_w"].rearrange("(t p) k -> p t k", p=P)).then_inc(w_in, 16)
            act.dma_start(keep["conv_b"][:], ins["conv_b"]).then_inc(w_in, 16)
            act.dma_start(keep["z_b"][:], ins["z_b"]).then_inc(w_in, 16)
            nc.scalar.preload_act_table_set("natural_log_exp_and_others")

            def signs(g):
                act.wait_ge(log_done, g + 1)
                if g:
                    act.wait_ge(abs_ready, g)
                if g >= 2:
                    act.wait_ge(dt_ready, g - 1)
                nc.scalar.activation(positive[:, g % 2], a_log[:, g % 2], ACT.Relu)
                nc.scalar.activation(negative[:], a_log[:, g % 2], ACT.Relu, scale=-1.0).then_inc(positive_ready, 1)

            def exponential(g):
                act.wait_ge(abs_ready, g + 1)
                nc.scalar.activation(e[:, g % 2], magnitude[:], ACT.Exp, scale=-1.0).then_inc(exp_done, 1)

            def high(g):
                act.wait_ge(sum_done, g + 1)
                if g >= 2:
                    act.wait_ge(out_done[g % 2], 32 * (g // 2))
                nc.scalar.activation(sum_copy[:, g % 2], sums[0:H, g % 2, :], ACT.Copy)
                nc.scalar.activation(parts[:, g % 2, :, 0, :], sums[0:H, g % 2, :].rearrange("h (c s) -> h c s", c=C8),
                                     ACT.Copy).then_inc(high_ready, 1)

            signs(0)
            exponential(0)
            for g in range(groups):
                if g + 1 < groups:
                    signs(g + 1)
                act.wait_ge(one_plus_ready, g + 1)
                nc.scalar.activation(lg[:], w1[:], ACT.Ln).then_inc(ln_done, 1)
                if g + 1 < groups:
                    exponential(g + 1)
                if g == 0:
                    act.wait_ge(w_in, 80)
                    nc.scalar.activation(keep["w_hi"][:], w_raw[:], ACT.Copy).then_inc(hi_ready, 1)
                    nc.scalar.activation(keep["wo_hi"][:], wo_raw[:], ACT.Copy).then_inc(hi_ready, 1)
                high(g)

        @block.gpsimd
        def _(pool):
            pool.wait_ge(w_in, 80)
            for t in (keep["conv_w"], keep["conv_b"], keep["z_b"]):
                nc.gpsimd.tensor_scalar(t[:], t[:], 0.5, None, ALU.mult).then_inc(halved, 1)
            pool.wait_ge(hi_ready, 2)
            nc.gpsimd.tensor_tensor(keep["w_lo"][:], w_raw[:], keep["w_hi"][:].bitcast(F32), ALU.subtract).then_inc(lo_ready, 1)
            nc.gpsimd.tensor_tensor(keep["wo_lo"][:], wo_raw[:], keep["wo_hi"][:].bitcast(F32), ALU.subtract).then_inc(lo_ready, 1)
            for g in range(groups - 1):
                split(pool, nc.gpsimd, g)
            pool.wait_ge(lo_ready, 2)
            pool.wait_ge(halved, 3)

        @block.vector
        def _(v):
            link = Chain(v, dve_chain)

            def magnitudes(g):
                v.wait_ge(positive_ready, g + 1)
                if g:
                    v.wait_ge(exp_done, g)
                nc.vector.tensor_tensor(magnitude[:], positive[:, g % 2], negative[:], ALU.add).then_inc(abs_ready, 1)

            magnitudes(0)
            v.wait_ge(const_in, 32)
            for g in range(groups):
                dtg, ddg = steps[:, g % 2, :, 0, :], steps[:, g % 2, :, 1, :]
                ex = e[:, g % 2]
                v.wait_ge(exp_done, g + 1)
                nc.vector.tensor_scalar(w1[:], ex, 1.0, None, ALU.add).then_inc(one_plus_ready, 1)
                v.wait_ge(one_plus_ready, g + 1)
                link(nc.vector.tensor_scalar(r[:], w1[:], -1.0, 2.0 ** -23, ALU.add, ALU.max))
                link(nc.vector.reciprocal(r[:], r[:]))
                if g + 1 < groups:
                    magnitudes(g + 1)
                v.wait_ge(ln_done, g + 1)
                link(nc.vector.tensor_tensor(lg[:], lg[:], r[:], ALU.mult))
                link(nc.vector.scalar_tensor_tensor(w1[:], w1[:], 1.0, lg[:], ALU.is_equal, ALU.max))
                link(nc.vector.tensor_tensor(ex, ex, w1[:], ALU.mult))
                if g >= 2:
                    v.wait_ge(out_done[g % 2], 32 * (g // 2))
                by_chunk = lambda t: t.rearrange("p (c h) -> p c h", c=C8)
                nc.vector.tensor_tensor(dtg, by_chunk(positive[:, g % 2]), by_chunk(ex), ALU.add).then_inc(dt_ready, 1)
                v.wait_ge(dt_ready, g + 1)
                nc.vector.reciprocal(ddg, dtg).then_inc(dd_ready, 1)
                v.wait_ge(dd_ready, g + 1)
                nc.vector.tensor_tensor(ddg, ddg, d_row[:, None, :].broadcast_to([P, C8, H]), ALU.mult).then_inc(dd_done, 1)
            split(v, nc.vector, groups - 1)


def mixer_phase(nc, ins, keep, scratch, u):
    with ExitStack() as ctx:
        b = Buffers(nc, ctx, "mix")
        x_raw = b.sb("x_raw", [P, KD, GROUP])
        x_hi = b.sb("x_hi", [P, 2, KD, GROUP], F32R)
        x_lo = b.sb("x_lo", [P, 2, KD, GROUP], F32R)
        raw = b.sb("raw", [P, CONV, 3 + GROUP])
        xbc = b.sb("xbc", [P, 2, CONV, GROUP])
        gate = b.sb("gate", [P, 2, 4, GROUP])
        th = b.sb("th", [P, 2, GROUP])
        zt = b.sb("zt", [P, 2, 2, GROUP])
        decay = b.sb("decay", [P, 2, 2, 512])
        cb = b.sb("cb", [P, 2, G, Q])
        sums = b.sb("sums", [P, 2, 4, H])
        steps = b.sb("steps", [P, 2, 2, H])
        x_blocks = b.sb("x_blocks", [P, 2, H, 2, HP])
        x_dec = b.sb("x_dec", [P, H, HP])
        y = b.sb("y", [P, 2, H, HP])
        tmp = b.sb("tmp", [P, H, HP])
        b_tok = b.sb("b_tok", [P, 512])
        state = b.sb("state", [P, 4, 2, Q])
        yg = b.sb("yg", [P, 4, P])
        yg_hi = b.sb("yg_hi", [P, 4, P], F32R)
        yg_lo = b.sb("yg_lo", [P, 4, P], F32R)
        x_res = b.sb("x_res", [P, 2, ROW])
        bn, bn_copy = b.sb("bn", [P, 6]), b.sb("bn_copy", [P, 1])
        ps_proj = b.ps("ps_proj", [P, 2, GROUP])
        ps_off = b.ps("ps_off", [P, H, HP])
        ps_decay = b.ps("ps_decay", [P, 2, 512])
        ps_diag = b.ps("ps_diag", [P, 2, 512])
        ps_turn = b.ps("ps_turn", [P, 512])
        ps_misc = b.ps("ps_misc", [P, 512])
        (x_in, init, x_hi_ready, x_lo_ready, proj_done, raw_ready, taps, th_ready, final, halo_ready,
         decay_done, exp_done, g_ready, diag_done, assembled, sums_done, sums_ready, xt_done, blocks_ready, xdec_ready,
         du_ready, bt_done, btok_ready, cb_done, cb_ready, off_done, st_done, state_ready, reset_ready, off_read,
         y_ready, yt_done, gated, yg_hi_ready, yg_lo_ready, out_done, res_done, bn_done, stat_done) = (b.sem(n) for n in (
            "x_in init x_hi_ready x_lo_ready proj_done raw_ready taps th_ready final halo_ready "
            "decay_done exp_done g_ready diag_done assembled sums_done sums_ready xt_done blocks_ready xdec_ready "
            "du_ready bt_done btok_ready cb_done cb_ready off_done st_done state_ready reset_ready off_read "
            "y_ready yt_done gated yg_hi_ready yg_lo_ready out_done res_done bn_done stat_done").split())
        steps_in = [b.sem(f"steps_in{k}") for k in range(2)]
        parts_in = [b.sem(f"parts_in{k}") for k in range(2)]
        res_in = [b.sem(f"res_in{k}") for k in range(2)]
        kept = [b.sem(f"kept{k}") for k in range(2)]
        ctx.callback(b.clear)
        block = ctx.enter_context(nc.Block())
        w_hi, w_lo, wo_hi, wo_lo = keep["w_hi"], keep["w_lo"], keep["wo_hi"], keep["wo_lo"]
        conv_w, conv_b, z_b = keep["conv_w"], keep["conv_b"], keep["z_b"]
        ident, sum_masks, keep_rows, mov, stat = (keep[n] for n in ("ident", "sum_masks", "keep_rows", "mov", "stat"))
        xT_src = ins["xT"].rearrange("(k p) t -> p k t", p=P)

        def run(engine, body):
            body(-1)
            body(0)
            with engine.Fori(1, 7) as i:
                body(i)
            body(7)
            body(8)

        def pair(i, m):
            k = m + 11
            return 2 * i + k // 8, k % 8, (k // 8) % 2

        def in_group(q):
            return (q // 2) % 2, (q % 2) * P

        @block.sync
        def _(sp):
            def body(i):
                for q in range(4):
                    if q % 2 == 0 and inside(i, 2, 2 + q // 2, 16):
                        g = 2 * i + 2 + q // 2
                        wait(sp, x_lo_ready, g)
                        sp.dma_start(x_raw[:], xT_src[:, :, bass.ds(g * GROUP, GROUP)]).then_inc(x_in, 16)
                    if inside(i, 4, q + 2, CHUNKS):
                        wait(sp, du_ready, 4 * i + q + 1)
                        sp.dma_start(steps[:, q % 2], scratch["steps"][bass.ds(4 * i + q + 2, 1)].rearrange(
                            "c p k h -> (c p) k h")).then_inc(steps_in[q % 2], 16)
                    if inside(i, 4, q + 1, CHUNKS):
                        k = (q + 1) % 2
                        wait(sp, decay_done, 4 * (4 * i + q))
                        src = scratch["parts"][bass.ds(4 * i + q + 1, 1)]
                        for part in range(3):
                            rows = src[:, :, part, :]
                            for blk in range(2):
                                r = Q + 2 * part + blk
                                sp.dma_start(mov[r:r + 1, k].rearrange("o (h s) -> o h s", s=Q),
                                             rows[:, :, blk * Q:(blk + 1) * Q]).then_inc(parts_in[k], 16)
                            r = 70 + 8 * part
                            sp.dma_start(stat[r:r + 8, k], rows.rearrange("c (g j) z -> (c j) g z", g=G)).then_inc(parts_in[k], 16)
                    if inside(i, 4, q - 2, CHUNKS - 1):
                        wait(sp, stat_done, 4 * i + q - 1)
                        sp.dma_start(u[:, bass.ds(4 * i + q - 2, 1), :], x_res[:, q % 2, None, :]).then_inc(kept[q % 2], 16)
                    if inside(i, 4, q, CHUNKS):
                        wait(sp, kept[q % 2], 16 * (2 * i + q // 2))
                        sp.dma_start(x_res[:, q % 2, 0:D], ins["x"][bass.ds((4 * i + q) * P, P), :]).then_inc(res_in[q % 2], 16)

            run(sp, body)
            for k in range(2):
                sp.wait_ge(kept[k], 16 * ((CHUNKS - k) // 2))

        @block.tensor
        def _(pe):
            pe.wait_ge(init, 6)

            def body(i):
                for m in range(16 if not (isinstance(i, int) and i == 8) else 4):
                    q, s = m // 4, m % 4
                    n = 16 * i + m
                    c = 4 * i + q
                    if inside(i, 16, m + 1, 128):
                        k = ((m + 1) // 4) % 2
                        if s == 3:
                            pe.wait_ge(parts_in[k], 144 * ((4 * i + q + 1 - k) // 2 + 1) if isinstance(i, int)
                                       else 144 * (2 * i + (q + 1) // 2 + 1))
                        wait(pe, exp_done, n + 1)
                        for t in range(2):
                            g = 2 * ((s + 1) % 4) + t
                            mm = nc.tensor.matmul(ps_decay[:, t, :], stat[:, k, g, :], mov[:, k, g * 512:(g + 1) * 512],
                                                  start=True, stop=True)
                        mm.then_inc(decay_done, 1)
                    if inside(i, 16, m + 11, 128):
                        g, p, slot = pair(i, m)
                        if p == 0:
                            pe.wait_ge(x_lo_ready, g + 1)
                        wait(pe, raw_ready, n + 11)
                        for t in range(2):
                            cols = slice((2 * p + t) * P, (2 * p + t + 1) * P)
                            for k in range(KD):
                                mm = product3(nc, ps_proj[:, t, :], w_hi[:, k, cols], w_lo[:, k, cols],
                                              x_hi[:, slot, k, :], x_lo[:, slot, k, :], k == 0, k == KD - 1)
                        mm.then_inc(proj_done, 1)
                    if inside(i, 4, q + 1, CHUNKS):
                        slot, t0 = in_group(q + 1)
                        tok = slice(t0, t0 + P)
                        grp = 2 * i + (q + 1) // 2
                        sl = (q + 1) % 2
                        if s == 0:
                            pe.wait_ge(steps_in[sl], 16 * ((4 * i + q + 1) // 2 + 1) if isinstance(i, int)
                                       else 16 * (2 * i + (q + 1) // 2 + 1))
                            wait(pe, cb_ready, 2 * (c + 1))
                            for k in range(4):
                                mm = nc.tensor.matmul(ps_misc[:, k * H:(k + 1) * H], sum_masks[:, k, :],
                                                      steps[:, sl, 0, :], start=True, stop=True)
                            mm.then_inc(sums_done, 1)
                            pe.wait_ge(final, 8 * grp + 2)
                            wait(pe, state_ready, 8 * (c + 1))
                            for k in range(4):
                                mm = nc.tensor.transpose(ps_turn[:, k * P:(k + 1) * P], xbc[:, slot, k, tok], ident[:])
                            mm.then_inc(xt_done, 1)
                        if s == 1:
                            pe.wait_ge(final, 8 * grp + 6)
                            pe.wait_ge(sums_ready, c + 2)
                            pe.wait_ge(du_ready, c + 2)
                            for k in range(4):
                                mm = nc.tensor.transpose(ps_turn[:, k * P:(k + 1) * P], xbc[:, slot, 4 + k, tok], ident[:])
                            mm.then_inc(bt_done, 1)
                            scores(slot, t0, 0)
                        if s == 2:
                            wait(pe, off_read, c + 1)
                            wait(pe, state_ready, 8 * (c + 1))
                            pe.wait_ge(reset_ready, (4 * i + q + 1) // 4 + 1 if isinstance(i, int) else i + (q + 1) // 4 + 1)
                            pe.wait_ge(cb_ready, 2 * c + 3)
                            from_state(slot, t0, 0)
                            scores(slot, t0, 1)
                            pe.wait_ge(btok_ready, c + 2)
                            to_state(0)
                        if s == 3:
                            pe.wait_ge(state_ready, 8 * (c + 1) + 4)
                            from_state(slot, t0, 1)
                            to_state(1)
                    if inside(i, 4, q - 1, CHUNKS):
                        if s == 0:
                            pe.wait_ge(assembled, 8 * c)
                            for k in range(4):
                                mm = nc.tensor.transpose(ps_diag[:, 1, k * P:(k + 1) * P],
                                                         y[:, (q - 1) % 2].rearrange("t h p -> t (h p)")[:, k * P:(k + 1) * P], ident[:])
                            mm.then_inc(yt_done, 1)
                    if inside(i, 4, q, CHUNKS):
                        pe.wait_ge(g_ready, n + 1)
                        if s == 0:
                            pe.wait_ge(blocks_ready, 2 * c + 2)
                            wait(pe, assembled, 8 * c)
                        if s == 2:
                            wait(pe, res_done, c)
                        for t in range(2):
                            for k in range(4):
                                h = 8 * (2 * s + t) + 2 * k
                                col = (2 * (s % 2) + t) * P + k * 32
                                mm = nc.tensor.matmul(ps_diag[:, s // 2, col:col + 32], decay[:, m % 2, t, k * P:(k + 1) * P],
                                                      x_blocks[:, q % 2, h:h + 2].rearrange("z h b p -> z (h b p)"),
                                                      start=True, stop=True)
                        mm.then_inc(diag_done, 1)
                    if inside(i, 4, q - 1, CHUNKS) and s == 1:
                        pe.wait_ge(yg_lo_ready, c)
                        for k in range(4):
                            mm = product3(nc, ps_diag[:, 1, 0:D], yg_hi[:, k, :], yg_lo[:, k, :],
                                          wo_hi[:, k, :], wo_lo[:, k, :], k == 0, k == 3)
                        mm.then_inc(out_done, 1)

            def scores(slot, t0, odd):
                rows = slice(64 * odd, 64 * odd + 64)
                for k in range(4):
                    for blk in range(2):
                        toks = slice(t0 + Q * blk, t0 + Q * blk + Q)
                        mm = nc.tensor.matmul(ps_misc[Q * blk:Q * blk + Q, (4 * odd + k) * Q:(4 * odd + k + 1) * Q],
                                              xbc[rows, slot, 4 + k, toks], xbc[rows, slot, 8 + k, toks], start=True, stop=True)
                mm.then_inc(cb_done, 1)

            def from_state(slot, t0, blk):
                toks = slice(t0 + Q * blk, t0 + Q * blk + Q)
                out = ps_off[Q * blk:Q * blk + Q].rearrange("t h p -> t (h p)")
                for k in range(4):
                    mm = nc.tensor.matmul(out[:, k * P:(k + 1) * P], xbc[:, slot, 8 + k, toks],
                                          state[:, k].rearrange("n a c -> n (a c)"), start=True, stop=True)
                mm.then_inc(off_done, 1)

            def to_state(blk):
                rows = slice(Q * blk, Q * blk + Q)
                xd = x_dec[rows].rearrange("t h p -> t (h p)")
                for k in range(4):
                    mm = nc.tensor.matmul(ps_turn[:, k * P:(k + 1) * P], b_tok[rows, k * P:(k + 1) * P],
                                          xd[:, k * P:(k + 1) * P], start=True, stop=True)
                mm.then_inc(st_done, 1)

            run(pe, body)

        @block.scalar
        def _(act):
            act.wait_ge(init, 6)

            def body(i):
                for m in range(16 if not (isinstance(i, int) and i == 8) else 4):
                    q, s = m // 4, m % 4
                    n = 16 * i + m
                    c = 4 * i + q
                    if inside(i, 16, m + 1, 128):
                        act.wait_ge(decay_done, n + 2)
                        wait(act, diag_done, n)
                        nc.scalar.activation(decay[:, (m + 1) % 2], ps_decay[:], ACT.Exp).then_inc(exp_done, 1)
                    if inside(i, 16, m + 9, 128) and (m + 9) % 8 < 6:
                        g, p, slot = pair(i, m - 2)
                        conv = 6 * g + p
                        act.wait_ge(taps, 6 * (conv + 1))
                        wait(act, final, n + 9)
                        nc.scalar.activation(th[:], xbc[:, slot, 2 * p:2 * p + 2, :], ACT.Tanh).then_inc(th_ready, 1)
                    if inside(i, 16, m + 11, 128):
                        g, p, slot = pair(i, m)
                        act.wait_ge(proj_done, n + 12)
                        if p < 6:
                            if p == 0:
                                act.wait_ge(halo_ready, g + 1)
                                wait(act, off_done, 2 * (2 * g - 2))
                            nc.scalar.activation(raw[:, 2 * p:2 * p + 2, 3:], ps_proj[:], ACT.Copy)
                            for t in range(2):
                                j = 2 * p + t
                                mm = nc.scalar.activation(xbc[:, slot, j, :], ps_proj[:, t], ACT.Identity,
                                                          bias=conv_b[:, j:j + 1], scale=conv_w[:, j, 3:4])
                            mm.then_inc(raw_ready, 1)
                        else:
                            wait(act, final, n + 4)
                            wait(act, gated, 2 * g - 2)
                            for t in range(2):
                                j = 2 * (p - 6) + t
                                nc.scalar.activation(zt[:, p % 2, t], ps_proj[:, t], ACT.Tanh, bias=z_b[:, j:j + 1], scale=0.5)
                                mm = nc.scalar.activation(gate[:, slot, j], ps_proj[:, t], ACT.Identity,
                                                          bias=z_b[:, j:j + 1], scale=0.5)
                            mm.then_inc(raw_ready, 1)
                    if inside(i, 4, q + 1, CHUNKS):
                        sl = (q + 1) % 2
                        if s == 0:
                            act.wait_ge(sums_done, c + 2)
                            wait(act, off_read, c)
                            nc.scalar.activation(sums[:, sl].rearrange("p a h -> p (a h)"), ps_misc[:, 0:4 * H],
                                                 ACT.Exp).then_inc(sums_ready, 1)
                            act.wait_ge(xt_done, c + 2)
                            wait(act, diag_done, 4 * c)
                            for blk in range(2):
                                rows = slice(Q * blk, Q * blk + Q)
                                nc.scalar.activation(x_blocks[rows, sl, :, blk, :],
                                                     ps_turn[rows].rearrange("t (h p) -> t h p", p=HP), ACT.Copy)\
                                    .then_inc(blocks_ready, 1)
                        if s == 1:
                            act.wait_ge(bt_done, c + 2)
                            wait(act, st_done, 2 * (c + 1))
                            nc.scalar.activation(b_tok[:], ps_turn[:], ACT.Copy).then_inc(btok_ready, 1)
                        if s in (1, 2):
                            odd = s - 1
                            act.wait_ge(cb_done, 2 * c + 3 + odd)
                            wait(act, g_ready, 4 * c)
                            nc.scalar.activation(cb[:, sl].rearrange("z (k a) s -> z k a s", a=2)[:, :, odd],
                                                 ps_misc[:, odd * 256:odd * 256 + 256].rearrange("z (k s) -> z k s", k=4),
                                                 ACT.Copy).then_inc(cb_ready, 1)
                    if inside(i, 4, q - 1, CHUNKS) and s == 0:
                        act.wait_ge(gated, c)
                        wait(act, out_done, c - 1)
                        nc.scalar.activation(yg_hi[:], yg[:], ACT.Copy).then_inc(yg_hi_ready, 1)
                    if (m + 13) % 8 == 0 and inside(i, 2, (m + 13) // 8, 16):
                        g = 2 * i + (m + 13) // 8
                        act.wait_ge(x_in, 16 * (g + 1))
                        wait(act, proj_done, 8 * (g - 1))
                        nc.scalar.activation(x_hi[:, ((m + 13) // 8) % 2], x_raw[:], ACT.Copy).then_inc(x_hi_ready, 1)

            run(act, body)

        @block.gpsimd
        def _(pool):
            def body(i):
                for m in range(16 if not (isinstance(i, int) and i == 8) else 4):
                    q, s = m // 4, m % 4
                    n = 16 * i + m
                    c = 4 * i + q
                    if inside(i, 16, m + 1, 128):
                        sc, sq = (m + 1) // 4, (m + 1) % 4
                        pool.wait_ge(exp_done, n + 2)
                        pool.wait_ge(cb_ready, 2 * (4 * i + sc) + 2)
                        d4 = decay[:, (m + 1) % 2].rearrange("z g (h s) -> z g h s", s=Q)
                        for t in range(2):
                            g = 2 * sq + t
                            mm = nc.gpsimd.tensor_tensor(d4[:, t], d4[:, t],
                                                         cb[:, sc % 2, g:g + 1, :].broadcast_to([P, 8, Q]), ALU.mult)
                        mm.then_inc(g_ready, 1)
                    if inside(i, 4, q + 1, CHUNKS) and s == 3:
                        sl = (q + 1) % 2
                        pool.wait_ge(off_read, c + 2)
                        pool.wait_ge(du_ready, c + 2)
                        nc.gpsimd.tensor_tensor(y[:, sl], y[:, sl], tmp[:], ALU.add).then_inc(y_ready, 1)

            run(pool, body)

        @block.vector
        def _(v):
            nc.vector.memset(state[:], 0.0).then_inc(reset_ready, 1)
            nc.vector.memset(x_blocks[:], 0.0).then_inc(init, 6)
            nc.vector.memset(raw[:, :, 0:3], 0.0).then_inc(halo_ready, 1)

            def body(i):
                for m in range(16 if not (isinstance(i, int) and i == 8) else 4):
                    q, s = m // 4, m % 4
                    n = 16 * i + m
                    c = 4 * i + q
                    if inside(i, 4, q - 1, CHUNKS) and s == 0:
                        v.wait_ge(diag_done, n)
                        assemble((q - 1) % 2, 1)
                    if inside(i, 4, q - 1, CHUNKS) and s == 1:
                        v.wait_ge(yg_hi_ready, c)
                        wait(v, out_done, c - 1)
                        nc.vector.tensor_tensor(yg_lo[:], yg[:], yg_hi[:].bitcast(F32), ALU.subtract).then_inc(yg_lo_ready, 1)
                    if inside(i, 16, m + 10, 128):
                        g, p, slot = pair(i, m - 1)
                        if p < 6:
                            base = 6 * (6 * g + p)
                            v.wait_ge(raw_ready, n + 11)
                            for k in range(1, 4):
                                for t in range(2):
                                    j = 2 * p + t
                                    to = xbc[:, slot, j, :]
                                    if k > 1:
                                        v.wait_ge(taps, base + 2 * (k - 2) + t + 1)
                                    nc.vector.scalar_tensor_tensor(to, raw[:, j, 3 - k:3 - k + GROUP], conv_w[:, j, 3 - k:4 - k],
                                                                   to, ALU.mult, ALU.add).then_inc(taps, 1)
                            if p == 5:
                                v.wait_ge(taps, base + 6)
                                if (m + 10) // 8 % 2 == 1:
                                    kr = keep_rows[:, bass.ds(i + ((m + 10) // 8 + 1) // 2, 1)]
                                    nc.vector.tensor_scalar(raw[:, :, 0:3], raw[:, :, GROUP:], kr, None, ALU.mult).then_inc(halo_ready, 1)
                                else:
                                    nc.vector.tensor_copy(raw[:, :, 0:3], raw[:, :, GROUP:]).then_inc(halo_ready, 1)
                    if inside(i, 16, m + 9, 128):
                        g, p, slot = pair(i, m - 2)
                        if p < 6:
                            v.wait_ge(th_ready, 6 * g + p + 1)
                            to, by = xbc[:, slot, 2 * p:2 * p + 2, :], th[:]
                        else:
                            v.wait_ge(raw_ready, n + 10)
                            to, by = gate[:, slot, 2 * (p - 6):2 * (p - 6) + 2, :], zt[:, p % 2]
                        nc.vector.scalar_tensor_tensor(to, by, 1.0, to, ALU.add, ALU.mult).then_inc(final, 1)
                    if inside(i, 4, q - 1, CHUNKS) and s == 2:
                        v.wait_ge(out_done, c)
                        v.wait_ge(res_in[(q - 1) % 2], 16 * ((4 * i + q - 1) // 2 + 1) if isinstance(i, int)
                                  else 16 * (2 * i + (q - 1) // 2 + 1))
                        residual = x_res[:, (q - 1) % 2]
                        row = u[:, CHUNKS - 1] if isinstance(i, int) and 4 * i + q - 1 == CHUNKS - 1 else residual
                        nc.vector.tensor_tensor(row[:, 0:D], ps_diag[:, 1, 0:D], residual[:, 0:D], ALU.add).then_inc(res_done, 1)
                        v.wait_ge(res_done, c)
                        nc.vector.bn_stats(bn[:], row[:, 0:D]).then_inc(bn_done, 1)
                        v.wait_ge(bn_done, c)
                        nc.vector.tensor_copy(bn_copy[:], bn[:, 0:1])
                        nc.vector.bn_aggr(row[:, D:ROW], bn[:]).then_inc(stat_done, 1)
                    if inside(i, 4, q + 1, CHUNKS):
                        sl = (q + 1) % 2
                        turned = ps_turn[:].rearrange("t (h p) -> t h p", p=HP)
                        if s == 0:
                            v.wait_ge(sums_ready, c + 2)
                            v.wait_ge(blocks_ready, 2 * (c + 1) + 2)
                            wait(v, st_done, 2 * (c + 1))
                            nc.vector.tensor_tensor(x_dec[:], turned, sums[:, sl, 1, :, None].broadcast_to([P, H, HP]),
                                                    ALU.mult).then_inc(xdec_ready, 1)
                            wait(v, yt_done, c)
                            nc.vector.tensor_tensor(y[:, sl], turned, steps[:, sl, 1, :, None].broadcast_to([P, H, HP]),
                                                    ALU.mult).then_inc(du_ready, 1)
                        if s >= 2:
                            blk = s - 2
                            base = 8 * (c + 1) + 4 * blk
                            v.wait_ge(off_done, 2 * (c + 1) + blk + 1)
                            for a in range(2):
                                rows = slice(64 * a, 64 * a + 64)
                                st = state[rows, :, a, :].rearrange("n k (h p) -> n k h p", p=HP)
                                el = sums[rows, sl, 2 + blk, :].rearrange("n (k a h) -> n k a h", k=4, a=2)[:, :, a, :, None]
                                nc.vector.tensor_tensor(st, st, el.broadcast_to([64, 4, 8, HP]), ALU.mult).then_inc(state_ready, 1)
                            v.wait_ge(st_done, 2 * (c + 1) + blk + 1)
                            for a in range(2):
                                rows = slice(64 * a, 64 * a + 64)
                                v.wait_ge(state_ready, base + a + 1)
                                new = ps_turn[rows].rearrange("n (k a c) -> n k a c", k=4, a=2)[:, :, a]
                                nc.vector.tensor_tensor(state[rows, :, a, :], state[rows, :, a, :], new, ALU.add).then_inc(state_ready, 1)
                            if blk == 1:
                                if q == 2:
                                    v.wait_ge(state_ready, base + 4)
                                    kr = keep_rows[:, bass.ds(i + 1, 1)]
                                    st = state[:].rearrange("n k a c -> n (k a c)")
                                    nc.vector.tensor_scalar(st, st, kr, None, ALU.mult).then_inc(reset_ready, 1)
                                wait(v, y_ready, c + 1)
                                nc.vector.tensor_tensor(tmp[:], ps_off[:], sums[:, sl, 0, :, None].broadcast_to([P, H, HP]),
                                                        ALU.mult).then_inc(off_read, 1)
                    if inside(i, 4, q, CHUNKS) and s == 2:
                        v.wait_ge(diag_done, n)
                        v.wait_ge(y_ready, c + 1)
                        assemble(q % 2, 0)
                    if inside(i, 4, q - 1, CHUNKS):
                        if s == 0:
                            slot, t0 = in_group(q - 1)
                            v.wait_ge(final, 8 * (2 * i + (q - 1) // 2) + 8)
                            v.wait_ge(yt_done, c)
                            wait(v, yg_lo_ready, c - 1)
                            wait(v, yg_hi_ready, c - 1)
                            nc.vector.tensor_tensor(yg[:], ps_diag[:, 1].rearrange("p (k t) -> p k t", k=4),
                                                    gate[:, slot, :, t0:t0 + P], ALU.mult).then_inc(gated, 1)
                    if (m + 13) % 8 == 0 and inside(i, 2, (m + 13) // 8, 16):
                        g = 2 * i + (m + 13) // 8
                        k = ((m + 13) // 8) % 2
                        v.wait_ge(x_hi_ready, g + 1)
                        nc.vector.tensor_tensor(x_lo[:, k], x_raw[:], x_hi[:, k].bitcast(F32), ALU.subtract).then_inc(x_lo_ready, 1)

            def assemble(slot, half):
                pairs = ps_diag[:, half].rearrange("r (k a b p) -> r k a b p", k=16, a=2, b=2)
                yh = y[:, slot].rearrange("t (f k a) p -> t f k a p", f=2, a=2)[:, half]
                for blk in range(2):
                    for a in range(2):
                        to = yh[Q * blk:Q * blk + Q, :, a, :]
                        nc.vector.tensor_tensor(to, to, pairs[Q * a:Q * a + Q, :, a, blk, :], ALU.add).then_inc(assembled, 1)

            run(v, body)
            v.wait_ge(stat_done, CHUNKS)


HIDDEN, FT = 704, 6
NG = TOKENS // 512


def run_groups(engine, body):
    body(0, 0)
    body(0, 1)
    with engine.Fori(1, NG // 2 - 1) as i:
        body(i, 0)
        body(i, 1)
    body(NG // 2 - 1, 0)
    body(NG // 2 - 1, 1)
    body(NG // 2, 0)


class Normalizer:

    def __init__(self, nc, b, u):
        self.nc, self.u = nc, u
        self.var, self.scale, self.t = (b.sb(f"norm_{n}", [P, CHUNKS]) for n in ("var", "scale", "t"))
        self.chain = b.sem("norm_chain")

    def scales(self, v):
        nc = self.nc
        link = Chain(v, self.chain)
        link(nc.vector.tensor_scalar(self.var[:], self.u[:, :, D + 1], LN_EPS, None, ALU.add))
        inverse_deviation(nc, link, self.var[:], self.scale[:], self.t[:])

    def rows(self, out, c):
        one = lambda t: t.rearrange("p c d -> p (c d)")
        row = self.u[:, bass.ds(c, 1)]
        return self.nc.vector.tensor_scalar(out, one(row[:, :, 0:D]), one(row[:, :, D:D + 1]),
                                            self.scale[:, bass.ds(c, 1)], ALU.subtract, ALU.mult)


def ffn_phase(nc, ins, u):
    with ExitStack() as ctx:
        b = Buffers(nc, ctx, "ffn")
        ident, ones = b.sb("ident", [P, P]), b.sb("ones", [P, P])
        w_raw = b.sb("w_raw", [P, 3, KD * FT * P])
        w_q = b.sb("w_q", [P, 3, KD * FT * P], F32R)
        below = b.sb("below", [P, KD * FT * P])
        mags, limit, neg_limit = b.sb("mags", [P, 3]), b.sb("limit", [P, 3]), b.sb("neg_limit", [P, 3])
        norm = Normalizer(nc, b, u)
        xn = b.sb("xn", [P, 2, 4, D])
        x_hi, x_lo = b.sb("x_hi", [P, 2, KD, 512], F32R), b.sb("x_lo", [P, 2, KD, 512], F32R)
        sig, h = b.sb("sig", [P, 2, 512]), b.sb("h", [P, 2, 512])
        h_hi, h_lo = b.sb("h_hi", [P, 2, FT, 512], F32R), b.sb("h_lo", [P, 2, FT, 512], F32R)
        row = b.sb("row", [P, 4, ROW])
        bn, bn_copy = b.sb("bn", [P, 6]), b.sb("bn_copy", [P, 1])
        ps_gate, ps_up = b.ps("ps_gate", [P, 2, 512]), b.ps("ps_up", [P, 2, 512])
        ps_turn, ps_out = b.ps("ps_turn", [P, KD, 512]), b.ps("ps_out", [P, 2, 512])
        (ident_in, mags_ready, mags_done, quantized, xn_ready, turned, x_hi_ready, x_lo_ready, up_done, sig_ready, h_ready,
         h_hi_ready, h_lo_ready, out_done, res_done, bn_done, stat_done) = (b.sem(n) for n in (
            "ident_in mags_ready mags_done quantized xn_ready turned x_hi_ready x_lo_ready up_done sig_ready h_ready "
            "h_hi_ready h_lo_ready out_done res_done bn_done stat_done").split())
        kept = [b.sem(f"kept{c}") for c in range(4)]
        w_in = [b.sem(f"w{k + 1}_in") for k in range(3)]
        w1, w2 = (w_q[:, k].rearrange("p (k c) -> p k c", k=KD) for k in range(2))
        w3 = w_q[:, 2].rearrange("p (f c) -> p f c", f=FT)
        ctx.callback(b.clear)
        block = ctx.enter_context(nc.Block())

        def exists(i, k):
            return tuple(inside(i, 2, k + d, NG) for d in (-1, 0, 1))

        def last(i, k):
            return isinstance(i, int) and 2 * i + k == NG

        @block.sync
        def _(sp):
            sp.dma_start(ident[:], ins["identity"]).then_inc(ident_in, 16)
            sp.dma_start(w_raw[:, 0].rearrange("p (k c) -> p k c", k=KD), ins["w1T"].rearrange("(k p) c -> p k c", p=P))\
                .then_inc(w_in[0], 16)

            def body(i, k):
                if exists(i, k)[0] and not last(i, k):
                    for c in range(4):
                        ci = 8 * i + 4 * k - 4 + c
                        sp.wait_ge(stat_done, ci + 1)
                        sp.dma_start(u[:, bass.ds(ci, 1), :], row[:, c, None, :]).then_inc(kept[c], 16)

            run_groups(sp, body)
            for c in range(4):
                sp.wait_ge(kept[c], 16 * (NG - 1))

        @block.tensor
        def _(pe):
            def turn(g, slot):
                pe.wait_ge(xn_ready, 4 * g + 4)
                wait(pe, x_lo_ready, g)
                for c in range(4):
                    for k in range(KD):
                        m = nc.tensor.transpose(ps_turn[:, k, c * P:(c + 1) * P], xn[:, slot, c, k * P:(k + 1) * P], ident[:])
                m.then_inc(turned, 1)

            def body(i, k):
                prev, cur, nxt = exists(i, k)
                g = 2 * i + k
                begins = isinstance(i, int) and i == 0 and k == 0
                for f in range(FT):
                    if cur:
                        if f == 0:
                            pe.wait_ge(x_lo_ready, g + 1)
                        wait(pe, h_ready, FT * g + f - 1)
                        cols = slice(f * P, (f + 1) * P)
                        for j, (w, out) in enumerate(((w1, ps_gate), (w2, ps_up))):
                            if begins and f == 0:
                                pe.wait_ge(quantized, 2 * (j + 1))
                            for d in range(KD):
                                nc.tensor.matmul(out[:, f % 2], w[:, d, cols], x_hi[:, k, d], start=(d == 0), stop=False)
                                m = nc.tensor.matmul(out[:, f % 2], w[:, d, cols], x_lo[:, k, d], start=False, stop=(d == KD - 1))
                        m.then_inc(up_done, 1)
                    if prev and f == 1:
                        ps = (k + 1) % 2
                        pe.wait_ge(h_lo_ready, FT * g)
                        if isinstance(i, int) and i == 0:
                            pe.wait_ge(quantized, 6)
                        for c in range(4):
                            wait(pe, res_done, 4 * (g - 1) + c - 1)
                            toks = slice(c * P, (c + 1) * P)
                            for j in range(FT):
                                nc.tensor.matmul(ps_out[:, c % 2, 0:D], h_hi[:, ps, j, toks], w3[:, j], start=(j == 0), stop=False)
                                m = nc.tensor.matmul(ps_out[:, c % 2, 0:D], h_lo[:, ps, j, toks], w3[:, j], start=False, stop=(j == FT - 1))
                            m.then_inc(out_done, 1)
                    if nxt and cur and f == 3:
                        turn(g + 1, (k + 1) % 2)

            pe.wait_ge(ident_in, 16)
            turn(0, 0)
            pe.wait_ge(mags_ready, 4)
            nc.tensor.matmul(ps_out[:, 0, 0:3], ones[:], mags[:], start=True, stop=True).then_inc(mags_done, 1)
            run_groups(pe, body)

        @block.scalar
        def _(act):
            act.dma_start(w_raw[:, 1].rearrange("p (k c) -> p k c", k=KD), ins["w2T"].rearrange("(k p) c -> p k c", p=P))\
                .then_inc(w_in[1], 16)
            act.dma_start(w_raw[:, 2].rearrange("p (f c) -> p f c", f=FT), ins["w3T"].rearrange("(f p) c -> p f c", p=P))\
                .then_inc(w_in[2], 16)

            def high(g, slot):
                act.wait_ge(turned, g + 1)
                nc.scalar.activation(x_hi[:, slot], ps_turn[:], ACT.Copy).then_inc(x_hi_ready, 1)

            def h_high(g, slot, f):
                act.wait_ge(h_ready, FT * g + f + 1)
                if f == 0:
                    wait(act, out_done, 4 * (g - 1))
                nc.scalar.activation(h_hi[:, slot, f], h[:, f % 2], ACT.Copy).then_inc(h_hi_ready, 1)

            def body(i, k):
                prev, cur, nxt = exists(i, k)
                g = 2 * i + k
                for f in range(FT):
                    if nxt and cur and f == 4:
                        high(g + 1, (k + 1) % 2)
                    if cur:
                        act.wait_ge(up_done, FT * g + f + 1)
                        wait(act, h_ready, FT * g + f - 1)
                        nc.scalar.activation(sig[:, f % 2], ps_gate[:, f % 2], ACT.Sigmoid).then_inc(sig_ready, 1)
                        if f:
                            h_high(g, k, f - 1)
                    if prev and f == 0:
                        h_high(g - 1, (k + 1) % 2, FT - 1)

            high(0, 0)
            run_groups(act, body)

        @block.vector
        def _(v):
            norm.scales(v)

            def rows(g, slot):
                for c in range(4):
                    if c == 0:
                        wait(v, turned, g - 1)
                        wait(v, res_done, 4 * (g - 1))
                    norm.rows(xn[:, slot, c], 4 * g + c).then_inc(xn_ready, 1)

            def low(g, slot):
                v.wait_ge(x_hi_ready, g + 1)
                nc.vector.tensor_tensor(x_lo[:, slot], ps_turn[:], x_hi[:, slot].bitcast(F32), ALU.subtract).then_inc(x_lo_ready, 1)

            rows(0, 0)
            nc.vector.memset(ones[:], 1.0).then_inc(mags_ready, 1)
            for k in range(3):
                v.wait_ge(w_in[k], 16)
                nc.vector.tensor_reduce(mags[:, k:k + 1], w_raw[:, k], AX.X, ALU.add, apply_absolute_value=True).then_inc(mags_ready, 1)
            low(0, 0)
            v.wait_ge(mags_done, 1)
            for t, sign in ((limit, 0.5), (neg_limit, -0.5)):
                nc.vector.tensor_scalar(t[:], ps_out[:, 0, 0:3], sign / (HIDDEN * D), sign * 1e-8, ALU.mult, ALU.add).then_inc(mags_ready, 1)
            v.wait_ge(mags_ready, 6)
            for k in range(3):
                wait(v, quantized, 2 * k)
                nc.vector.tensor_scalar(below[:], w_raw[:, k], neg_limit[:, k:k + 1], None, ALU.is_lt).then_inc(quantized, 1)
                v.wait_ge(quantized, 2 * k + 1)
                nc.vector.scalar_tensor_tensor(w_q[:, k], w_raw[:, k], limit[:, k:k + 1], below[:],
                                               ALU.is_gt, ALU.subtract).then_inc(quantized, 1)

            def h_low(g, slot, f):
                v.wait_ge(h_hi_ready, FT * g + f + 1)
                nc.vector.tensor_tensor(h_lo[:, slot, f], h[:, f % 2], h_hi[:, slot, f].bitcast(F32), ALU.subtract).then_inc(h_lo_ready, 1)

            def body(i, k):
                prev, cur, nxt = exists(i, k)
                g = 2 * i + k
                ps = (k + 1) % 2
                for f in range(FT):
                    if cur:
                        if nxt and f == 2:
                            rows(g + 1, ps)
                        if nxt and f == 4:
                            low(g + 1, ps)
                        v.wait_ge(sig_ready, FT * g + f + 1)
                        wait(v, h_lo_ready, FT * g + f - 1)
                        nc.vector.tensor_tensor(h[:, f % 2], ps_up[:, f % 2], sig[:, f % 2], ALU.mult).then_inc(h_ready, 1)
                        if f:
                            h_low(g, k, f - 1)
                    if prev and f == 0:
                        h_low(g - 1, ps, FT - 1)
                    if prev and f == 1:
                        for c in range(4):
                            ci = 8 * i + 4 * k - 4 + c
                            v.wait_ge(out_done, ci + 1)
                            wait(v, kept[c], 16 * (g - 1))
                            to = u[:, ci] if last(i, k) else row[:, c]
                            nc.vector.tensor_tensor(to[:, 0:D], ps_out[:, c % 2, 0:D], xn[:, ps, c], ALU.add).then_inc(res_done, 1)
                            v.wait_ge(res_done, ci + 1)
                            nc.vector.bn_stats(bn[:], to[:, 0:D]).then_inc(bn_done, 1)
                            v.wait_ge(bn_done, ci + 1)
                            nc.vector.tensor_copy(bn_copy[:], bn[:, 0:1])
                            nc.vector.bn_aggr(to[:, D:ROW], bn[:]).then_inc(stat_done, 1)

            run_groups(v, body)


NH, HD, NM = 16, 16, 4
VW = HD + 1
ATT_EPS = 1e-6


def attention_phase(nc, ins, u):
    with ExitStack() as ctx:
        b = Buffers(nc, ctx, "att")
        ctx.callback(b.clear)
        kept = {
            "phi_q": b.sb("phi_q", [P, NG, 2, 512]),
            "local": b.sb("local", [P, CHUNKS, D]),
            "q_sums": b.sb("q_sums", [P, NG, 2]),
            "w_hi": b.sb("w_hi", [P, KD, D], F32R), "w_lo": b.sb("w_lo", [P, KD, D], F32R),
            "mem": b.sb("mem", [P, 2, NM + 1, 8 * VW]),
            "coef": b.sb("coef", [P, NG // 2, NM + 1, NH]),
            "head_gate": b.sb("head_gate", [P, NH]),
            "local_gate": b.sb("local_gate", [P, NH]),
            "gate_raw": b.sb("gate_raw", [P, NH]), "ident": b.sb("ident", [P, P]),
            "eg_w1": b.sb("eg_w1", [P, KD, 64]), "eg_b1": b.sb("eg_b1", [64, 1]),
            "eg_w2": b.sb("eg_w2", [64, 1]), "eg_b2": b.sb("eg_b2", [P, 1]),
            "offset": b.sb("offset", [P, CHUNKS]),
        }
        norm = Normalizer(nc, b, u)
        causal_pass(nc, ins, u, norm, kept)
        memory_weights(nc, ins, u, norm, kept)
        memory_pass(nc, ins, u, norm, kept)


def causal_pass(nc, ins, u, norm, kept):
    with ExitStack() as ctx:
        b = Buffers(nc, ctx, "causal")
        ident = b.sb("ident", [P, P])
        mask = b.sb("mask", [P, Q])
        head_blocks = b.sb("head_blocks", [P, 2, 8 * VW])
        parity = b.sb("parity", [P, 2])
        keep_rows = b.sb("keep_rows", [P, NG // 2 + 1])
        w_raw = b.sb("w_raw", [P, 4, KD, D])
        w_hi, w_lo = b.sb("w_hi", [P, KD, 3 * D], F32R), b.sb("w_lo", [P, KD, 3 * D], F32R)
        xn = b.sb("xn", [P, 4, D])
        x_hi, x_lo = b.sb("x_hi", [P, 2, KD, 512], F32R), b.sb("x_lo", [P, 2, KD, 512], F32R)
        e, r = (w_raw[:, 2 * k:2 * k + 2].rearrange("p t k c -> p t (k c)") for k in range(2))
        pq, pk = b.sb("pq", [P, 2, 2, 512]), b.sb("pk", [P, 2, 2, 512])
        pq_half = b.sb("pq_half", [P, 2, 2, 2, 512])
        ek, rk = b.sb("ek", [P, D]), b.sb("rk", [P, D])
        k_tok = b.sb("k_tok", [P, 2, D])
        v_blocks = b.sb("v_blocks", [P, 2, NH, 2, VW])
        sc = b.sb("sc", [P, 2, 4, 2, 2, Q])
        acc = b.sb("acc", [P, 2, 2 * 8 * VW])
        state = b.sb("state", [P, 2, 2, 2, 4, 2, VW])
        den, zero = b.sb("den", [P, NH]), b.sb("zero", [P, 2])
        red = b.sb("red", [P, 2])
        ps_turn, ps_proj = b.ps("ps_turn", [P, 512]), b.ps("ps_proj", [P, 512])
        ps_sc = b.ps("ps_sc", [P, 4, 512])
        ps_num, ps_state = b.ps("ps_num", [P, 512]), b.ps("ps_state", [P, 512])
        (const_in, mem_in, w_ready, w_lo_ready, zeroed, xn_ready, turned, x_hi_ready, x_lo_ready, kv_done, kv_read, k_ready, qk_done,
         qk_read, phi_ready, half_ready, sc_done, sc_ready, num_done, num_read, den_ready, st_done, acc_ready, start_ready, mid_ready, reset_ready,
         red_ready, sum_kept) = (b.sem(n) for n in (
            "const_in mem_in w_ready w_lo_ready zeroed xn_ready turned x_hi_ready x_lo_ready kv_done kv_read k_ready qk_done "
            "qk_read phi_ready half_ready sc_done sc_ready num_done num_read den_ready st_done acc_ready start_ready mid_ready reset_ready "
            "red_ready sum_kept").split())
        w_in = [b.sem(f"w_in{k}") for k in range(2)]
        phi_kept = [b.sem(f"phi_kept{k}") for k in range(2)]
        ctx.callback(b.clear)
        block = ctx.enter_context(nc.Block())

        def run(engine, body):
            body(-1)
            body(0)
            with engine.Fori(1, NG // 2 - 1) as i:
                body(i)
            body(NG // 2 - 1)

        def next_group(i, j):
            k = j // 4 + 1
            return (2 * i + k, k % 2) if inside(i, 2, k, NG) else (None, None)

        @block.sync
        def _(sp):
            for t, name in ((ident, "identity"), (mask, "upper_ones"), (head_blocks, "head_blocks"), (parity, "parity"),
                            (keep_rows, "keep_batches")):
                sp.dma_start(t[:], ins[name]).then_inc(const_in, 16)
            sp.dma_start(kept["mem"][:, :, 1:], ins["mem_blocks"]).then_inc(mem_in, 16)
            sp.dma_start(kept["gate_raw"][:], ins["gate_rows"]).then_inc(mem_in, 16)

            def body(i):
                for j in (1, 5):
                    g, slot = next_group(i, j)
                    if g is not None:
                        sp.wait_ge(phi_ready, 4 * g + 2)
                        sp.dma_start(kept["phi_q"][:, bass.ds(g, 1)], pq[:, slot:slot + 1]).then_inc(phi_kept[slot], 16)

            run(sp, body)
            sp.wait_ge(mem_in, 32)
            for k in range(2):
                sp.wait_ge(phi_kept[k], 16 * NG // 2)

        @block.tensor
        def _(pe):
            pe.wait_ge(const_in, 80)

            def project(out, w0, w1, g_slot, toks=None):
                for k in range(KD):
                    w = (w_hi[:, k, w0:w1], w_lo[:, k, w0:w1])
                    if toks is None:
                        m = product3(nc, out, *w, x_hi[:, g_slot, k], x_lo[:, g_slot, k], k == 0, k == KD - 1)
                    else:
                        m = product3(nc, out, x_hi[:, g_slot, k, toks], x_lo[:, g_slot, k, toks], *w, k == 0, k == KD - 1)
                return m

            def half_of_next(i, j, h):
                g, slot = next_group(i, j)
                ci, c = 8 * i + j, j % 4
                if g is None or c == 3:
                    return
                if c == 0:
                    wait(pe, x_lo_ready, 2 * g)
                    if h == 0:
                        pe.wait_ge(xn_ready, 4 * g + 4)
                        wait(pe, acc_ready, 2 * (ci + 1))
                    elif inside(i, 8, j + 1, CHUNKS):
                        wait(pe, kv_read, ci + 2)
                    for t in range(4):
                        m = nc.tensor.transpose((ps_turn, ps_proj)[h][:, t * P:(t + 1) * P], xn[:, t, h * P:(h + 1) * P], ident[:])
                    m.then_inc(turned, 1)
                else:
                    if inside(i, 8, j + 1, CHUNKS):
                        wait(pe, kv_read, ci + 2)
                    pe.wait_ge(x_lo_ready, 2 * g + 2)
                    wait(pe, qk_read, 4 * g + 2 * (c - 1) + h)
                    if isinstance(i, int) and i == -1:
                        pe.wait_ge(w_lo_ready, c)
                    w0 = (c - 1) * D + h * P
                    project(ps_proj[:], w0, w0 + P, slot).then_inc(qk_done, 1)

            def body(i):
                for j in range(8):
                    ci, c = 8 * i + j, j % 4
                    g, slot = next_group(i, j)
                    nxt = ((j + 1) // 4) % 2
                    toks = slice(((j + 1) % 4) * P, ((j + 1) % 4 + 1) * P)
                    if inside(i, 8, j + 1, CHUNKS):
                        wait(pe, kv_read, ci + 1)
                        if c == 1 and g is not None:
                            pe.wait_ge(x_lo_ready, 2 * g + 2)
                        begun = 0 if next_group(i, j)[0] is None else (0, 0, 2, 4)[c]
                        wait(pe, qk_read, 4 * (2 * i + j // 4) + 4 + begun)
                        if isinstance(i, int) and i == -1:
                            pe.wait_ge(w_lo_ready, 3)
                        project(ps_proj[:], D, 3 * D, nxt, toks).then_inc(kv_done, 1)
                    if inside(i, 8, j + 1, CHUNKS):
                        gn = 2 * i + (j + 1) // 4
                        pe.wait_ge(half_ready, 4 * gn + 4)
                        pe.wait_ge(phi_ready, 4 * gn + 4)
                        wait(pe, sc_ready, 4 * (ci + 1))
                        for t in range(2):
                            for blk in range(2):
                                for rt in range(4):
                                    rows = slice(32 * rt, 32 * rt + 32)
                                    ts = slice(toks.start + Q * blk, toks.start + Q * blk + Q)
                                    m = nc.tensor.matmul(ps_sc[Q * blk:Q * blk + Q, rt, t * P:(t + 1) * P], pk[rows, nxt, t, ts],
                                                         pq_half[rows, nxt, t, :, ts], start=True, stop=True,
                                                         tile_position=(32 * rt, Q * blk))
                        m.then_inc(sc_done, 1)
                    half_of_next(i, j, 0)
                    if c == 0:
                        half_of_next(i, j, 1)
                    if inside(i, 8, j, CHUNKS):
                        now = (j // 4) % 2
                        wait(pe, num_read, 4 * ci)
                        wait(pe, start_ready, ci + 1)
                        wait(pe, mid_ready, ci + 1)
                        num = ps_num[:, 0:NH * VW].rearrange("q (k b e) -> q k b e", b=2, e=VW)
                        for t in range(2):
                            for blk in range(2):
                                for par in range(2):
                                    ts = slice(c * P + Q * blk, c * P + Q * blk + Q)
                                    nc.tensor.matmul(num[Q * par:Q * par + Q, 4 * t:4 * t + 4, blk], pq[:, now, t, ts],
                                                     state[:, j % 2, blk, t, :, par], start=(t == 0 and blk == 0), stop=False,
                                                     skip_group_check=True)
                        pe.wait_ge(sc_ready, 4 * (ci + 1))
                        for h in range(NH):
                            t, rt, par = h // 8, (h % 8) // 2, h % 2
                            m = nc.tensor.matmul(num[Q * par:Q * par + Q, h // 2].rearrange("q b e -> q (b e)"), sc[:, j % 2, rt, t, par],
                                                 v_blocks[:, j % 2, h].rearrange("j b e -> j (b e)"),
                                                 start=False, stop=(h >= NH - 2), skip_group_check=True)
                        m.then_inc(num_done, 1)
                    if c > 0:
                        half_of_next(i, j, 1)
                    if inside(i, 8, j + 1, CHUNKS):
                        pe.wait_ge(k_ready, ci + 2)
                        pe.wait_ge(kv_read, ci + 2)
                        wait(pe, acc_ready, 2 * (ci + 1))
                        if g is not None and c == 0:
                            pe.wait_ge(x_lo_ready, 2 * g + 1)
                        for blk, out in enumerate((ps_state, ps_turn)):
                            rows = slice(Q * blk, Q * blk + Q)
                            for t in range(2):
                                m = nc.tensor.matmul(out[:, t * 8 * VW:(t + 1) * 8 * VW], k_tok[rows, (j + 1) % 2, t * P:(t + 1) * P],
                                                     v_blocks[rows, (j + 1) % 2, 8 * t:8 * t + 8, blk], start=True, stop=True)
                            m.then_inc(st_done, 1)

            run(pe, body)

        @block.scalar
        def _(act):
            for k, name in enumerate(("wqT", "wkT", "wvT", "woT")):
                act.dma_start(w_raw[:, k], ins[name].rearrange("(k p) c -> p k c", p=P)).then_inc(w_in[k // 2], 16)
            act.wait_ge(w_in[0], 32)
            for k in range(3):
                if k == 2:
                    act.wait_ge(w_in[1], 32)
                nc.scalar.activation(w_hi[:, :, k * D:(k + 1) * D], w_raw[:, k], ACT.Copy).then_inc(w_ready, 1)
            nc.scalar.activation(kept["w_hi"][:], w_raw[:, 3], ACT.Copy).then_inc(w_ready, 1)
            act.wait_ge(zeroed, 5)

            def body(i):
                for j in range(8):
                    ci, c = 8 * i + j, j % 4
                    if inside(i, 8, j + 1, CHUNKS):
                        act.wait_ge(kv_done, ci + 2)
                        wait(act, k_ready, ci + 1)
                        wait(act, num_done, ci)
                        nc.scalar.activation(ek[:], ps_proj[:, 0:D], ACT.Exp)
                        nc.scalar.activation(rk[:], ps_proj[:, 0:D], ACT.Relu)
                        for blk in range(2):
                            rows = slice(Q * blk, Q * blk + Q)
                            m = nc.scalar.activation(v_blocks[rows, (j + 1) % 2, :, blk, 0:HD],
                                                     ps_proj[rows, D:2 * D].rearrange("p (h e) -> p h e", e=HD), ACT.Copy)
                        m.then_inc(kv_read, 1)
                    g, slot = next_group(i, j)
                    if g is not None:
                        if c == 0:
                            for k in range(KD):
                                act.wait_ge(turned, 2 * g + k + 1)
                                nc.scalar.activation(x_hi[:, slot, k], (ps_turn, ps_proj)[k][:], ACT.Copy).then_inc(x_hi_ready, 1)
                        if c in (1, 2):
                            for t in range(2):
                                n = 4 * g + 2 * (c - 1) + t
                                act.wait_ge(qk_done, n + 1)
                                if isinstance(i, int) and i == -1:
                                    act.wait_ge(w_lo_ready, 4)
                                wait(act, phi_ready, n - 1)
                                nc.scalar.activation(e[:, t], ps_proj[:], ACT.Exp)
                                nc.scalar.activation(r[:, t], ps_proj[:], ACT.Relu).then_inc(qk_read, 1)

            run(act, body)

        @block.gpsimd
        def _(pool):
            for k in range(4):
                pool.wait_ge(w_ready, k + 1)
                hi, lo = ((w_hi[:, :, k * D:(k + 1) * D], w_lo[:, :, k * D:(k + 1) * D]) if k < 3 else (kept["w_hi"][:], kept["w_lo"][:]))
                nc.gpsimd.tensor_tensor(lo, w_raw[:, k], hi.bitcast(F32), ALU.subtract).then_inc(w_lo_ready, 1)

            masks = head_blocks[:].rearrange("p t c -> p (t c)")
            view = lambda slot, blk: state[:, slot, blk].rearrange("p t k a e -> p (t k a e)")
            pool.wait_ge(const_in, 80)

            def body(i):
                for j in range(8):
                    ci = 8 * i + j
                    g, slot = next_group(i, j)
                    if g is not None and j % 4 == 1:
                        wait(pool, sc_done, 4 * (g - 1))
                        for t in range(2):
                            pool.wait_ge(phi_ready, 4 * g + t + 1)
                            for par in range(2):
                                nc.gpsimd.tensor_tensor(pq_half[:, slot, t, par], pq[:, slot, t],
                                                        parity[:, par:par + 1].broadcast_to([P, 512]), ALU.mult).then_inc(half_ready, 1)
                    if inside(i, 8, j + 1, CHUNKS):
                        pool.wait_ge(acc_ready, 2 * (ci + 1) + 1)
                        wait(pool, num_done, ci)
                        nc.gpsimd.tensor_tensor(view((j + 1) % 2, 1), acc[:, 0], masks, ALU.mult).then_inc(mid_ready, 1)
                        pool.wait_ge(acc_ready, 2 * (ci + 2))
                        if j == 6:
                            pool.wait_ge(reset_ready, i + 1)
                        wait(pool, num_done, ci + 1)
                        nc.gpsimd.tensor_tensor(view(j % 2, 0), acc[:, 1], masks, ALU.mult).then_inc(start_ready, 1)

            run(pool, body)

        @block.vector
        def _(v):
            norm.scales(v)
            for t in range(4):
                norm.rows(xn[:, t], t).then_inc(xn_ready, 1)
            nc.vector.memset(v_blocks[:], 0.0).then_inc(zeroed, 1)
            v.wait_ge(zeroed, 1)
            for blk in range(2):
                nc.vector.memset(v_blocks[Q * blk:Q * blk + Q, :, :, blk, HD:VW], 1.0).then_inc(zeroed, 1)
            nc.vector.memset(acc[:], 0.0).then_inc(zeroed, 1)
            nc.vector.memset(zero[:], 0.0).then_inc(zeroed, 1)
            nc.vector.memset(state[:], 0.0).then_inc(start_ready, 1)
            v.wait_ge(zeroed, 5)

            def half_of_next(i, j, h):
                g, slot = next_group(i, j)
                c = j % 4
                if g is None:
                    return
                if c == 0:
                    v.wait_ge(x_hi_ready, 2 * g + h + 1)
                    nc.vector.tensor_tensor(x_lo[:, slot, h], (ps_turn, ps_proj)[h][:], x_hi[:, slot, h].bitcast(F32), ALU.subtract)\
                        .then_inc(x_lo_ready, 1)
                if c in (1, 2):
                    if c == 1 and h == 0:
                        wait(v, num_done, 4 * (g - 1))
                        wait(v, half_ready, 4 * (g - 1))
                        wait(v, phi_kept[slot], 16 * (i + (j // 4 + 1) // 2))
                        wait(v, red_ready, g - 1)
                    v.wait_ge(qk_read, 4 * g + 2 * (c - 1) + h + 1)
                    nc.vector.scalar_tensor_tensor((pq, pk)[c - 1][:, slot, h], e[:, h], 1.0, r[:, h], ALU.min, ALU.add).then_inc(phi_ready, 1)
                if c == 3 and h == 1:
                    v.wait_ge(phi_ready, 4 * g + 2)
                    wait(v, sum_kept, g)
                    nc.vector.tensor_reduce(red[:], pq[:, slot], AX.X, ALU.add).then_inc(red_ready, 1)
                    v.wait_ge(red_ready, g + 1)
                    nc.vector.tensor_tensor(kept["q_sums"][:, bass.ds(g, 1)].rearrange("p g t -> p (g t)"), red[:], zero[:],
                                            ALU.add).then_inc(sum_kept, 1)

            def body(i):
                for j in range(8):
                    ci, c = 8 * i + j, j % 4
                    if inside(i, 8, j + 1, CHUNKS):
                        v.wait_ge(kv_read, ci + 2)
                        wait(v, st_done, 2 * ci)
                        nc.vector.scalar_tensor_tensor(k_tok[:, (j + 1) % 2], ek[:], 1.0, rk[:], ALU.min, ALU.add).then_inc(k_ready, 1)
                    if inside(i, 8, j + 1, CHUNKS):
                        v.wait_ge(sc_done, ci + 2)
                        wait(v, num_done, ci)
                        for rt in range(4):
                            nc.vector.tensor_tensor(sc[:, (j + 1) % 2, rt].rearrange("p t a i -> p (t a) i"),
                                                    ps_sc[:, rt, 0:4 * Q].rearrange("p (c i) -> p c i", i=Q),
                                                    mask[:, None, :].broadcast_to([P, 4, Q]), ALU.mult).then_inc(sc_ready, 1)
                    if c == 3 and (not isinstance(i, int) or 8 * i + j != -5) and inside(i, 2, (j + 1) // 4 + 1, NG):
                        g = 2 * i + (j + 1) // 4 + 1
                        wait(v, turned, 2 * g)
                        for t in range(4):
                            norm.rows(xn[:, t], 4 * g + t).then_inc(xn_ready, 1)
                    half_of_next(i, j, 0)
                    if c == 0:
                        half_of_next(i, j, 1)
                    if inside(i, 8, j, CHUNKS):
                        num = ps_num[:, 0:NH * VW].rearrange("q (k b e) -> q k b e", b=2, e=VW)
                        v.wait_ge(num_done, ci + 1)
                        wait(v, num_read, 4 * ci)
                        dn = den[:].rearrange("q (k b) -> q k b", b=2)
                        nc.vector.tensor_scalar(dn, num[:, :, :, HD], ATT_EPS, None, ALU.max).then_inc(den_ready, 1)
                        v.wait_ge(den_ready, 2 * ci + 1)
                        nc.vector.reciprocal(den[:], den[:]).then_inc(den_ready, 1)
                        v.wait_ge(den_ready, 2 * ci + 2)
                        for blk in range(2):
                            out = kept["local"][Q * blk:Q * blk + Q, bass.ds(ci, 1)].rearrange("p c (k a e) -> p (c k) a e", a=2, e=HD)
                            for par in range(2):
                                rows = slice(Q * par, Q * par + Q)
                                nc.vector.tensor_tensor(out[:, :, par], num[rows, :, blk, 0:HD],
                                                        dn[rows, :, blk, None].broadcast_to([Q, 8, HD]), ALU.mult).then_inc(num_read, 1)
                    if c > 0:
                        half_of_next(i, j, 1)
                    if inside(i, 8, j + 1, CHUNKS):
                        v.wait_ge(st_done, 2 * (ci + 1) + 1)
                        wait(v, acc_ready, 2 * (ci + 1))
                        wait(v, mid_ready, ci + 1)
                        wait(v, start_ready, ci + 2)
                        if j == 7:
                            wait(v, reset_ready, i + 1)
                        W2 = 2 * 8 * VW
                        nc.vector.tensor_tensor(acc[:, 0], acc[:, 1], ps_state[:, 0:W2], ALU.add).then_inc(acc_ready, 1)
                        v.wait_ge(st_done, 2 * (ci + 2))
                        v.wait_ge(acc_ready, 2 * (ci + 1) + 1)
                        nc.vector.tensor_tensor(acc[:, 1], acc[:, 0], ps_turn[:, 0:W2], ALU.add).then_inc(acc_ready, 1)
                        if j == 6:
                            v.wait_ge(acc_ready, 2 * (ci + 2))
                            nc.vector.tensor_scalar(acc[:, 1], acc[:, 1], keep_rows[:, bass.ds(i + 1, 1)], None, ALU.mult).then_inc(reset_ready, 1)

            run(v, body)
            v.wait_ge(num_read, 4 * CHUNKS)
            v.wait_ge(sum_kept, NG)


def memory_weights(nc, ins, u, norm, kept):
    with ExitStack() as ctx:
        b = Buffers(nc, ctx, "memw")
        mem, coef = kept["mem"], kept["coef"]
        ones = b.sb("ones", [P, P])
        gate_raw = kept["gate_raw"]
        mean = b.sb("mean", [P, BATCHES, 2])
        mean_rows = b.sb("mean_rows", [P, BATCHES, 2, P])
        norms = b.sb("norms", [P, NM])
        alive = b.sb("alive", [P, NM + 1])
        top, total = b.sb("top", [P, BATCHES * NH]), b.sb("total", [P, BATCHES * NH])
        rel = b.sb("rel", [P, NM, BATCHES * NH])
        ps_rel, ps_norms = b.ps("ps_rel", [P, BATCHES, 2, NM, 8]), b.ps("ps_norms", [P, 512])
        const_in, step, pe_done, act_done = b.sem("const_in"), b.sem("step"), b.sem("pe_done"), b.sem("act_done")
        ctx.callback(b.clear)
        block = ctx.enter_context(nc.Block())
        mem6 = mem[:].rearrange("p t m (h e) -> p t m h e", e=VW)

        @block.sync
        def _(sp):
            sp.dma_start(kept["ident"][:], ins["identity"]).then_inc(const_in, 16)
            sp.dma_start(kept["eg_w1"][:], ins["eg_w1T"].rearrange("(k p) c -> p k c", p=P)).then_inc(const_in, 16)
            for name, source in (("eg_b1", "eg_b1"), ("eg_w2", "eg_w2T"), ("eg_b2", "eg_b2_rows")):
                sp.dma_start(kept[name][:], ins[source]).then_inc(const_in, 16)
            sp.wait_ge(const_in, 80)

        @block.tensor
        def _(pe):
            pe.wait_ge(step, STEPS_READY)
            nc.tensor.matmul(ps_norms[:, 0:NM], ones[:], norms[:], start=True, stop=True).then_inc(pe_done, 1)
            for s in range(BATCHES):
                for t in range(2):
                    m = nc.tensor.matmul(ps_rel[:, s, t].rearrange("p m h -> p (m h)"), mean_rows[:, s, t],
                                         mem6[:, t, 1:, :, HD],
                                         start=True, stop=True)
            m.then_inc(pe_done, 1)

        @block.scalar
        def _(act):
            nc.scalar.activation(kept["head_gate"][:], gate_raw[:], ACT.Sigmoid)
            nc.scalar.activation(kept["local_gate"][:], gate_raw[:], ACT.Sigmoid, scale=-1.0)
            act.wait_ge(step, EXP_READY)
            nc.scalar.activation(rel[:], rel[:], ACT.Exp).then_inc(act_done, 1)

        @block.vector
        def _(v):
            link = Chain(v, step)
            link(nc.vector.memset(ones[:], 1.0))
            link.beside(nc.vector.scalar_tensor_tensor(kept["offset"][:], u[:, :, D], -1.0, norm.scale[:], ALU.mult, ALU.mult))
            link(nc.vector.tensor_tensor(mem[:, :, 0], mem[:, :, 1], mem[:, :, 2], ALU.add))
            link(nc.vector.tensor_tensor(mem[:, :, 0], mem[:, :, 0], mem[:, :, 3], ALU.add))
            link(nc.vector.tensor_tensor(mem[:, :, 0], mem[:, :, 0], mem[:, :, 4], ALU.add))
            for m in range(NM):
                link.beside(nc.vector.tensor_reduce(norms[:, m:m + 1], mem6[:, :, m + 1, :, HD], AX.XY, ALU.add))
            gs = NG // BATCHES
            link(nc.vector.tensor_reduce(mean[:], kept["q_sums"][:].rearrange("p (s g) t -> p s t g", g=gs), AX.X, ALU.add))
            for s in range(BATCHES):
                for t in range(2):
                    link(nc.vector.tensor_scalar(mean_rows[:, s, t], ones[:], mean[:, s, t:t + 1], 1.0 / (TOKENS // BATCHES),
                                                 ALU.mult, ALU.mult))
            assert link.n == STEPS_READY
            v.wait_ge(pe_done, 2)
            link(nc.vector.tensor_scalar(alive[:, 1:], ps_norms[:, 0:NM], ATT_EPS, None, ALU.is_ge))
            link(nc.vector.tensor_reduce(alive[:, 0:1], ps_norms[:, 0:NM], AX.X, ALU.add))
            link(nc.vector.tensor_scalar(alive[:, 0:1], alive[:, 0:1], ATT_EPS, None, ALU.is_ge))
            for m in range(NM):
                link.beside(nc.vector.tensor_copy(rel[:, m].rearrange("p (s t h) -> p s t h", s=BATCHES, t=2), ps_rel[:, :, :, m]))
            v.wait_ge(step, link.n)
            link(nc.vector.tensor_tensor(top[:], rel[:, 0], rel[:, 1], ALU.max))
            link(nc.vector.tensor_tensor(top[:], top[:], rel[:, 2], ALU.max))
            link(nc.vector.tensor_tensor(top[:], top[:], rel[:, 3], ALU.max))
            link(nc.vector.tensor_tensor(rel[:], rel[:], top[:, None, :].broadcast_to([P, NM, BATCHES * NH]), ALU.subtract))
            assert link.n == EXP_READY
            v.wait_ge(act_done, 1)
            link(nc.vector.tensor_tensor(total[:], rel[:, 0], rel[:, 1], ALU.add))
            link(nc.vector.tensor_tensor(total[:], total[:], rel[:, 2], ALU.add))
            link(nc.vector.tensor_tensor(total[:], total[:], rel[:, 3], ALU.add))
            link(nc.vector.reciprocal(total[:], total[:]))
            link(nc.vector.tensor_tensor(rel[:], rel[:], total[:, None, :].broadcast_to([P, NM, BATCHES * NH]), ALU.mult))
            link(nc.vector.memset(coef[:, :, 0], 1.0))
            link(nc.vector.tensor_scalar(coef[:, :, 0], coef[:, :, 0], alive[:, 0:1], None, ALU.mult))
            its = NG // 2 // BATCHES
            for s in range(BATCHES):
                for m in range(NM):
                    link.beside(nc.vector.tensor_scalar(coef[:, s * its:(s + 1) * its, m + 1],
                                                 rel[:, m, None, s * NH:(s + 1) * NH].broadcast_to([P, its, NH]),
                                                 alive[:, m + 1:m + 2], None, ALU.mult))


STEPS_READY = 5 + NM + 1 + 2 * BATCHES
EXP_READY = STEPS_READY + 3 + NM + 4


def memory_pass(nc, ins, u, norm, kept):
    with ExitStack() as ctx:
        b = Buffers(nc, ctx, "mem")
        ident, eg_w1, eg_b1, eg_w2, eg_b2 = (kept[n] for n in ("ident", "eg_w1", "eg_b1", "eg_w2", "eg_b2"))
        pq = b.sb("pq", [P, 4, 2, P])
        den = b.sb("den", [P, 2, NM + 1, NH])
        prod = b.sb("prod", [P, 2, NM + 1, D])
        pair_sum, fine = b.sb("pair_sum", [P, 2, D]), b.sb("fine", [P, 2, D])
        local_part = b.sb("local_part", [P, 2, D])
        c_T = b.sb("c_T", [P, 2, P])
        hidden = b.sb("hidden", [64, P])
        choice = b.sb("choice", [P, 2])
        mix = b.sb("mix", [P, 2, D])
        o_hi, o_lo = b.sb("o_hi", [P, KD, P], F32R), b.sb("o_lo", [P, KD, P], F32R)
        xn = b.sb("xn", [P, 2, D])
        row = b.sb("row", [P, 2, ROW])
        bn, bn_copy = b.sb("bn", [P, 6]), b.sb("bn_copy", [P, 1])
        ps_a, ps_b = b.ps("ps_a", [P, 2, 512]), b.ps("ps_b", [P, 2, 512])
        ps_coarse, ps_hidden = b.ps("ps_coarse", [P, 512]), b.ps("ps_hidden", [P, 512])
        ps_turn, ps_out = b.ps("ps_turn", [P, 512]), b.ps("ps_out", [P, 512])
        (mem_done, den_ready, rden_ready, coef_ready, prod_ready, pair_ready, fine_ready, diff_ready, ct_done, ct_ready,
         hidden_done, hidden_ready, choice_done, choice_ready, mix_step, mixed, ot_done, o_hi_ready, o_lo_ready, out_done, xn_ready, local_ready,
         res_done, bn_done, stat_done) = (b.sem(n) for n in (
            "mem_done den_ready rden_ready coef_ready prod_ready pair_ready fine_ready diff_ready ct_done ct_ready "
            "hidden_done hidden_ready choice_done choice_ready mix_step mixed ot_done o_hi_ready o_lo_ready out_done xn_ready local_ready "
            "res_done bn_done stat_done").split())
        pq_in = [b.sem(f"pq_in{k}") for k in range(4)]
        u_kept = [b.sem(f"u_kept{k}") for k in range(2)]
        ctx.callback(b.clear)
        block = ctx.enter_context(nc.Block())
        N8 = CHUNKS // 8

        def run(engine, body):
            body(0)
            with engine.Fori(1, N8 - 1) as i:
                body(i)
            body(N8 - 1)
            body(N8)

        def width(i):
            return 3 if isinstance(i, int) and i == N8 else 8

        @block.sync
        def _(sp):
            def load(i, j):
                wait(sp, mem_done, 8 * i + j - 3)
                group = kept["phi_q"][:, bass.ds(2 * i + j // 4, 1)]
                sp.dma_start(pq[:, j % 4, None], group[:, :, :, (j % 4) * P:(j % 4 + 1) * P]).then_inc(pq_in[j % 4], 16)

            load(0, 0)
            load(0, 1)

            def body(i):
                for j in range(width(i)):
                    c = 8 * i + j
                    if inside(i, 8, j + 2, CHUNKS):
                        load(i, j + 2)
                    if inside(i, 8, j - 3, CHUNKS - 3):
                        wait(sp, stat_done, c - 2)
                        sp.dma_start(u[:, bass.ds(c - 3, 1), :], row[:, (j - 3) % 2, None, :]).then_inc(u_kept[(j - 3) % 2], 16)

            run(sp, body)
            for k in range(2):
                sp.wait_ge(u_kept[k], 16 * ((CHUNKS - 2 - k) // 2))

        @block.tensor
        def _(pe):
            def body(i):
                for j in range(width(i)):
                    c = 8 * i + j
                    if inside(i, 8, j - 3, CHUNKS):
                        wait(pe, mixed, c - 2)
                        wait(pe, o_lo_ready, c - 3)
                        for k in range(KD):
                            m = nc.tensor.transpose(ps_turn[:, k * P:(k + 1) * P], mix[:, (j - 3) % 2, k * P:(k + 1) * P], ident[:])
                        m.then_inc(ot_done, 1)
                    if inside(i, 8, j, CHUNKS):
                        pe.wait_ge(pq_in[j % 4], 16 * (2 * i + j // 4 + 1))
                        for n, (out, m0, m1, t) in enumerate(((ps_a, 0, 3, 0), (ps_a, 0, 3, 1), (ps_b, 3, 5, 0), (ps_b, 3, 5, 1))):
                            wait(pe, prod_ready, 4 * (c - 1) + n + 1)
                            m = nc.tensor.matmul(out[:, t, 0:(m1 - m0) * 8 * VW], pq[:, j % 4, t],
                                                 kept["mem"][:, t, m0:m1].rearrange("p m c -> p (m c)"), start=True, stop=True)
                        m.then_inc(mem_done, 1)
                    if inside(i, 8, j - 1, CHUNKS):
                        wait(pe, prod_ready, 4 * c)
                        wait(pe, ct_ready, c - 1)
                        for k in range(KD):
                            m = nc.tensor.transpose(ps_coarse[:, k * P:(k + 1) * P], prod[:, (j - 1) % 2, 0, k * P:(k + 1) * P], ident[:])
                        m.then_inc(ct_done, 1)
                    if inside(i, 8, j - 3, CHUNKS):
                        wait(pe, res_done, c - 3)
                        wait(pe, o_lo_ready, c - 2)
                        for k in range(KD):
                            m = product3(nc, ps_out[:, 0:D], o_hi[:, k], o_lo[:, k], kept["w_hi"][:, k], kept["w_lo"][:, k],
                                         k == 0, k == KD - 1)
                        m.then_inc(out_done, 1)
                    if inside(i, 8, j - 1, CHUNKS):
                        wait(pe, choice_ready, c - 1)
                        wait(pe, ct_ready, c)
                        for k in range(KD):
                            m = nc.tensor.matmul(ps_hidden[0:64, 0:P], eg_w1[:, k], c_T[:, k], start=(k == 0), stop=(k == KD - 1))
                        m.then_inc(hidden_done, 1)
                    if inside(i, 8, j - 1, CHUNKS):
                        wait(pe, hidden_ready, c)
                        nc.tensor.matmul(ps_hidden[:, 256:257], hidden[:], eg_w2[:], start=True, stop=True).then_inc(choice_done, 1)

            run(pe, body)

        @block.scalar
        def _(act):
            def body(i):
                for j in range(width(i)):
                    c = 8 * i + j
                    if inside(i, 8, j - 3, CHUNKS):
                        wait(act, ot_done, c - 2)
                        wait(act, out_done, c - 3)
                        wait(act, res_done, c - 4)
                        nc.scalar.activation(o_hi[:].rearrange("p k t -> p (k t)"), ps_turn[:, 0:D], ACT.Copy).then_inc(o_hi_ready, 1)
                        chunk, col = u[:, bass.ds(c - 3, 1)], bass.ds(c - 3, 1)
                        nc.scalar.activation(xn[:, (j - 3) % 2], chunk[:, :, 0:D].rearrange("p c d -> p (c d)"), ACT.Identity,
                                             bias=kept["offset"][:, col], scale=norm.scale[:, col]).then_inc(xn_ready, 1)
                    if inside(i, 8, j - 1, CHUNKS):
                        wait(act, ct_done, c)
                        wait(act, hidden_done, c - 1)
                        nc.scalar.activation(c_T[:].rearrange("p k t -> p (k t)"), ps_coarse[:, 0:D], ACT.Copy).then_inc(ct_ready, 1)
                    if inside(i, 8, j - 1, CHUNKS):
                        wait(act, hidden_done, c)
                        wait(act, choice_done, c - 1)
                        nc.scalar.activation(hidden[:], ps_hidden[0:64, 0:P], ACT.Relu, bias=eg_b1[:]).then_inc(hidden_ready, 1)
                        wait(act, choice_done, c)
                        wait(act, mix_step, 2 * (c - 2))
                        nc.scalar.activation(choice[:, (j - 1) % 2:(j - 1) % 2 + 1], ps_hidden[:, 256:257], ACT.Sigmoid,
                                             bias=eg_b2[:]).then_inc(choice_ready, 1)

            run(act, body)

        @block.gpsimd
        def _(pool):
            def body(i):
                for j in range(width(i)):
                    c = 8 * i + j
                    if inside(i, 8, j - 2, CHUNKS):
                        wait(pool, mix_step, 2 * (c - 1))
                        wait(pool, local_ready, c - 1)
                        nc.gpsimd.tensor_tensor(mix[:, j % 2], mix[:, j % 2], local_part[:, j % 2], ALU.add).then_inc(mixed, 1)
                    if inside(i, 8, j, CHUNKS):
                        s = j % 2
                        pool.wait_ge(prod_ready, 4 * (c + 1))
                        wait(pool, mix_step, 2 * (c - 1))
                        wait(pool, mixed, c - 1)
                        nc.gpsimd.tensor_tensor(pair_sum[:], prod[:, s, 1:3], prod[:, s, 3:5], ALU.add).then_inc(pair_ready, 1)
                        pool.wait_ge(pair_ready, c + 1)
                        nc.gpsimd.tensor_tensor(fine[:, s], pair_sum[:, 0], pair_sum[:, 1], ALU.add).then_inc(fine_ready, 1)
                        pool.wait_ge(fine_ready, c + 1)
                        nc.gpsimd.tensor_tensor(fine[:, s], fine[:, s], prod[:, s, 0], ALU.subtract).then_inc(diff_ready, 1)
                        nc.gpsimd.tensor_tensor(local_part[:, s].rearrange("p (h e) -> p h e", e=HD),
                                                kept["local"][:, bass.ds(c, 1)].rearrange("p c (h e) -> p (c h) e", e=HD),
                                                kept["local_gate"][:, :, None].broadcast_to([P, NH, HD]), ALU.mult).then_inc(local_ready, 1)

            run(pool, body)

        @block.vector
        def _(v):
            def body(i):
                for j in range(width(i)):
                    c = 8 * i + j
                    s1 = (j - 3) % 2
                    to = u[:, c - 3] if isinstance(i, int) and i == N8 else row[:, s1]
                    if inside(i, 8, j - 3, CHUNKS):
                        wait(v, o_hi_ready, c - 2)
                        wait(v, out_done, c - 3)
                        nc.vector.tensor_tensor(o_lo[:].rearrange("p k t -> p (k t)"), ps_turn[:, 0:D],
                                                o_hi[:].bitcast(F32).rearrange("p k t -> p (k t)"), ALU.subtract).then_inc(o_lo_ready, 1)
                    if inside(i, 8, j, CHUNKS):
                        s = j % 2
                        v.wait_ge(mem_done, c + 1)
                        wait(v, mix_step, 2 * (c - 1))
                        wait(v, diff_ready, c - 1)
                        wait(v, ct_done, c - 1)
                        dn = den[:, s].rearrange("p m (t h) -> p m t h", t=2)
                        src = [(ps_a[:, t, 0:3 * 8 * VW].rearrange("p (m h e) -> p m h e", m=3, e=VW), 0, 3, t) for t in range(2)] + \
                              [(ps_b[:, t, 0:2 * 8 * VW].rearrange("p (m h e) -> p m h e", m=2, e=VW), 3, 5, t) for t in range(2)]
                        for ps, m0, m1 in ((ps_a, 0, 3), (ps_b, 3, 5)):
                            sums = ps[:, :, 0:(m1 - m0) * 8 * VW].rearrange("p t (m h e) -> p t m h e", m=m1 - m0, e=VW)[:, :, :, :, HD]
                            nc.vector.tensor_scalar(dn[:, m0:m1].rearrange("p m t h -> p t m h"), sums, ATT_EPS, None, ALU.max)\
                                .then_inc(den_ready, 1)
                        v.wait_ge(den_ready, 2 * c + 2)
                        nc.vector.reciprocal(den[:, s], den[:, s]).then_inc(rden_ready, 1)
                        v.wait_ge(rden_ready, c + 1)
                        nc.vector.tensor_tensor(den[:, s], den[:, s], kept["coef"][:, bass.ds(i, 1)].rearrange("p i m h -> p (i m) h"),
                                                ALU.mult).then_inc(coef_ready, 1)
                        v.wait_ge(coef_ready, c + 1)
                        pr = prod[:, s].rearrange("p m (t h e) -> p m t h e", t=2, e=HD)
                        for ps, m0, m1, t in src:
                            for_all = dn[:, m0:m1, t, :, None].broadcast_to([P, m1 - m0, 8, HD])
                            nc.vector.tensor_tensor(pr[:, m0:m1, t], ps[:, :, :, 0:HD], for_all, ALU.mult).then_inc(prod_ready, 1)
                    if inside(i, 8, j - 3, CHUNKS):
                        wait(v, out_done, c - 2)
                        wait(v, xn_ready, c - 2)
                        if not (isinstance(i, int) and i == N8):
                            wait(v, u_kept[s1], 16 * (4 * i + (j - 3) // 2))
                        nc.vector.tensor_tensor(to[:, 0:D], ps_out[:, 0:D], xn[:, s1], ALU.add).then_inc(res_done, 1)
                    if inside(i, 8, j - 1, CHUNKS):
                        s = (j - 1) % 2
                        wait(v, diff_ready, c)
                        wait(v, choice_ready, c)
                        wait(v, ot_done, c - 2)
                        nc.vector.scalar_tensor_tensor(mix[:, s], fine[:, s], choice[:, s:s + 1], prod[:, s, 0],
                                                       ALU.mult, ALU.add).then_inc(mix_step, 1)
                    if inside(i, 8, j - 3, CHUNKS):
                        wait(v, res_done, c - 2)
                        nc.vector.bn_stats(bn[:], to[:, 0:D]).then_inc(bn_done, 1)
                    if inside(i, 8, j - 1, CHUNKS):
                        wait(v, mix_step, 2 * (c - 1) + 1)
                        mh = mix[:, s].rearrange("p (h e) -> p h e", e=HD)
                        nc.vector.tensor_tensor(mh, mh, kept["head_gate"][:, :, None].broadcast_to([P, NH, HD]), ALU.mult).then_inc(mix_step, 1)
                    if inside(i, 8, j - 3, CHUNKS):
                        wait(v, bn_done, c - 2)
                        nc.vector.tensor_copy(bn_copy[:], bn[:, 0:1])
                        nc.vector.bn_aggr(to[:, D:ROW], bn[:]).then_inc(stat_done, 1)

            run(v, body)


E, E1 = 16, 17


def experts_phase(nc, ins, u, out):
    with ExitStack() as ctx:
        b = Buffers(nc, ctx, "moe")
        ident = b.sb("ident", [P, P])
        rank, r_bias = b.sb("rank", [P, E]), b.sb("r_bias", [P, E])
        wr_raw = b.sb("wr_raw", [P, KD, E])
        wr_hi, wr_lo = b.sb("wr_hi", [P, KD, E], F32R), b.sb("wr_lo", [P, KD, E], F32R)
        RAW = 4
        gu_raw, d_raw = b.sb("gu_raw", [P, RAW, KD, 2, P]), b.sb("d_raw", [P, RAW, D])
        gu_hi, gu_lo = b.sb("gu_hi", [P, E1, KD, 2, P], F32R), b.sb("gu_lo", [P, E1, KD, 2, P], F32R)
        d_hi, d_lo = b.sb("d_hi", [P, E1, D], F32R), b.sb("d_lo", [P, E1, D], F32R)
        norm = Normalizer(nc, b, u)
        xn = b.sb("xn", [P, 2, 4, D])
        x_hi, x_lo = b.sb("x_hi", [P, 2, KD, 512], F32R), b.sb("x_lo", [P, 2, KD, 512], F32R)
        logit, cand, first, second, rest = (b.sb(n, [P, 4, E]) for n in ("logit", "cand", "first", "second", "rest"))
        top, total, chosen = (b.sb(n, [P, 4]) for n in ("top", "total", "chosen"))
        weight = b.sb("weight", [P, 2, 4, E1])
        sil, h = b.sb("sil", [P, 2, 512]), b.sb("h", [P, 2, 512])
        h_hi, h_lo = b.sb("h_hi", [P, 2, 512], F32R), b.sb("h_lo", [P, 2, 512], F32R)
        row = b.sb("row", [P, 2, 4, D])
        bn, bn_copy, stats = b.sb("bn", [P, 4, 6]), b.sb("bn_copy", [P, 1]), b.sb("stats", [P, 4, 2])
        var, dev, dev_t = b.sb("var", [P, 4]), b.sb("dev", [P, 4]), b.sb("dev_t", [P, 4])
        ps_g, ps_u = b.ps("ps_g", [P, 2, 512]), b.ps("ps_u", [P, 2, 512])
        ps_turn, ps_out = b.ps("ps_turn", [P, 512]), b.ps("ps_out", [P, 4, D])
        (ident_in, const_in, wr_ready, w_hi_ready, w_lo_ready, zeroed, xn_ready, turned, x_hi_ready, x_lo_ready, logits_done, route_step,
         exp_ready, g_done, u_done, sil_ready, h_ready, h_hi_ready, h_lo_ready, down_done,
         sum_ready, bn_done, stat_done, dev_step, row_ready, stored) = (b.sem(n) for n in (
            "ident_in const_in wr_ready w_hi_ready w_lo_ready zeroed xn_ready turned x_hi_ready x_lo_ready logits_done route_step "
            "exp_ready g_done u_done sil_ready h_ready h_hi_ready h_lo_ready down_done "
            "sum_ready bn_done stat_done dev_step row_ready stored").split())
        raw_in = [b.sem(f"raw_in{k}") for k in range(RAW)]
        out_rows = out.rearrange("(g c p) d -> p g c d", p=P, c=4)
        ROUTE, DEV = 20, 11
        ctx.callback(b.clear)
        block = ctx.enter_context(nc.Block())

        def run(engine, body):
            body(-1, 1)
            run_groups(engine, body)

        def exists(i, k):
            return tuple(inside(i, 2, k + d, NG) for d in (-1, 0, 1))

        def loaded(i, k, e):
            return e + 3 if isinstance(i, int) and i == 0 and k == 0 and e + 3 < E1 else None

        @block.sync
        def _(sp):
            sp.dma_start(ident[:], ins["identity"]).then_inc(ident_in, 16)
            for e in range(E1):
                wait(sp, w_lo_ready, e - RAW + 1)
                sp.dma_start(gu_raw[:, e % RAW].rearrange("p k w i -> p k (w i)"),
                             ins["w_gate_up"][e].rearrange("(k p) c -> p k c", p=P)).then_inc(raw_in[e % RAW], 16)
                sp.dma_start(d_raw[:, e % RAW], ins["w_down"][e]).then_inc(raw_in[e % RAW], 16)

            def body(i, k):
                if exists(i, k)[0]:
                    g = 2 * i + k - 1
                    sp.wait_ge(row_ready, 4 * (g + 1))
                    sp.dma_start(out_rows[:, bass.ds(g, 1)], row[:, (k + 1) % 2, None]).then_inc(stored, 16)

            run(sp, body)
            sp.wait_ge(stored, 16 * NG)

        @block.tensor
        def _(pe):
            def body(i, k):
                prev, cur, nxt = exists(i, k)
                g = 2 * i + k
                ns = (k + 1) % 2
                for e in range(E1):
                    n = E1 * g + e
                    s = (k + e) % 2
                    if cur:
                        if isinstance(i, int) and i == 0 and k == 0:
                            pe.wait_ge(w_lo_ready, e + 1)
                        if e == 0:
                            pe.wait_ge(x_lo_ready, 2 * (g + 1))
                        for w, to, read, done in ((0, ps_g, sil_ready, g_done), (1, ps_u, h_ready, u_done)):
                            wait(pe, read, n - 1)
                            for d in range(KD):
                                m = product3(nc, to[:, s], gu_hi[:, e, d, w], gu_lo[:, e, d, w], x_hi[:, k, d], x_lo[:, k, d],
                                             d == 0, d == KD - 1)
                            m.then_inc(done, 1)
                    if (cur if e >= 2 else prev):
                        ee = (e - 2) % E1
                        pe.wait_ge(h_lo_ready, n - 1)
                        wait(pe, sum_ready, 4 * (n - 2))
                        for c in range(4):
                            toks = slice(c * P, (c + 1) * P)
                            m = product3(nc, ps_out[:, c], h_hi[:, s, toks], h_lo[:, s, toks], d_hi[:, ee], d_lo[:, ee], True, True)
                        m.then_inc(down_done, 1)
                    if nxt:
                        if e in (3, 5):
                            d = (e - 3) // 2
                            if e == 3:
                                pe.wait_ge(xn_ready, 4 * (g + 2))
                                wait(pe, route_step, ROUTE * (g + 1))
                                if isinstance(i, int) and i < 0:
                                    pe.wait_ge(ident_in, 16)
                            else:
                                pe.wait_ge(x_lo_ready, 2 * (g + 1) + 1)
                            for c in range(4):
                                m = nc.tensor.transpose(ps_turn[:, c * P:(c + 1) * P], xn[:, ns, c, d * P:(d + 1) * P], ident[:])
                            m.then_inc(turned, 1)
                        if e in (7, 8, 9, 10):
                            c = e - 7
                            if c == 0:
                                pe.wait_ge(x_lo_ready, 2 * (g + 2))
                                pe.wait_ge(wr_ready, 2)
                            toks = slice(c * P, (c + 1) * P)
                            for d in range(KD):
                                m = product3(nc, ps_turn[:, c * E:(c + 1) * E], x_hi[:, ns, d, toks], x_lo[:, ns, d, toks],
                                             wr_hi[:, d], wr_lo[:, d], d == 0, d == KD - 1)
                            m.then_inc(logits_done, 1)
                    if not (cur or nxt) and e == 1:
                        break

            run(pe, body)

        @block.scalar
        def _(act):
            for t, name in ((r_bias, "router_bias"), (rank, "rank")):
                act.dma_start(t[:], ins[name]).then_inc(const_in, 16)
            act.dma_start(wr_raw[:], ins["router_T"].rearrange("(k p) e -> p k e", p=P)).then_inc(const_in, 16)
            act.wait_ge(const_in, 48)
            nc.scalar.activation(wr_hi[:], wr_raw[:], ACT.Copy).then_inc(wr_ready, 1)

            def weights(e):
                act.wait_ge(raw_in[e % RAW], 32 * (e // RAW + 1))
                nc.scalar.activation(gu_hi[:, e], gu_raw[:, e % RAW], ACT.Copy)
                nc.scalar.activation(d_hi[:, e], d_raw[:, e % RAW], ACT.Copy).then_inc(w_hi_ready, 1)

            def body(i, k):
                prev, cur, nxt = exists(i, k)
                g = 2 * i + k
                ns = (k + 1) % 2
                for e in range(E1):
                    n = E1 * g + e
                    s = (k + e) % 2
                    if cur:
                        act.wait_ge(g_done, n + 1)
                        wait(act, h_ready, n - 1)
                        nc.scalar.activation(sil[:, s], ps_g[:, s], ACT.Silu).then_inc(sil_ready, 1)
                    if (cur if e >= 1 else prev):
                        act.wait_ge(h_ready, n)
                        wait(act, down_done, n - 2)
                        nc.scalar.activation(h_hi[:, 1 - s], h[:, 1 - s], ACT.Copy).then_inc(h_hi_ready, 1)
                    if loaded(i, k, e):
                        weights(loaded(i, k, e))
                    if nxt:
                        if e in (3, 5):
                            act.wait_ge(turned, 2 * (g + 1) + (e - 3) // 2 + 1)
                            nc.scalar.activation(x_hi[:, ns, (e - 3) // 2], ps_turn[:], ACT.Copy).then_inc(x_hi_ready, 1)
                        if e == 12:
                            act.wait_ge(route_step, ROUTE * (g + 1) + 3)
                            nc.scalar.activation(rest[:], rest[:], ACT.Exp).then_inc(exp_ready, 1)
                    if not (cur or nxt) and e == 0:
                        break

            for e in range(3):
                weights(e)
            body(-1, 1)
            run_groups(act, body)

        @block.gpsimd
        def _(pool):
            pool.wait_ge(wr_ready, 1)
            nc.gpsimd.tensor_tensor(wr_lo[:], wr_raw[:], wr_hi[:].bitcast(F32), ALU.subtract).then_inc(wr_ready, 1)

            def weights(e):
                pool.wait_ge(w_hi_ready, e + 1)
                nc.gpsimd.tensor_tensor(gu_lo[:, e], gu_raw[:, e % RAW], gu_hi[:, e].bitcast(F32), ALU.subtract)
                nc.gpsimd.tensor_tensor(d_lo[:, e], d_raw[:, e % RAW], d_hi[:, e].bitcast(F32), ALU.subtract).then_inc(w_lo_ready, 1)

            def body(i, k):
                cur = exists(i, k)[1]
                for e in range(E1):
                    n = E1 * (2 * i + k) + e
                    s = (k + e) % 2
                    if cur:
                        pool.wait_ge(h_hi_ready, n + 1)
                        wait(pool, down_done, n - 1)
                        nc.gpsimd.tensor_tensor(h_lo[:, s], h[:, s], h_hi[:, s].bitcast(F32), ALU.subtract).then_inc(h_lo_ready, 1)
                    if loaded(i, k, e):
                        weights(loaded(i, k, e))

            for e in range(3):
                weights(e)
            run(pool, body)

        @block.vector
        def _(v):
            nc.vector.memset(weight[:], 1.0).then_inc(zeroed, 1)
            v.wait_ge(zeroed, 1)
            norm.scales(v)

            def over(t, width):
                return t[:, :, None].broadcast_to([P, 4, width])

            def route(g, slot, part):
                if part == 0:
                    link = Chain(v, route_step, ROUTE * g)
                    lg = ps_turn[:, 0:4 * E].rearrange("p (c e) -> p c e", e=E)
                    link(nc.vector.tensor_tensor(logit[:], lg, r_bias[:, None, :].broadcast_to([P, 4, E]), ALU.add))
                    link(nc.vector.tensor_reduce(top[:], logit[:], AX.X, ALU.max))
                    link(nc.vector.tensor_tensor(rest[:], logit[:], over(top, E), ALU.subtract))
                if part == 1:
                    link = Chain(v, route_step, ROUTE * g + 3)
                    link(nc.vector.tensor_tensor(cand[:], logit[:], over(top, E), ALU.is_equal))
                    link(nc.vector.tensor_tensor(cand[:], cand[:], rank[:, None, :].broadcast_to([P, 4, E]), ALU.mult))
                    link(nc.vector.tensor_reduce(top[:], cand[:], AX.X, ALU.max))
                    link(nc.vector.tensor_tensor(first[:], cand[:], over(top, E), ALU.is_equal))
                    link(nc.vector.scalar_tensor_tensor(logit[:], first[:], -1e30, logit[:], ALU.mult, ALU.add))
                if part == 2:
                    link = Chain(v, route_step, ROUTE * g + 8)
                    link(nc.vector.tensor_reduce(top[:], logit[:], AX.X, ALU.max))
                    link(nc.vector.tensor_tensor(cand[:], logit[:], over(top, E), ALU.is_equal))
                    link(nc.vector.tensor_tensor(cand[:], cand[:], rank[:, None, :].broadcast_to([P, 4, E]), ALU.mult))
                    link(nc.vector.tensor_reduce(top[:], cand[:], AX.X, ALU.max))
                    link(nc.vector.tensor_tensor(second[:], cand[:], over(top, E), ALU.is_equal))
                if part == 3:
                    link = Chain(v, route_step, ROUTE * g + 13)
                    v.wait_ge(exp_ready, g + 1)
                    link(nc.vector.tensor_tensor(first[:], first[:], second[:], ALU.add))
                    link(nc.vector.tensor_tensor(first[:], first[:], rest[:], ALU.mult))
                    link(nc.vector.tensor_reduce(total[:], rest[:], AX.X, ALU.add))
                    link(nc.vector.tensor_reduce(chosen[:], first[:], AX.X, ALU.add))
                    link(nc.vector.scalar_tensor_tensor(chosen[:], total[:], 1e-9, chosen[:], ALU.mult, ALU.add))
                if part == 4:
                    link = Chain(v, route_step, ROUTE * g + 18)
                    link(nc.vector.reciprocal(chosen[:], chosen[:]))
                    wait(v, sum_ready, 4 * E1 * (g - 1))
                    link(nc.vector.tensor_tensor(weight[:, slot, :, 0:E], first[:], over(chosen, E), ALU.mult))

            def deviation(g, part):
                link = Chain(v, dev_step, DEV * g + max(0, 3 * part - 1))
                if part == 0:
                    link(nc.vector.tensor_scalar(var[:], stats[:, :, 1], LN_EPS, None, ALU.add))
                    first_guess(nc, link, var[:], dev[:])
                else:
                    newton_step(nc, link, var[:], dev[:], dev_t[:])

            def body(i, k):
                prev, cur, nxt = exists(i, k)
                g = 2 * i + k
                ns = (k + 1) % 2
                for e in range(E1):
                    n = E1 * g + e
                    s = (k + e) % 2
                    if prev:
                        if e == 2:
                            v.wait_ge(sum_ready, 4 * E1 * g)
                            for c in range(4):
                                nc.vector.bn_stats(bn[:, c], row[:, ns, c]).then_inc(bn_done, 1)
                            v.wait_ge(bn_done, 4 * g)
                            nc.vector.tensor_copy(bn_copy[:], bn[:, 3, 0:1])
                            for c in range(4):
                                nc.vector.bn_aggr(stats[:, c], bn[:, c]).then_inc(stat_done, 1)
                        if e in (3, 4, 5, 6):
                            if e == 3:
                                v.wait_ge(stat_done, 4 * g)
                            deviation(g - 1, e - 3)
                        if e == 7:
                            for c in range(4):
                                nc.vector.tensor_scalar(row[:, ns, c], row[:, ns, c], stats[:, c, 0:1], dev[:, c:c + 1],
                                                        ALU.subtract, ALU.mult).then_inc(row_ready, 1)
                    if cur:
                        v.wait_ge(sil_ready, n + 1)
                        v.wait_ge(u_done, n + 1)
                        wait(v, h_lo_ready, n - 1)
                        nc.vector.tensor_tensor(h[:, s], ps_u[:, s], sil[:, s], ALU.mult).then_inc(h_ready, 1)
                    if (cur if e >= 2 else prev):
                        ee, slot = (e - 2) % E1, k if e >= 2 else ns
                        v.wait_ge(down_done, n - 1)
                        wait(v, sum_ready, 4 * (n - 2))
                        if ee == 0:
                            wait(v, stored, 16 * (g - 1))
                            if isinstance(i, int) and i == 0 and k == 0:
                                v.wait_ge(route_step, ROUTE)
                        for c in range(4):
                            before = xn[:, slot, c] if ee == 0 else row[:, slot, c]
                            nc.vector.scalar_tensor_tensor(row[:, slot, c], ps_out[:, c], weight[:, slot, c, ee:ee + 1], before,
                                                           ALU.mult, ALU.add).then_inc(sum_ready, 1)
                    if nxt:
                        if e == 2:
                            for c in range(4):
                                norm.rows(xn[:, ns, c], 4 * (g + 1) + c).then_inc(xn_ready, 1)
                        if e in (3, 5):
                            d = (e - 3) // 2
                            v.wait_ge(x_hi_ready, 2 * (g + 1) + d + 1)
                            nc.vector.tensor_tensor(x_lo[:, ns, d], ps_turn[:], x_hi[:, ns, d].bitcast(F32), ALU.subtract).then_inc(x_lo_ready, 1)
                        if e == 11:
                            v.wait_ge(const_in, 48)
                            v.wait_ge(logits_done, 4 * (g + 2))
                        if e in (11, 12, 13, 14, 15):
                            route(g + 1, ns, e - 11)
                    if not (cur or nxt) and e == 7:
                        break

            run(v, body)


def mixer_constants():
    import numpy as np

    t = np.arange(P)
    same = (t[:, None] // Q) == (t[None, :] // Q)
    upto = same & (t[:, None] <= t[None, :])
    after = same & (t[:, None] > t[None, :])
    first = np.repeat((t < Q)[:, None], P, 1)
    sums = -np.stack([upto, after, first, ~first], 1).astype(np.float32)
    stat = np.zeros((94, G, P), np.float32)
    stat[:Q] = np.where((t[None, :] % Q) > np.arange(Q)[:, None], -1e30, 0.0)[:, None, :]
    for k in range(3):
        for block in range(2):
            stat[Q + 2 * k + block] = (t // Q == block)
    mov = np.zeros((94, H, Q), np.float32)
    mov[:Q] = np.eye(Q)[:, None, :]
    for k in range(3):
        for j in range(8):
            mov[70 + 8 * k + j, j::8] = -1
    keep = np.ones((P, 9), np.float32)
    keep[:, 4] = 0
    bf = np.dtype("bfloat16")
    return {"neg_tri": np.ascontiguousarray(sums[:, 0]), "sum_masks": sums, "stat_const": stat.astype(bf),
            "mov_const": mov.reshape(94, H * Q).astype(bf), "keep_rows": keep, "identity": np.eye(P, dtype=np.float32)}


def layouts(x):
    import numpy as np

    c = np.ascontiguousarray
    tokens = c(x["L0_attn_input_"]).reshape(TOKENS, D)
    w_in = x["L0_attn_in_proj_w"]
    a = {
        "x": tokens, "xT": c(tokens.T), "w_projT": c(w_in[:2048].T), "w_stepT": c(w_in[2048:].T),
        "d_rows": c(np.broadcast_to(x["L0_attn_D"], (P, H))),
        "conv_w": c(x["L0_attn_conv1d_weight"].reshape(CONV * P, 4)),
        "conv_b": c(x["L0_attn_conv1d_bias"].reshape(CONV, P).T),
        "z_b": c(x["L0_attn_z_bias"].reshape(4, P).T),
        "w_outT": c(x["L0_attn_out_proj_w"].T),
        "w1T": np.pad(x["L0_ffn_w1"].T, ((0, 0), (0, FT * P - HIDDEN))),
        "w2T": np.pad(x["L0_ffn_w2"].T, ((0, 0), (0, FT * P - HIDDEN))),
        "w3T": np.pad(x["L0_ffn_w3"].T, ((0, FT * P - HIDDEN), (0, 0))),
    }
    for n in "qkvo":
        a[f"w{n}T"] = c(x[f"L1_attn_w_{n}"].T)
    mem = np.zeros((2, 8, HD, NM, 8, VW), np.float32)
    fine = x["L1_attn_fine_memories"].reshape(NM, 2, 8, HD, HD)
    norms = x["L1_attn_fine_memory_norms"].reshape(NM, 2, 8, HD)
    for h in range(8):
        mem[:, h, :, :, h, :HD] = fine[:, :, h].transpose(1, 2, 0, 3)
        mem[:, h, :, :, h, HD] = norms[:, :, h].transpose(1, 2, 0)
    a["mem_blocks"] = c(mem.reshape(2, P, NM, 8 * VW).transpose(1, 0, 2, 3))
    a["gate_rows"] = c(np.broadcast_to(x["L1_attn_memory_gate"], (P, NH)))
    a["eg_w1T"], a["eg_w2T"] = c(x["L1_attn_eg_w1"].T), c(x["L1_attn_eg_w2"].T)
    a["eg_b1"] = c(x["L1_attn_eg_b1"].reshape(64, 1))
    a["eg_b2_rows"] = c(np.broadcast_to(x["L1_attn_eg_b2"], (P, 1)))
    a.update(mixer_constants())
    ch = np.arange(P)
    blocks = (ch[:, None] // HD == np.arange(8)[None, :]).astype(np.float32)
    a["head_blocks"] = c(np.broadcast_to(np.repeat(blocks, VW, 1)[:, None], (P, 2, 8 * VW)))
    a["parity"] = np.stack([(ch // HD % 2 == k).astype(np.float32) for k in range(2)], 1)
    a["upper_ones"] = np.tile(np.triu(np.ones((Q, Q), np.float32)), (P // Q, 1))
    kb = np.ones((P, NG // 2 + 1), np.float32)
    kb[:, 2] = 0
    a["keep_batches"] = kb
    stack = lambda n: np.concatenate([x[f"L1_ffn_{n}"], x[f"L1_ffn_s{n}"][None]])
    a["w_gate_up"], a["w_down"] = np.concatenate([stack("Wg"), stack("Wu")], 2), stack("Wd")
    a["router_T"], a["router_bias"] = c(x["L1_ffn_Wr"].T), c(np.broadcast_to(x["L1_ffn_bias"], (P, E)))
    a["rank"] = c(np.broadcast_to(np.arange(E, 0, -1, dtype=np.float32), (P, E)))
    return a


def mixer_keep(nc, ctx):
    b = Buffers(nc, ctx, "keep")
    return {
        "w_hi": b.sb("w_hi", [P, KD, 2048], F32R), "w_lo": b.sb("w_lo", [P, KD, 2048], F32R),
        "wo_hi": b.sb("wo_hi", [P, 4, D], F32R), "wo_lo": b.sb("wo_lo", [P, 4, D], F32R),
        "conv_w": b.sb("conv_w", [P, CONV, 4]), "conv_b": b.sb("conv_b", [P, CONV]), "z_b": b.sb("z_b", [P, 4]),
        "ident": b.sb("ident", [P, P]), "sum_masks": b.sb("sum_masks", [P, 4, P]), "keep_rows": b.sb("keep_rows", [P, 9]),
        "mov": b.sb("mov", [94, 2, H * Q], BF16), "stat": b.sb("stat", [94, 2, G, P], BF16),
    }


def build_program(nc, ins, out):
    with ExitStack() as ctx:
        u = Buffers(nc, ctx, "all").sb("u", [P, CHUNKS, ROW])
        scratch = {"steps": nc.dram_tensor("steps_scratch", [CHUNKS, P, 2, H], F32).ap(),
                   "parts": nc.dram_tensor("parts_scratch", [CHUNKS, H, 3, P], BF16).ap()}
        with ExitStack() as mixer_ctx:
            keep = mixer_keep(nc, mixer_ctx)
            steps_phase(nc, ins, keep, scratch)
            mixer_phase(nc, ins, keep, scratch, u)
        ffn_phase(nc, ins, u)
        attention_phase(nc, ins, u)
        experts_phase(nc, ins, u, out)


def kernel(**inputs):
    import numpy as np
    import concourse.bacc as bacc
    from concourse.bass_utils import run_bass_kernel_spmd

    nc = bacc.Bacc("TRN2", target_bir_lowering=False, num_devices=1)
    arrays = {name: np.ascontiguousarray(a) for name, a in layouts({k: np.asarray(a) for k, a in inputs.items()}).items()}
    ins = {name: nc.dram_tensor(name, list(a.shape), mybir.dt.from_np(a.dtype), kind="ExternalInput").ap()
           for name, a in arrays.items()}
    out = nc.dram_tensor("out", [TOKENS, D], F32, kind="ExternalOutput").ap()
    build_program(nc, ins, out)
    launched = run_bass_kernel_spmd(nc, [arrays], core_ids=[0])
    return launched.results[0]["out"].reshape(BATCHES, TOKENS // BATCHES, D)
```
